# Optimizing a Trainium2 kernel written in Bass

```python
import numpy as np
import jax
import jax.numpy as jnp

def _softmax(x, axis=-1):
    return jax.nn.softmax(x, axis=axis)

def _gelu(x):
    return jax.nn.gelu(x, approximate=True)

def _silu(x):
    return jax.nn.silu(x)

def _sigmoid(x):
    return jax.nn.sigmoid(x)

def _layernorm(x, axis=-1, eps=1e-05):
    m = jnp.mean(x, axis=axis, keepdims=True)
    v = jnp.var(x, axis=axis, keepdims=True)
    return (x - m) / jnp.sqrt(v + eps)

def _scatter_add(tgt, idx, src, axis=0):
    return tgt.at[idx].add(src)

def _segment_sum(src, seg, n):
    return jax.ops.segment_sum(src, seg, n)
kernel_name = 'mk_adaln_d1_jaxref_r4_22f9aa'

def setup_inputs(seed: int=0):
    np.random.seed(seed)
    _w = jnp.asarray

    def _L0_attn_setup():
        import jax, jax.numpy as jnp
        import numpy as np
        EPS = 1e-06
        ROPE_BASE = 10000.0

        def rmsnorm(x, w):
            return x * jax.lax.rsqrt(jnp.mean(x * x, axis=-1, keepdims=True) + EPS) * w

        def apply_rope(x, seq_axis_len):
            hd = x.shape[-1]
            inv_freq = 1.0 / ROPE_BASE ** (jnp.arange(0, hd, 2, dtype=jnp.float32) / hd)
            ang = jnp.arange(seq_axis_len, dtype=jnp.float32)[:, None] * inv_freq[None, :]
            cos = jnp.concatenate([jnp.cos(ang), jnp.cos(ang)], axis=-1)
            sin = jnp.concatenate([jnp.sin(ang), jnp.sin(ang)], axis=-1)
            x1, x2 = (x[..., :hd // 2], x[..., hd // 2:])
            rot = jnp.concatenate([-x2, x1], axis=-1)
            return x * cos + rot * sin
        key = jax.random.key(seed)
        ks = jax.random.split(key, 9)
        B, S, D, H = (2, 512, 512, 16)
        hd = D // H
        s = 0.02
        return {'x': jax.random.normal(ks[0], (B, S, D), dtype=jnp.float32), 'Wq': jax.random.normal(ks[1], (D, D), dtype=jnp.float32) * s, 'Wk': jax.random.normal(ks[2], (hd, D), dtype=jnp.float32) * s, 'Wv': jax.random.normal(ks[3], (hd, D), dtype=jnp.float32) * s, 'Wo': jax.random.normal(ks[4], (D, D), dtype=jnp.float32) * s, 'w_pre': jnp.ones((D,), dtype=jnp.float32), 'w_qn': jnp.ones((hd,), dtype=jnp.float32), 'w_kn': jnp.ones((hd,), dtype=jnp.float32)}
    _L0_attn_in = _L0_attn_setup()

    def _L0_ffn_setup():
        import jax, jax.numpy as jnp
        import numpy as np
        from jax import lax
        E = 64
        H = 512
        I = 176
        G = 8
        TOPK_GROUP = 4
        K = 8
        B, S = (2, 512)
        N = B * S
        CAP = 2 * N * K // E
        SCALE = 2.5

        def _route(x, router_weight, e_bias):
            logits = x.astype(jnp.float32) @ router_weight.astype(jnp.float32).T
            scores = jax.nn.sigmoid(logits)
            sc = scores + e_bias
            n = x.shape[0]
            group_scores = lax.top_k(sc.reshape(n, G, E // G), 2)[0].sum(-1)
            grp_idx = lax.top_k(group_scores, TOPK_GROUP)[1]
            group_mask = jnp.zeros((n, G), jnp.float32).at[jnp.arange(n)[:, None], grp_idx].set(1.0)
            score_mask = jnp.repeat(group_mask, E // G, axis=1)
            masked = jnp.where(score_mask > 0, sc, 0.0)
            topk_idx = lax.top_k(masked, K)[1]
            topk_w = jnp.take_along_axis(scores, topk_idx, axis=1)
            topk_w = topk_w / (topk_w.sum(-1, keepdims=True) + 1e-20)
            return (topk_idx, topk_w * SCALE)

        def _moe_experts(x, topk_idx, topk_w, w_gate, w_up, w_down):
            n = x.shape[0]
            flat_e = topk_idx.reshape(-1)
            rows = jnp.repeat(jnp.arange(n), K)
            oh = jax.nn.one_hot(flat_e, E, dtype=jnp.int32)
            pos = jnp.cumsum(oh, axis=0) - oh
            pos = jnp.take_along_axis(pos, flat_e[:, None], axis=1)[:, 0]
            valid = (pos < CAP).astype(x.dtype)
            p = jnp.minimum(pos, CAP - 1)
            buf = jnp.zeros((E, CAP, H), x.dtype).at[flat_e, p].add(x[rows] * valid[:, None])
            g = jnp.einsum('ech,ehi->eci', buf, w_gate)
            u = jnp.einsum('ech,ehi->eci', buf, w_up)
            y = jnp.einsum('eci,eih->ech', jax.nn.silu(g) * u, w_down)
            y_tok = y[flat_e, p] * (topk_w.reshape(-1) * valid)[:, None]
            return jnp.zeros((n, H), x.dtype).at[rows].add(y_tok)

        def _shared_mlp(x, sh_gate, sh_up, sh_down):
            return jax.nn.silu(x @ sh_gate) * (x @ sh_up) @ sh_down
        key = jax.random.key(seed)
        ks = jax.random.split(key, 9)
        f32 = jnp.float32
        return {'hidden_states': jax.random.normal(ks[0], (B, S, H), f32), 'router_weight': jax.random.normal(ks[1], (E, H), f32) * (2.0 / H) ** 0.5, 'e_bias': jnp.zeros((E,), f32), 'w_gate': jax.random.normal(ks[2], (E, H, I), f32) * (1.0 / H) ** 0.5, 'w_up': jax.random.normal(ks[3], (E, H, I), f32) * (1.0 / H) ** 0.5, 'w_down': jax.random.normal(ks[4], (E, I, H), f32) * (1.0 / I) ** 0.5, 'sh_gate': jax.random.normal(ks[5], (H, I), f32) * (1.0 / H) ** 0.5, 'sh_up': jax.random.normal(ks[6], (H, I), f32) * (1.0 / H) ** 0.5, 'sh_down': jax.random.normal(ks[7], (I, H), f32) * (1.0 / I) ** 0.5}
    _L0_ffn_in = _L0_ffn_setup()
    _L0_c = _w((lambda *s: np.random.randn(*s).astype(np.float32) * 0.05)(2, 512))
    _L0_wmod = _w((lambda *s: np.random.randn(*s).astype(np.float32) * 0.05)(512, 6 * 512) * 512 ** (-0.5))
    _d = {'L0_attn_x': _L0_attn_in['x'], 'L0_attn_Wq': _L0_attn_in['Wq'], 'L0_attn_Wk': _L0_attn_in['Wk'], 'L0_attn_Wv': _L0_attn_in['Wv'], 'L0_attn_Wo': _L0_attn_in['Wo'], 'L0_attn_w_pre': _L0_attn_in['w_pre'], 'L0_attn_w_qn': _L0_attn_in['w_qn'], 'L0_attn_w_kn': _L0_attn_in['w_kn'], 'L0_ffn_router_weight': _L0_ffn_in['router_weight'], 'L0_ffn_e_bias': _L0_ffn_in['e_bias'], 'L0_ffn_w_gate': _L0_ffn_in['w_gate'], 'L0_ffn_w_up': _L0_ffn_in['w_up'], 'L0_ffn_w_down': _L0_ffn_in['w_down'], 'L0_ffn_sh_gate': _L0_ffn_in['sh_gate'], 'L0_ffn_sh_up': _L0_ffn_in['sh_up'], 'L0_ffn_sh_down': _L0_ffn_in['sh_down'], 'L0_c': _L0_c, 'L0_wmod': _L0_wmod}
    _x0 = _d['L0_attn_x']
    _d['L0_attn_x'] = jax.random.normal(jax.random.fold_in(jax.random.key(seed), 1), (2, 1024, 512), dtype=_x0.dtype)
    del _x0
    return _d

def reference(L0_attn_x, L0_attn_Wq, L0_attn_Wk, L0_attn_Wv, L0_attn_Wo, L0_attn_w_pre, L0_attn_w_qn, L0_attn_w_kn, L0_ffn_router_weight, L0_ffn_e_bias, L0_ffn_w_gate, L0_ffn_w_up, L0_ffn_w_down, L0_ffn_sh_gate, L0_ffn_sh_up, L0_ffn_sh_down, L0_c, L0_wmod):

    def _L0_attn_ref(x, Wq, Wk, Wv, Wo, w_pre, w_qn, w_kn):
        import jax, jax.numpy as jnp
        import numpy as np
        EPS = 1e-06
        ROPE_BASE = 10000.0

        def rmsnorm(x, w):
            return x * jax.lax.rsqrt(jnp.mean(x * x, axis=-1, keepdims=True) + EPS) * w

        def apply_rope(x, seq_axis_len):
            hd = x.shape[-1]
            inv_freq = 1.0 / ROPE_BASE ** (jnp.arange(0, hd, 2, dtype=jnp.float32) / hd)
            ang = jnp.arange(seq_axis_len, dtype=jnp.float32)[:, None] * inv_freq[None, :]
            cos = jnp.concatenate([jnp.cos(ang), jnp.cos(ang)], axis=-1)
            sin = jnp.concatenate([jnp.sin(ang), jnp.sin(ang)], axis=-1)
            x1, x2 = (x[..., :hd // 2], x[..., hd // 2:])
            rot = jnp.concatenate([-x2, x1], axis=-1)
            return x * cos + rot * sin
        B, S, D = x.shape
        H = 16
        hd = D // H
        scale = hd ** (-0.5)
        q = (x @ Wq.T).reshape(B, S, H, hd).transpose(0, 2, 1, 3)
        k = x @ Wk.T
        v = x @ Wv.T
        q = apply_rope(q, S)
        k = apply_rope(k, S)
        q = rmsnorm(q, w_qn)
        k = rmsnorm(k, w_kn)
        scores = jnp.einsum('bhqd,bkd->bhqk', q, k) * scale
        causal = jnp.tril(jnp.ones((S, S), dtype=bool))
        scores = jnp.where(causal, scores, jnp.finfo(scores.dtype).min)
        attn = jax.nn.softmax(scores, axis=-1)
        out = jnp.einsum('bhqk,bkd->bhqd', attn, v)
        out = out.transpose(0, 2, 1, 3).reshape(B, S, D)
        out = rmsnorm(out, w_pre)
        return out @ Wo.T

    def _L0_ffn_ref(hidden_states, router_weight, e_bias, w_gate, w_up, w_down, sh_gate, sh_up, sh_down):
        import jax, jax.numpy as jnp
        import numpy as np
        from jax import lax
        E = 64
        H = 512
        I = 176
        G = 8
        TOPK_GROUP = 4
        K = 8
        B, S = (2, 512)
        N = B * S
        CAP = 2 * N * K // E
        SCALE = 2.5

        def _route(x, router_weight, e_bias):
            logits = x.astype(jnp.float32) @ router_weight.astype(jnp.float32).T
            scores = jax.nn.sigmoid(logits)
            sc = scores + e_bias
            n = x.shape[0]
            group_scores = lax.top_k(sc.reshape(n, G, E // G), 2)[0].sum(-1)
            grp_idx = lax.top_k(group_scores, TOPK_GROUP)[1]
            group_mask = jnp.zeros((n, G), jnp.float32).at[jnp.arange(n)[:, None], grp_idx].set(1.0)
            score_mask = jnp.repeat(group_mask, E // G, axis=1)
            masked = jnp.where(score_mask > 0, sc, 0.0)
            topk_idx = lax.top_k(masked, K)[1]
            topk_w = jnp.take_along_axis(scores, topk_idx, axis=1)
            topk_w = topk_w / (topk_w.sum(-1, keepdims=True) + 1e-20)
            return (topk_idx, topk_w * SCALE)

        def _moe_experts(x, topk_idx, topk_w, w_gate, w_up, w_down):
            n = x.shape[0]
            flat_e = topk_idx.reshape(-1)
            rows = jnp.repeat(jnp.arange(n), K)
            oh = jax.nn.one_hot(flat_e, E, dtype=jnp.int32)
            pos = jnp.cumsum(oh, axis=0) - oh
            pos = jnp.take_along_axis(pos, flat_e[:, None], axis=1)[:, 0]
            valid = (pos < CAP).astype(x.dtype)
            p = jnp.minimum(pos, CAP - 1)
            buf = jnp.zeros((E, CAP, H), x.dtype).at[flat_e, p].add(x[rows] * valid[:, None])
            g = jnp.einsum('ech,ehi->eci', buf, w_gate)
            u = jnp.einsum('ech,ehi->eci', buf, w_up)
            y = jnp.einsum('eci,eih->ech', jax.nn.silu(g) * u, w_down)
            y_tok = y[flat_e, p] * (topk_w.reshape(-1) * valid)[:, None]
            return jnp.zeros((n, H), x.dtype).at[rows].add(y_tok)

        def _shared_mlp(x, sh_gate, sh_up, sh_down):
            return jax.nn.silu(x @ sh_gate) * (x @ sh_up) @ sh_down
        orig_shape = hidden_states.shape
        x = hidden_states.reshape(-1, H)
        topk_idx, topk_w = _route(x, router_weight, e_bias)
        moe_out = _moe_experts(x, topk_idx, topk_w.astype(x.dtype), w_gate, w_up, w_down)
        out = moe_out + _shared_mlp(x, sh_gate, sh_up, sh_down)
        return out.reshape(orig_shape)
    x = L0_attn_x
    mod = (_silu(L0_c) @ L0_wmod).reshape(L0_c.shape[0], 6, 1, -1)
    sa, ca, ga, sb, cb, gb = (mod[:, 0], mod[:, 1], mod[:, 2], mod[:, 3], mod[:, 4], mod[:, 5])
    ga = (2 * (ga >= 0) - 1) * jnp.maximum(jnp.abs(ga), 0.25)
    gb = (2 * (gb >= 0) - 1) * jnp.maximum(jnp.abs(gb), 0.25)
    h = _layernorm(x, axis=-1) * (1 + ca) + sa
    x = x + ga * _L0_attn_ref(h, L0_attn_Wq, L0_attn_Wk, L0_attn_Wv, L0_attn_Wo, L0_attn_w_pre, L0_attn_w_qn, L0_attn_w_kn)
    h = _layernorm(x, axis=-1) * (1 + cb) + sb
    x = x + gb * _L0_ffn_ref(h, L0_ffn_router_weight, L0_ffn_e_bias, L0_ffn_w_gate, L0_ffn_w_up, L0_ffn_w_down, L0_ffn_sh_gate, L0_ffn_sh_up, L0_ffn_sh_down)
    return x

_drawn_inputs = setup_inputs


def setup_inputs(seed=0):
    import zlib

    import numpy as np

    out = dict(_drawn_inputs(seed))
    spreads = {'L0_attn_w_pre': (1.0, 0.2),
     'L0_attn_w_qn': (1.0, 0.2),
     'L0_attn_w_kn': (1.0, 0.555),
     'L0_ffn_e_bias': (0.0, 0.1)}
    factors = {}
    for name, (base, spread) in spreads.items():
        noise = np.random.default_rng([zlib.crc32(name.encode()), seed]).standard_normal(out[name].shape)
        drawn = base * np.exp(spread * noise) if base else spread * noise
        out[name] = jnp.asarray(drawn.astype(out[name].dtype))
    for name, factor in factors.items():
        out[name] = (out[name] * factor).astype(out[name].dtype)
    return out
```

```python
import concourse.bass as bass
from concourse import mybir
from contextlib import ExitStack

B, S, D = 2, 1024, 512
H, HD = 16, 32
P = 128
NTOK = B * S
TPB = S // P
NT = NTOK // P
CH = 512
TPC = CH // P
QC = S // CH
KC = D // P
GH = 4
NG = H // GH
E, EI, TOPK, GROUPS, TOPG = 64, 176, 8, 8, 4
CAP = 2 * 1024 * TOPK // E
HALVES = CAP // P
NSLOT = E * CAP
ROUTED_SCALE = 2.5
LN_EPS, RMS_EPS = 1e-5, 1e-6
EXTRA = CAP
IA = 112
IB = EI - IA
IBP = 96
NSH = NTOK // CAP
UNITS_B = sum(NG * 2 * TPC * (qc + 1) for qc in range(QC))
PVS_B = UNITS_B // 2

C_ID, C_BIAS, C_UP = 0, 128, 256
C_COS = 384
C_SIN = C_COS + TPB * HD
C_EROW = C_SIN + TPB * HD
C_TRI = C_EROW + E
C_TRASH = C_TRI + GROUPS * GROUPS
NCONST = C_TRASH + TPC * TOPK


def build_program(nc, x, c_t, wmod, wq_t, wkv_t, wo_t, w_pre, w_qn, w_kn, router_t, e_bias,
                  gate_up, w_down, sh_gate_up, sh_down, consts, tokids, slot_init, out):
    f32, f32r, bf16, i32 = mybir.dt.float32, mybir.dt.float32r, mybir.dt.bfloat16, mybir.dt.int32
    ALU, ACT, AX = mybir.AluOpType, mybir.ActivationFunctionType, mybir.AxisListType
    ds = bass.ds

    h2_dram = nc.dram_tensor("h2_dram", [NTOK + EXTRA, D], f32).ap()
    acc_dram = nc.dram_tensor("acc_dram", [NTOK + EXTRA, D], f32).ap()
    slot_dram = nc.dram_tensor("slot_dram", [NSLOT + TPC * TOPK * P, 2], i32).ap()

    ctx = ExitStack()
    with ctx:
        def sem(name):
            return ctx.enter_context(nc.semaphore(name))

        def sb(where, name, shape, dt=f32):
            return where.enter_context(nc.sbuf_tensor(name, shape, dt))

        xres = sb(ctx, "xres", [P, NT, D])
        con = sb(ctx, "con", [P, NCONST])
        ga = sb(ctx, "ga", [P, B, D])
        sbias = sb(ctx, "sbias", [P, B, D])
        cscale = sb(ctx, "cscale", [P, B, D])
        gb = sb(ctx, "gb", [P, B, D])
        mcol = sb(ctx, "mcol", [P, 2, KC, B])
        ident_b = sb(ctx, "ident_b", [P, P], bf16)
        bias_b = sb(ctx, "bias_b", [P, P], bf16)
        upper_b = sb(ctx, "upper_b", [P, P], bf16)
        ones_b = sb(ctx, "ones_b", [P, P], bf16)
        ones = sb(ctx, "ones", [P, HD])
        mhalf = sb(ctx, "mhalf", [P, H + 1])
        tokid = sb(ctx, "tokid", [P, NT], i32)
        ebias = sb(ctx, "ebias", [P, E])
        wkq = sb(ctx, "wkq", [P, HD])
        wqn_s = sb(ctx, "wqn_s", [P, HD])
        wkn_s = sb(ctx, "wkn_s", [P, HD])
        wpre = sb(ctx, "wpre", [P, KC])
        silu_c = sb(ctx, "silu_c", [P, KC, B])
        rw = sb(ctx, "rw", [P, KC, E])
        wo = sb(ctx, "wo", [P, KC, D])

        att = ExitStack()
        qT = sb(att, "qT", [P, H, CH], f32r)
        kpad = sb(att, "kpad", [P, GH, S], f32r)
        probs = sb(att, "probs", [P, 2, GH, CH])
        qs = sb(att, "qs", [P, 2, H, P])
        kT = sb(att, "kT", [P, S], f32r)
        v_sb = sb(att, "v_sb", [P, TPB, HD])
        ks = sb(att, "ks", [P, P])
        kh4 = sb(att, "kh4", [P, GH, HD])
        qh = sb(att, "qh", [P, H, HD])
        qpT = sb(att, "qpT", [P, NG, P], f32r)
        oT = sb(att, "oT", [P, NG, CH])
        osq = sb(att, "osq", [P, NG, CH])
        scratch = sb(att, "scratch", [P, CH])
        wq = sb(att, "wq", [P, KC, D])
        wkv = sb(att, "wkv", [P, KC, 2 * HD])
        h2 = sb(att, "h2", [P, 2, D])
        h2T = sb(att, "h2T", [P, 2, KC, P])
        st = sb(att, "st", [P, TPC, 6])
        mv = sb(att, "mv", [P, TPC, 2])
        ve = sb(att, "ve", [P, TPC])
        rstd = sb(att, "rstd", [P, TPC])
        mv2 = sb(att, "mv2", [P, TPC, 2])
        ve2 = sb(att, "ve2", [P, TPC])
        rstd2 = sb(att, "rstd2", [P, TPC])
        oms = sb(att, "oms", [P, TPC])
        orstd = sb(att, "orstd", [P, TPC])
        ssq = sb(att, "ssq", [P, H + 1])
        ms = sb(att, "ms", [P, H + 1])
        rr = sb(att, "rr", [P, H + 1])
        nmax = sb(att, "nmax", [P, H])
        seen = sb(att, "seen", [P, E])
        seen_b = sb(att, "seen_b", [P, E], bf16)
        idx8 = sb(att, "idx8", [P, TPC, TOPK], i32)
        pay = sb(att, "pay", [P, TPC, TOPK, 2], i32)
        proj = ExitStack()
        qk = sb(proj, "qk", [P, H + 1, HD])
        t1 = sb(proj, "t1", [P, H + 1, HD])
        t2 = sb(proj, "t2", [P, H + 1, HD])
        qr = sb(proj, "qr", [P, H + 1, HD])
        xn = sb(proj, "xn", [P, 2, D])
        hT = sb(proj, "hT", [P, 2, KC, P])
        proj.close()
        rout = ExitStack()
        ex = sb(rout, "ex", [P, TPC, E])
        score = sb(rout, "score", [P, TPC, E])
        biased = sb(rout, "biased", [P, TPC, E])
        hi4 = sb(rout, "hi4", [P, TPC * GROUPS, 4])
        lo4 = sb(rout, "lo4", [P, TPC * GROUPS, 4])
        hi2 = sb(rout, "hi2", [P, TPC * GROUPS, 2])
        lo2 = sb(rout, "lo2", [P, TPC * GROUPS, 2])
        mid2 = sb(rout, "mid2", [P, TPC * GROUPS, 2])
        hi1 = sb(rout, "hi1", [P, TPC * GROUPS])
        lo1 = sb(rout, "lo1", [P, TPC * GROUPS])
        mid1 = sb(rout, "mid1", [P, TPC * GROUPS])
        gsum = sb(rout, "gsum", [P, TPC, GROUPS])
        cmp_a = sb(rout, "cmp_a", [P, TPC, GROUPS, GROUPS])
        cmp_b = sb(rout, "cmp_b", [P, TPC, GROUPS, GROUPS])
        grank = sb(rout, "grank", [P, TPC, GROUPS])
        masked = sb(rout, "masked", [P, TPC, E])
        top8 = sb(rout, "top8", [P, TPC, TOPK])
        marked = sb(rout, "marked", [P, TPC, E])
        sel = sb(rout, "sel", [P, TPC, E])
        sel_b = sb(rout, "sel_b", [P, TPC, E], bf16)
        selsum = sb(rout, "selsum", [P, E])
        wts = sb(rout, "wts", [P, TPC, E])
        wsum = sb(rout, "wsum", [P, TPC])
        wrec = sb(rout, "wrec", [P, TPC])
        hv = sb(rout, "hv", [P, TPC, E])
        valid = sb(rout, "valid", [P, TPC, E])
        key = sb(rout, "key", [P, TPC, E])
        key8 = sb(rout, "key8", [P, TPC, TOPK])
        eq8 = sb(rout, "eq8", [P, TOPK, E])
        w8 = sb(rout, "w8", [P, TPC, TOPK])
        miss8 = sb(rout, "miss8", [P, TPC, TOPK])
        rout.close()
        att.close()

        pre = ExitStack()
        wmod_s = sb(pre, "wmod_s", [P, KC, 6 * D])
        ct_s = sb(pre, "ct_s", [P, KC, B])
        csb = sb(pre, "csb", [P, KC, B, P])
        gate_t = sb(pre, "gate_t", [P, D])
        gate_a = sb(pre, "gate_a", [P, D])
        pre.close()

        moe = ExitStack()
        sh_gu = sb(moe, "sh_gu", [P, KC, 2 * EI])
        sh_da = sb(moe, "sh_da", [IA, D])
        sh_db = sb(moe, "sh_db", [IBP, D])
        e_gu = [sb(moe, f"e_gu{p}", [P, KC, 2 * EI]) for p in range(2)]
        e_da = [sb(moe, f"e_da{p}", [IA, D]) for p in range(2)]
        e_db = [sb(moe, f"e_db{p}", [IBP, D]) for p in range(2)]
        xg = [sb(moe, f"xg{p}", [P, HALVES, D]) for p in range(2)]
        xgT = [sb(moe, f"xgT{p}", [P, KC, CAP]) for p in range(2)]
        gact_a = [sb(moe, f"gact_a{p}", [IA, CAP]) for p in range(2)]
        gact_b = [sb(moe, f"gact_b{p}", [IB, CAP]) for p in range(2)]
        hid_a = [sb(moe, f"hid_a{p}", [IA, CAP]) for p in range(2)]
        hid_b = [sb(moe, f"hid_b{p}", [IBP, CAP]) for p in range(2)]
        y = [sb(moe, f"y{p}", [P, HALVES, D]) for p in range(2)]
        slots = sb(moe, "slots", [P, E * HALVES, 2], i32)
        slot_ix = [sb(moe, f"slot_ix{q}", [P, HALVES], i32) for q in range(4)]
        moe.close()
        fin = ExitStack()
        fin_acc = sb(fin, "fin_acc", [P, 2, TPC, D])
        fin.close()

        ps = ctx.enter_context(nc.psum_tensor("ps", [P, 8, 512], f32))

        def pair(n):
            return ps[:, 2 * n:2 * n + 2, :]

        ident = con[:, C_ID:C_ID + P]
        cos = con[:, C_COS:C_SIN].rearrange("p (t d) -> p t d", d=HD)
        sin = con[:, C_SIN:C_EROW].rearrange("p (t d) -> p t d", d=HD)
        erow = con[:, C_EROW:C_TRI]
        tri = con[:, C_TRI:C_TRASH].rearrange("p (a b) -> p a b", b=GROUPS)
        trash = con[:, C_TRASH:NCONST].rearrange("p (t j) -> p t j", j=TOPK)

        s_mod_in = sem("s_mod_in")
        s_small = sem("s_small")
        s_x = sem("s_x")
        s_init = sem("s_init")
        s_h2_out = [sem(f"s_h2_out{p}") for p in range(2)]
        s_slot = sem("s_slot")
        s_slots_in = sem("s_slots_in")
        s_sh_w = sem("s_sh_w")
        s_w = [sem(f"s_w{p}") for p in range(2)]
        s_xg = [sem(f"s_xg{p}") for p in range(2)]
        s_eg = [sem(f"s_eg{p}") for p in range(2)]
        s_added = sem("s_added")
        s_fin_in = [sem(f"s_fin_in{p}") for p in range(2)]
        s_out = sem("s_out")
        s_silu, s_csb, s_mod, s_modv, s_ready = (sem(n) for n in ("s_silu", "s_csb", "s_mod", "s_modv", "s_ready"))
        s_zero = sem("s_zero")
        (s_var, s_rstd, s_xn, s_xT, s_hT, s_q, s_qk, s_rope, s_ms, s_rr, s_parts, s_pack, s_packT, s_mm,
         s_max, s_nmax, s_st, s_qT) = (sem("s_" + n) for n in (
             "var", "rstd", "xn", "xT", "hT", "q", "qk", "rope", "ms", "rr", "parts", "pack", "packT", "mm",
             "max", "nmax", "st", "qT"))
        s_sc, s_exp, s_mask, s_pv, s_on, s_sq = (sem("s_" + n) for n in ("sc", "exp", "mask", "pv", "on", "sq"))
        (s_oss, s_oms, s_orstd, s_at, s_atd, s_var2, s_rstd2, s_h2, s_h2t, s_h2T, s_lg, s_ex, s_sel, s_pos,
         s_pay) = (sem("s_" + n) for n in (
             "oss", "oms", "orstd", "at", "atd", "var2", "rstd2", "h2", "h2t", "h2T", "lg", "ex", "sel", "pos",
             "pay"))
        s_T, s_xa, s_xd, s_gu, s_act, s_hid, s_dn, s_ya, s_yd = (sem("s_e" + n) for n in (
            "T", "xa", "xd", "gu", "act", "hid", "dn", "ya", "yd"))
        s_ix, s_fin = sem("s_ix"), sem("s_fin")
        s_yfree = sem("s_yfree")
        s_step = sem("s_step")

        def hold(eng, semaphore, value):
            eng.wait_ge(semaphore, value)
            eng.sem_inc(s_step, 1)

        def xtile(t):
            return xres[:, ds(t, 1), :].rearrange("p a n -> p (a n)")

        def rows(b, tile):
            return tile[:, ds(b, 1), :].rearrange("p a n -> p (a n)")

        N_SMALL = 11

        block = ctx.enter_context(nc.Block())

        @block.sync
        def _(sp):
            sp.dma_start(ct_s[:, :, :], c_t).then_inc(s_mod_in, 16)
            sp.dma_start(wmod_s[:, :, :], wmod.rearrange("(c p) n -> p c n", p=P)).then_inc(s_mod_in, 16)
            xv = x.rearrange("(t p) n -> p t n", p=P)
            for c in range(4):
                sp.dma_start(xres[:, 4 * c:4 * c + 4, :], xv[:, 4 * c:4 * c + 4, :]).then_inc(s_x, 16)
            sp.wait_ge(s_zero, 1)
            zb = qs[:, 0, 0:D // P, :].rearrange("p h n -> p (h n)").unsqueeze(1)
            sp.dma_start(h2_dram[NTOK:NTOK + EXTRA, :].rearrange("(t p) n -> p t n", p=P),
                         zb.to_broadcast([P, EXTRA // P, D])).then_inc(s_init, 16)
            sp.dma_start(acc_dram.rearrange("(t p) n -> p t n", p=P),
                         zb.to_broadcast([P, (NTOK + EXTRA) // P, D])).then_inc(s_init, 16)
            sp.dma_start(slot_dram[0:NSLOT, :].rearrange("(p s) c -> p (s c)", p=P), slot_init).then_inc(s_init, 16)
            with sp.Fori(0, B) as b:
                for i in range(TPB):
                    t = b * TPB + i
                    sp.wait_ge(s_h2, t + 1)
                    sp.dma_start(h2_dram[ds(t * P, P), :], h2[:, i % 2, :]).then_inc(s_h2_out[i % 2], 16)
            sp.wait_ge(s_lg, NT)
            sp.dma_start(sh_gu[:, :, :], sh_gate_up).then_inc(s_sh_w, 16)
            sp.dma_start(sh_da[:, :], sh_down[0:IA, :]).then_inc(s_sh_w, 16)
            sp.dma_start(sh_db[0:IB, :], sh_down[IA:EI, :]).then_inc(s_sh_w, 16)

            def load_expert(e, p):
                sp.dma_start(e_gu[p][:, :, :], gate_up[ds(e, 1), :, :, :].rearrange("a p c n -> p (a c) n"))\
                  .then_inc(s_w[p], 16)
                sp.dma_start(e_da[p][:, :], w_down[ds(e, 1), 0:IA, :].rearrange("a i n -> (a i) n"))\
                  .then_inc(s_w[p], 16)
                sp.dma_start(e_db[p][0:IB, :], w_down[ds(e, 1), IA:EI, :].rearrange("a i n -> (a i) n"))\
                  .then_inc(s_w[p], 16)

            for p in range(2):
                sp.wait_ge(s_h2_out[p], 16 * NT // 2)
            with sp.Fori(0, NSH // 2) as i:
                for p in range(2):
                    n = i * 2 + p
                    sp.wait_ge(s_T, n + 1)
                    for h in range(HALVES):
                        sp.dma_start(xg[p][:, h, :], h2_dram[ds(n * CAP + h * P, P), :]).then_inc(s_xg[p], 16)
            for p in range(2):
                load_expert(p, p)
            with sp.Fori(0, E // 2 - 1) as i:
                for p in range(2):
                    e = i * 2 + p
                    sp.wait_ge(s_dn, e + NSH + 3)
                    load_expert(e + 2, p)
            sp.wait_ge(s_added, 16 * HALVES * E)
            av = acc_dram[0:NTOK, :].rearrange("(t p) n -> p t n", p=P)
            ov = out.rearrange("(t p) n -> p t n", p=P)
            for c in range(2):
                sp.dma_start(fin_acc[:, c, :, :], av[:, TPC * c:TPC * c + TPC, :]).then_inc(s_fin_in[c], 16)
            for c in range(NT // TPC):
                sp.wait_ge(s_fin, c + 1)
                sp.dma_start(ov[:, TPC * c:TPC * c + TPC, :], xres[:, TPC * c:TPC * c + TPC, :]).then_inc(s_out, 16)
                if c + 2 < NT // TPC:
                    sp.dma_start(fin_acc[:, c % 2, :, :], av[:, TPC * (c + 2):TPC * (c + 3), :])\
                      .then_inc(s_fin_in[c % 2], 16)
            sp.wait_ge(s_out, 16 * (NT // TPC))

        @block.gpsimd
        def _(pool):
            def inv_sqrt(dst, src, n):
                return pool.tensor_tensor(dst, src, mhalf[:, 0:n], ALU.pow)

            pool.wait_ge(s_ready, 1)
            pool.wait_ge(s_init, 48)
            with pool.Fori(0, B) as b:
                for qc in range(QC):
                    c = b * QC + qc
                    hold(pool, s_var, c + 1)
                    inv_sqrt(rstd[:, :], ve[:, :], TPC).then_inc(s_rstd, 1)
                    for ii in range(TPC):
                        hold(pool, s_ms, b * TPB + qc * TPC + ii + 1)
                        inv_sqrt(rr[:, :], ms[:, :], H + 1).then_inc(s_rr, 1)
                    kts = TPC * (qc + 1)
                    with pool.Fori(0, NG) as g:
                        for dd in range(TPC):
                            kt = TPC * qc + dd
                            unit = b * UNITS_B + qc * (NG * 2 * TPC) + g * (2 * kts) + 2 * kt
                            hold(pool, s_exp, unit + 4)
                            tile = probs[:, kt % 2, :, dd * P:dd * P + P]
                            pool.affine_select(out=tile, in_=tile, compare_op=ALU.is_ge, fill=0.0, base=0,
                                               pattern=[[0, GH], [1, P]], channel_multiplier=-1).then_inc(s_mask, 1)
                    hold(pool, s_oms, c + 1)
                    inv_sqrt(orstd[:, :], oms[:, :], TPC).then_inc(s_orstd, 1)
                    hold(pool, s_var2, c + 1)
                    inv_sqrt(rstd2[:, :], ve2[:, :], TPC).then_inc(s_rstd2, 1)
                    hold(pool, s_pay, c + 1)
                    for ii in range(TPC):
                        for j in range(TOPK):
                            pool.indirect_dma_start(
                                out=slot_dram, out_offset=bass.IndirectOffsetOnAxis(ap=idx8[:, ii, j:j + 1], axis=0),
                                in_=pay[:, ii, j, :], in_offset=None).then_inc(s_slot, 16)
            pool.wait_ge(s_slot, 16 * NT * TOPK)
            pool.dma_start(slots[:, :, :], slot_dram[0:NSLOT, :].rearrange("(p s) c -> p s c", p=P))\
                .then_inc(s_slots_in, 16)
            pool.wait_ge(s_slots_in, 16)

            def gather(e, q):
                n = e + NSH
                hold(pool, s_T, n + 1)
                pool.tensor_copy(slot_ix[q][:, :], slots[:, ds(e * HALVES, HALVES), 0]).then_inc(s_ix, 1)
                hold(pool, s_ix, e + 1)
                for h in range(HALVES):
                    pool.indirect_dma_start(
                        out=xg[q % 2][:, h, :], out_offset=None, in_=h2_dram,
                        in_offset=bass.IndirectOffsetOnAxis(ap=slot_ix[q][:, h:h + 1], axis=0)).then_inc(s_eg[q % 2], 16)

            def add_rows(e, q):
                hold(pool, s_ya, e + NSH + 1)
                hold(pool, s_yd, e + NSH + 1)
                pool.wait_ge(s_added, e * (16 * HALVES))
                pool.sem_inc(s_yfree, 1)
                for h in range(HALVES):
                    pool.indirect_dma_start(
                        out=acc_dram, out_offset=bass.IndirectOffsetOnAxis(ap=slot_ix[q][:, h:h + 1], axis=0),
                        in_=y[q % 2][:, h, :], in_offset=None, compute_op=ALU.add).then_inc(s_added, 16)

            gather(0, 0)
            with pool.Fori(0, E // 4 - 1) as i:
                for q in range(4):
                    gather(i * 4 + (q + 1), (q + 1) % 4)
                    add_rows(i * 4 + q, q)
            for q in range(4):
                e = E - 4 + q
                if q < 3:
                    gather(e + 1, q + 1)
                add_rows(e, q)

        @block.scalar
        def _(act):
            act.dma_start(con[:, :], consts).then_inc(s_small, 16)
            act.dma_start(wq[:, :, :], wq_t).then_inc(s_small, 16)
            act.dma_start(wkv[:, :, :], wkv_t).then_inc(s_small, 16)
            act.dma_start(wo[:, :, :], wo_t).then_inc(s_small, 16)
            act.dma_start(rw[:, :, :], router_t).then_inc(s_small, 16)
            act.dma_start(wpre[:, :], w_pre).then_inc(s_small, 16)
            act.dma_start(tokid[:, :], tokids).then_inc(s_small, 16)
            act.dma_start(ebias[:, :], e_bias.unsqueeze(0).to_broadcast([P, E])).then_inc(s_small, 16)
            act.dma_start(wqn_s[:, :], w_qn.unsqueeze(0).to_broadcast([P, HD])).then_inc(s_small, 16)
            act.dma_start(wkn_s[:, :], w_kn.unsqueeze(0).to_broadcast([P, HD])).then_inc(s_small, 16)
            act.wait_ge(s_mod_in, 32)
            act.activation(silu_c[:, :, :], ct_s[:, :, :], ACT.Silu).then_inc(s_silu, 1)

            def project(b, i):
                t = b * TPB + i
                hold(act, s_xT, t + 1)
                hold(act, s_q, b * TPB + max(i - 1, 0))
                for cc in range(KC):
                    last = act.activation(hT[:, i % 2, cc, :], ps[:, 6, cc * P:(cc + 1) * P], ACT.Identity,
                                          bias=mcol[:, 0, cc, ds(b, 1)], scale=mcol[:, 1, cc, ds(b, 1)])
                last.then_inc(s_hT, 1)
                hold(act, s_rope, t)
                hold(act, s_on, b * (QC * NG))
                act.wait_ge(s_q, t + 1)
                act.activation(qk[:, 0:H, :], ps[:, 4, :].rearrange("p (h d) -> p h d", d=HD), ACT.Copy)
                act.activation(qk[:, H, :], ps[:, 7, 0:HD], ACT.Copy)
                act.activation(v_sb[:, i, :], ps[:, 7, HD:2 * HD], ACT.Copy).then_inc(s_qk, 1)

            def pack(b, i):
                t = b * TPB + i
                act.wait_ge(s_pack, t + 1)
                act.activation(qpT[:, :, :], ps[:, 5, :].rearrange("p (g t) -> p g t", t=P), ACT.Copy)
                act.activation(kT[:, i * P:i * P + P], ps[:, 7, 0:P], ACT.Copy)
                for j in range(GH):
                    r = slice(HD * j, HD * j + HD)
                    last = act.activation(kpad[r, j, i * P:i * P + P], ps[r, 7, P:2 * P], ACT.Copy)
                last.then_inc(s_packT, 1)

            def stack(b, i):
                ii = i % TPC
                for q4 in range(NG):
                    act.wait_ge(s_st, (b * TPB + i) * NG + q4 + 1)
                    act.activation(qT[:, GH * q4:GH * q4 + GH, ii * P:ii * P + P],
                                   ps[:, 5 + 2 * (q4 % 2), :].rearrange("p (g t) -> p g t", t=P), ACT.Copy)\
                       .then_inc(s_qT, 1)

            act.wait_ge(s_modv, 1)
            act.sem_inc(s_exp, 2)
            with act.Fori(0, B) as b:
                for qc in range(QC):
                    i0 = qc * TPC
                    c = b * QC + qc
                    project(b, i0)
                    for ii in range(TPC):
                        pack(b, i0 + ii)
                        if ii + 1 < TPC:
                            project(b, i0 + ii + 1)
                        stack(b, i0 + ii)
                    kts = TPC * (qc + 1)
                    with act.Fori(0, NG) as g:
                        for kt in range(kts):
                            off = max(0, kt - TPC * qc) * P
                            pv = b * PVS_B + qc * (NG * TPC) + g * kts + kt
                            hold(act, s_pv, pv + 1)
                            for pr in range(2):
                                unit = b * UNITS_B + qc * (NG * 2 * TPC) + g * (2 * kts) + (2 * kt + pr)
                                act.wait_ge(s_sc, unit + 1)
                                act.activation(probs[:, kt % 2, 2 * pr:2 * pr + 2, off:CH],
                                               pair(pr)[:, :, off:CH], ACT.Exp).then_inc(s_exp, 1)
                    for ii in range(TPC):
                        i = i0 + ii
                        t = b * TPB + i
                        hold(act, s_lg, b * TPB + max(i - 1, 0))
                        act.wait_ge(s_h2t, t + 1)
                        act.activation(h2T[:, ii % 2, :, :], ps[:, 6 - 2 * (ii % 2), :].rearrange("p (c t) -> p c t", t=P),
                                       ACT.Copy).then_inc(s_h2T, 1)
                    act.wait_ge(s_lg, (c + 1) * TPC)
                    act.activation(ex[:, :, :], ps[:, 5, 0:TPC * E].rearrange("p (t e) -> p t e", e=E), ACT.Exp,
                                   scale=-1.0).then_inc(s_ex, 1)

            def x_out(n, p):
                hold(act, s_gu, n + 1)
                act.wait_ge(s_T, n + 3)
                act.activation(xgT[p][:, 0:2, :], ps[:, 0, :].rearrange("p (c t) -> p c t", t=CAP), ACT.Copy)\
                   .then_inc(s_xa, 1)

            def gates(n, p):
                hold(act, s_hid, n + 1)
                act.wait_ge(s_gu, n + 3)
                act.activation(gact_a[p][:, :], ps[0:IA, 2 + p, 0:CAP], ACT.Silu)
                act.activation(gact_b[p][:, :], ps[0:IB, 4 + p, 0:CAP], ACT.Silu).then_inc(s_act, 1)

            x_out(0, 0)
            with act.Fori(0, NSH // 2) as i:
                for p in range(2):
                    n = i * 2 + p
                    gates(n, p)
                    x_out(n + 1, 1 - p)

            def weighted(e, p):
                hold(act, s_yfree, e)
                act.wait_ge(s_slots_in, 16)
                hold(act, s_dn, e + NSH + 3)
                act.activation(y[p][:, 0, :], ps[:, 6, :], ACT.Copy,
                               scale=slots[:, ds(e * HALVES, 1), 1].bitcast(f32)).then_inc(s_ya, 1)

            with act.Fori(0, E // 2 - 1) as i:
                for p in range(2):
                    gates(i * 2 + (p + NSH), p)
                    x_out(i * 2 + (p + NSH + 1), 1 - p)
                    weighted(i * 2 + p, p)
            for p in range(2):
                e = E - 2 + p
                gates(e + NSH, p)
                if p == 0:
                    x_out(e + NSH + 1, 1)
                weighted(e, p)

        @block.tensor
        def _(pe):
            pe.wait_ge(s_silu, 1)
            for m in range(2):
                for cc in range(KC):
                    for k in range(KC):
                        col = (m * KC + cc) * B
                        last = pe.matmul(ps[:, 0, col:col + B], wmod_s[:, k, m * D + cc * P:m * D + (cc + 1) * P],
                                         silu_c[:, k, :], start=(k == 0), stop=(k == KC - 1))
            last.then_inc(s_mod, 1)
            pe.wait_ge(s_csb, 1)
            for n, m in enumerate((2, 3, 4, 5)):
                for b in range(B):
                    u = n * B + b
                    if u >= 4:
                        pe.wait_ge(s_modv, u - 2)
                    for k in range(KC):
                        last = pe.matmul(ps[:, 1 + u % 4, :], csb[:, k, b, :], wmod_s[:, k, m * D:(m + 1) * D],
                                         start=(k == 0), stop=(k == KC - 1))
                    last.then_inc(s_mod, 1)
            pe.wait_ge(s_modv, 9)
            pe.wait_ge(s_small, 160)
            pe.wait_ge(s_ready, 1)
            pe.sem_inc(s_pv, 2)

            def project(b, i):
                t = b * TPB + i
                pe.wait_ge(s_xn, t + 1)
                for cc in range(KC):
                    last = pe.transpose(ps[:, 6, cc * P:(cc + 1) * P], xn[:, i % 2, cc * P:(cc + 1) * P], ident)
                last.then_inc(s_xT, 1)
                pe.wait_ge(s_hT, t + 1)
                if i % TPC == 0:
                    pe.wait_ge(s_atd, b * TPB + i)
                for cc in range(KC):
                    pe.matmul(ps[:, 4, :], hT[:, i % 2, cc, :], wq[:, cc, :], start=(cc == 0), stop=(cc == KC - 1))
                pe.wait_ge(s_packT, t)
                for cc in range(KC):
                    last = pe.matmul(ps[:, 7, 0:2 * HD], hT[:, i % 2, cc, :], wkv[:, cc, :],
                                     start=(cc == 0), stop=(cc == KC - 1))
                last.then_inc(s_q, 1)

            def pack(b, i):
                t = b * TPB + i
                pe.wait_ge(s_parts, t + 1)
                if i % TPC == 0:
                    pe.wait_ge(s_pay, (b * TPB + i) // TPC if isinstance(b, int) else b * QC + i // TPC)
                pe.wait_ge(s_qk, t + 1)
                pe.wait_ge(s_qT, t * NG)
                pe.transpose(ps[:, 7, 0:P], ks[:, :], ident)
                pe.transpose(ps[:, 7, P:2 * P], kh4[:, :, :].rearrange("p j d -> p (j d)"), ident)
                for g in range(NG):
                    last = pe.transpose(ps[:, 5, g * P:(g + 1) * P], qh[:, GH * g:GH * g + GH, :].rearrange("p j d -> p (j d)"), ident)
                last.then_inc(s_pack, 1)

            def row_max(b, i):
                t = b * TPB + i
                pe.wait_ge(s_packT, t + 1)
                for h in range(H):
                    if h < 2:
                        pe.wait_ge(s_max, t * H)
                    else:
                        pe.wait_ge(s_max, t * H + (h - 1))
                    flat = pair(h % 2).rearrange("p a n -> p (a n)")
                    width = (i + 1) * P
                    for lo in range(0, width, 512):
                        hi = min(lo + 512, width)
                        pe.matmul(flat[:, lo:hi], qpT[:, h // GH, :], kpad[:, h % GH, lo:hi], start=True,
                                  stop=(hi < width))
                    pe.matmul(flat[:, width - P:width], ident_b[:, :], bias_b[:, :], start=False, stop=True)\
                      .then_inc(s_mm, 1)

            def stack(b, i):
                t = b * TPB + i
                pe.wait_ge(s_nmax, t + 1)
                if i % TPC < TPC - 1:
                    pe.wait_ge(s_qk, t + 2)
                for q4 in range(NG):
                    if q4 >= 2:
                        pe.wait_ge(s_qT, t * NG + (q4 - 1))
                    for j in range(GH):
                        last = pe.transpose(ps[:, 5 + 2 * (q4 % 2), j * P:(j + 1) * P], qs[:, i % 2, GH * q4 + j, :], ident)
                    last.then_inc(s_st, 1)

            def attend(b, qc):
                kts = TPC * (qc + 1)
                hold(pe, s_qT, (b * TPB + (qc + 1) * TPC) * NG)

                def scores(g, kt):
                    off = max(0, kt - TPC * qc) * P
                    for pr in range(2):
                        unit = b * UNITS_B + qc * (NG * 2 * TPC) + g * (2 * kts) + (2 * kt + pr)
                        hold(pe, s_exp, unit + 1)
                        for jj in range(2):
                            last = pe.matmul(ps[:, 2 * pr + jj, off:CH], kT[:, kt * P:kt * P + P],
                                             qT[:, ds(g * GH + (2 * pr + jj), 1), off:CH], start=True, stop=True)
                        last.then_inc(s_sc, 1)

                def values(g, kt):
                    off = max(0, kt - TPC * qc) * P
                    unit = b * UNITS_B + qc * (NG * 2 * TPC) + g * (2 * kts) + 2 * kt
                    if kt == 0:
                        pe.wait_ge(s_on, b * (QC * NG) + qc * NG + g)
                    if kt >= TPC * qc:
                        pe.wait_ge(s_mask, b * (QC * NG * TPC) + qc * (NG * TPC) + g * TPC + (kt - TPC * qc + 1))
                    else:
                        pe.wait_ge(s_exp, unit + 4)
                    for bank, left in ((4, v_sb[:, kt, :]), (5, ones[:, :])):
                        for j in range(GH):
                            last = pe.matmul(ps[HD * j:HD * j + HD, bank, off:CH], left, probs[:, kt % 2, j, off:CH],
                                             start=(kt == 0), stop=(kt == kts - 1))
                    last.then_inc(s_pv, 1)

                with pe.Fori(0, NG) as g:
                    for kt in range(kts):
                        scores(g, kt)
                        if kt:
                            values(g, kt - 1)
                    values(g, kts - 1)

            def out_project(b, qc):
                c = b * QC + qc
                pe.wait_ge(s_sq, (c + 1) * NG)
                for ii in range(TPC):
                    for g in range(NG):
                        last = pe.matmul(ps[:, 6, ii:ii + 1], osq[:, g, ii * P:ii * P + P], ones[:, 0:1],
                                         start=(g == 0), stop=(g == NG - 1))
                last.then_inc(s_oss, 1)
                for ii in range(TPC):
                    if ii >= 2:
                        pe.wait_ge(s_atd, c * TPC + (ii - 1))
                    for g in range(NG):
                        last = pe.matmul(ps[:, 7 - 3 * (ii % 2), :], oT[:, g, ii * P:ii * P + P], wo[:, g, :],
                                         start=(g == 0), stop=(g == NG - 1))
                    last.then_inc(s_at, 1)

            def route(b, qc):
                c = b * QC + qc

                def turn(ii):
                    t = c * TPC + ii
                    pe.wait_ge(s_h2, t + 1)
                    if ii >= 2:
                        pe.wait_ge(s_h2T, c * TPC + (ii - 1))
                    for cc in range(KC):
                        last = pe.transpose(ps[:, 6 - 2 * (ii % 2), cc * P:(cc + 1) * P],
                                            h2[:, ii % 2, cc * P:(cc + 1) * P], ident)
                    last.then_inc(s_h2t, 1)

                def logits(ii):
                    t = c * TPC + ii
                    pe.wait_ge(s_h2T, t + 1)
                    for cc in range(KC):
                        last = pe.matmul(ps[:, 5, ii * E:(ii + 1) * E], h2T[:, ii % 2, cc, :], rw[:, cc, :],
                                         start=(cc == 0), stop=(cc == KC - 1))
                    last.then_inc(s_lg, 1)

                turn(0)
                for ii in range(TPC):
                    if ii + 1 < TPC:
                        turn(ii + 1)
                    logits(ii)
                pe.wait_ge(s_sel, c + 1)
                for ii in range(TPC):
                    dst = ps[:, 7, ii * E:(ii + 1) * E]
                    pe.matmul(dst, ones_b[:, :], seen_b[:, :], start=True, stop=False)
                    for before in range(ii):
                        pe.matmul(dst, ones_b[:, :], sel_b[:, before, :], start=False, stop=False)
                    last = pe.matmul(dst, upper_b[:, :], sel_b[:, ii, :], start=False, stop=True)
                last.then_inc(s_pos, 1)

            with pe.Fori(0, B) as b:
                for qc in range(QC):
                    i0 = qc * TPC
                    project(b, i0)
                    for ii in range(TPC):
                        pack(b, i0 + ii)
                        if ii + 1 < TPC:
                            project(b, i0 + ii + 1)
                        row_max(b, i0 + ii)
                        stack(b, i0 + ii)
                    attend(b, qc)
                    out_project(b, qc)
                    route(b, qc)

            pe.sem_inc(s_T, 2)
            pe.sem_inc(s_gu, 2)
            pe.sem_inc(s_dn, 2)

            def turn_rows(n, p, arrived, loads):
                pe.wait_ge(s_xa, n)
                pe.wait_ge(s_xd, n)
                pe.wait_ge(arrived[p], loads * 32)
                for cc in range(KC):
                    for h in range(HALVES):
                        col = (cc % 2) * CAP + h * P
                        last = pe.transpose(ps[:, cc // 2, col:col + P], xg[p][:, h, cc * P:(cc + 1) * P], ident)
                last.then_inc(s_T, 1)

            def up(n, p, w):
                pe.wait_ge(s_xa, n + 1)
                pe.wait_ge(s_xd, n + 1)
                pe.wait_ge(s_hid, n + 1)
                for s, col in enumerate((0, IA + 2 * IB)):
                    for cc in range(KC):
                        pe.matmul(ps[0:IA, 2 + p, s * CAP:(s + 1) * CAP], w[:, cc, col:col + IA], xgT[p][:, cc, :],
                                  start=(cc == 0), stop=(cc == KC - 1))
                for cc in range(KC):
                    last = pe.matmul(ps[:, 4 + p, 0:CAP], w[:, cc, IA:IA + 2 * IB], xgT[p][:, cc, :],
                                     start=(cc == 0), stop=(cc == KC - 1))
                last.then_inc(s_gu, 1)

            def down(n, p, wa, wb):
                pe.wait_ge(s_hid, n + 3)
                pe.wait_ge(s_ya, n)
                pe.wait_ge(s_yd, n)
                for h in range(HALVES):
                    pe.matmul(ps[:, 6 + h, :], hid_a[p][:, h * P:(h + 1) * P], wa[:, :], start=True, stop=False)
                    last = pe.matmul(ps[:, 6 + h, :], hid_b[p][:, h * P:(h + 1) * P], wb[:, :], start=False, stop=True)
                last.then_inc(s_dn, 1)

            turn_rows(0, 0, s_xg, 1)
            pe.wait_ge(s_sh_w, 48)
            with pe.Fori(0, NSH // 2 - 1) as i:
                for p in range(2):
                    n = i * 2 + p
                    up(n, p, sh_gu)
                    turn_rows(n + 1, 1 - p, s_xg, i + (1 + p))
                    down(n, p, sh_da, sh_db)
            for p in range(2):
                n = NSH - 2 + p
                up(n, p, sh_gu)
                turn_rows(n + 1, 1 - p, s_xg if p == 0 else s_eg, NSH // 2 if p == 0 else 1)
                down(n, p, sh_da, sh_db)

            def expert(e, p, loads, last):
                n = e + NSH
                pe.wait_ge(s_w[p], loads * 48)
                up(n, p, e_gu[p])
                if not last:
                    turn_rows(n + 1, 1 - p, s_eg, loads + p)
                down(n, p, e_da[p], e_db[p])

            with pe.Fori(0, E // 2 - 1) as i:
                for p in range(2):
                    expert(i * 2 + p, p, i + 1, False)
            for p in range(2):
                expert(E - 2 + p, p, E // 2, p == 1)

        @block.vector
        def _(dve):
            dve.memset(qs[:, :, :, :], 0.0).then_inc(s_zero, 1)
            dve.memset(ones[:, :], 1.0)
            dve.memset(ones_b[:, :], 1.0)
            dve.memset(mhalf[:, :], -0.5)
            dve.memset(ks[:, :], 0.0)
            dve.memset(seen[:, :], 0.0)
            dve.memset(seen_b[:, :], 0.0)
            dve.wait_ge(s_small, 160)
            dve.tensor_copy(ident_b[:, :], ident)
            dve.tensor_copy(bias_b[:, :], con[:, C_BIAS:C_BIAS + P])
            dve.tensor_copy(upper_b[:, :], con[:, C_UP:C_UP + P])
            dve.drain()
            dve.memset(ks[:, 3 * HD:3 * HD + 2], 1.0)
            dve.scalar_tensor_tensor(wkq[:, :], wqn_s[:, :], float(HD) ** -0.5, wkn_s[:, :], ALU.mult, ALU.mult)
            for cc in range(KC):
                dve.tensor_scalar(wo[:, cc, :], wo[:, cc, :], wpre[:, cc:cc + 1], None, ALU.mult)
            dve.wait_ge(s_silu, 1)
            for k in range(KC):
                last = dve.tensor_copy(csb[:, k, :, :], silu_c[:, k, :].unsqueeze(2).to_broadcast([P, B, P]))
            last.then_inc(s_csb, 1)
            dve.wait_ge(s_mod, 1)
            cols = ps[:, 0, 0:2 * KC * B].rearrange("p (m c b) -> p m c b", m=2, c=KC)
            dve.tensor_copy(mcol[:, 0, :, :], cols[:, 0, :, :])
            dve.tensor_scalar(mcol[:, 1, :, :], cols[:, 1, :, :], 1.0, None, ALU.add).then_inc(s_modv, 1)
            for n, dst in enumerate((ga, sbias, cscale, gb)):
                for b in range(B):
                    u = n * B + b
                    dve.wait_ge(s_mod, u + 2)
                    src = ps[:, 1 + u % 4, :]
                    if dst is sbias:
                        dve.tensor_copy(dst[:, b, :], src).then_inc(s_modv, 1)
                    elif dst is cscale:
                        dve.tensor_scalar(dst[:, b, :], src, 1.0, None, ALU.add).then_inc(s_modv, 1)
                    else:
                        dve.drain()
                        dve.tensor_scalar(gate_t[:, :], src, 0.0, 0.5, ALU.is_ge, ALU.subtract)
                        dve.drain()
                        dve.scalar_tensor_tensor(gate_a[:, :], gate_t[:, :], 2.0, src, ALU.mult, ALU.mult)\
                           .then_inc(s_modv, 1)
                        dve.drain()
                        dve.tensor_scalar(gate_a[:, :], gate_a[:, :], 0.25, 2.0, ALU.max, ALU.mult)
                        dve.drain()
                        dve.tensor_tensor(dst[:, b, :], gate_t[:, :], gate_a[:, :], ALU.mult)
            dve.memset(kpad[:, :, :].bitcast(f32), 0.0)
            dve.drain()
            dve.sem_inc(s_ready, 1)
            dve.wait_ge(s_init, 48)
            dve.wait_ge(s_x, 64)

            def chunk_stats(b, i0, mean_var, var_eps, ready):
                for ii in range(TPC):
                    dve.bn_stats(st[:, ii, :], xtile(b * TPB + (i0 + ii)))
                dve.drain()
                for ii in range(TPC):
                    dve.bn_aggr(mean_var[:, ii, :], st[:, ii, :])
                dve.drain()
                dve.tensor_scalar(var_eps[:, :], mean_var[:, :, 1], LN_EPS, None, ALU.add).then_inc(ready, 1)

            def normalise(b, i):
                ii = i % TPC
                dve.wait_ge(s_xT, b * TPB + max(i - 1, 0))
                if ii == 0:
                    dve.wait_ge(s_rstd, b * QC + i // TPC + 1)
                dve.tensor_scalar(xn[:, i % 2, :], xtile(b * TPB + i), mv[:, ii, 0:1], rstd[:, ii:ii + 1],
                                  ALU.subtract, ALU.mult).then_inc(s_xn, 1)

            def rotate(b, i):
                t = b * TPB + i
                half = HD // 2
                shape = [P, H + 1, half]
                dve.wait_ge(s_qk, t + 1)
                dve.tensor_tensor(t1[:, :, :], qk[:, :, :], cos[:, i, :].unsqueeze(1).to_broadcast([P, H + 1, HD]), ALU.mult)
                dve.tensor_tensor(t2[:, :, 0:half], qk[:, :, half:HD],
                                  sin[:, i, 0:half].unsqueeze(1).to_broadcast(shape), ALU.mult)
                dve.tensor_tensor(t2[:, :, half:HD], qk[:, :, 0:half],
                                  sin[:, i, half:HD].unsqueeze(1).to_broadcast(shape), ALU.mult).then_inc(s_rope, 1)
                dve.drain()
                dve.tensor_tensor(qr[:, :, :], t1[:, :, :], t2[:, :, :], ALU.add)
                dve.drain()
                dve.tensor_tensor(t1[:, :, :], qr[:, :, :], qr[:, :, :], ALU.mult)
                dve.drain()
                dve.reduce_sum(ssq[:, :], t1[:, :, :], AX.X)
                dve.drain()
                dve.tensor_scalar(ms[:, :], ssq[:, :], 1.0 / HD, RMS_EPS, ALU.mult, ALU.add).then_inc(s_ms, 1)

            def split(b, i):
                t = b * TPB + i
                q_parts = qs[:, i % 2, :, :]
                dve.wait_ge(s_rr, t + 1)
                dve.tensor_tensor(t2[:, :, :], qr[:, :, :], rr[:, :].unsqueeze(2).to_broadcast([P, H + 1, HD]), ALU.mult)
                dve.drain()
                dve.wait_ge(s_st, (b * TPB + max(i - 1, 0)) * NG)
                dve.tensor_copy(q_parts[:, :, 0:HD].bitcast(f32r), t2[:, 0:H, :])
                dve.tensor_copy(q_parts[:, :, HD:2 * HD].bitcast(f32r), t2[:, 0:H, :])
                dve.tensor_tensor(t1[:, H, :], t2[:, H, :], wkq[:, :], ALU.mult)
                dve.drain()
                dve.wait_ge(s_pack, t)
                dve.tensor_copy(qh[:, :, :].bitcast(f32r), t2[:, 0:H, :])
                dve.tensor_copy(ks[:, 0:HD].bitcast(f32r), t1[:, H, :])
                dve.tensor_copy(ks[:, 2 * HD:3 * HD].bitcast(f32r), t1[:, H, :])
                dve.tensor_copy(kh4[:, :, :].bitcast(f32r), t1[:, H, :].unsqueeze(1).to_broadcast([P, GH, HD]))
                dve.tensor_tensor(q_parts[:, :, 2 * HD:3 * HD].bitcast(f32r), t2[:, 0:H, :], q_parts[:, :, 0:HD],
                                  ALU.subtract)
                dve.drain()
                dve.tensor_tensor(ks[:, HD:2 * HD].bitcast(f32r), t1[:, H, :], ks[:, 0:HD], ALU.subtract)\
                   .then_inc(s_parts, 1)

            def row_max(b, i):
                t = b * TPB + i
                q_parts = qs[:, i % 2, :, :]
                for h in range(H):
                    dve.wait_ge(s_mm, t * H + (h + 1))
                    dve.tensor_reduce(nmax[:, h:h + 1], pair(h % 2).rearrange("p a n -> p (a n)")[:, 0:(i + 1) * P],
                                      AX.X, ALU.max, negate=True).then_inc(s_max, 1)
                dve.drain()
                dve.tensor_copy(q_parts[:, :, 3 * HD].bitcast(f32r), nmax[:, :])
                dve.drain()
                dve.tensor_tensor(q_parts[:, :, 3 * HD + 1].bitcast(f32r), nmax[:, :], q_parts[:, :, 3 * HD],
                                  ALU.subtract).then_inc(s_nmax, 1)

            def divide(b, qc):
                kts = TPC * (qc + 1)
                c = b * QC + qc
                hold(dve, s_at, c * TPC)
                with dve.Fori(0, NG) as g:
                    dve.wait_ge(s_pv, b * PVS_B + qc * (NG * TPC) + g * kts + (kts + 2))
                    dve.reciprocal(scratch[:, :], ps[:, 5, :])
                    dve.drain()
                    row = oT[:, ds(g, 1), :].rearrange("p a n -> p (a n)")
                    dve.tensor_tensor(row, ps[:, 4, :], scratch[:, :], ALU.mult).then_inc(s_on, 1)
                    dve.drain()
                    dve.tensor_tensor(osq[:, ds(g, 1), :].rearrange("p a n -> p (a n)"), row, row, ALU.mult)\
                       .then_inc(s_sq, 1)

            def residual(b, qc):
                c = b * QC + qc
                dve.wait_ge(s_oss, c + 1)
                dve.tensor_scalar(oms[:, :], ps[:, 6, 0:TPC], 1.0 / D, RMS_EPS, ALU.mult, ALU.add).then_inc(s_oms, 1)
                dve.wait_ge(s_orstd, c + 1)
                for ii in range(TPC):
                    dve.wait_ge(s_at, c * TPC + (ii + 1))
                    dve.scalar_tensor_tensor(scratch[:, :], ps[:, 7 - 3 * (ii % 2), :], orstd[:, ii:ii + 1], rows(b, ga),
                                             ALU.mult, ALU.mult).then_inc(s_atd, 1)
                    dve.drain()
                    xt = xtile(c * TPC + ii)
                    dve.tensor_tensor(xt, xt, scratch[:, :], ALU.add)
                    dve.drain()
                chunk_stats(b, qc * TPC, mv2, ve2, s_var2)
                dve.wait_ge(s_rstd2, c + 1)
                for ii in range(TPC):
                    i = qc * TPC + ii
                    row = h2[:, i % 2, :]
                    dve.wait_ge(s_h2_out[i % 2], (b * (TPB // 2) + i // 2) * 16)
                    dve.wait_ge(s_h2t, b * TPB + max(i - 1, 0))
                    dve.tensor_scalar(row, xtile(c * TPC + ii), mv2[:, ii, 0:1], rstd2[:, ii:ii + 1],
                                      ALU.subtract, ALU.mult)
                    dve.drain()
                    dve.tensor_tensor(row, row, rows(b, cscale), ALU.mult)
                    dve.drain()
                    dve.tensor_tensor(row, row, rows(b, sbias), ALU.add).then_inc(s_h2, 1)

            def route(b, qc):
                c = b * QC + qc
                four = [P, TPC, E]
                grp = [P, TPC, GROUPS, GROUPS]
                dve.wait_ge(s_ex, c + 1)
                dve.tensor_scalar(biased[:, :, :], ex[:, :, :], 1.0, None, ALU.add)
                dve.drain()
                dve.reciprocal(score[:, :, :], biased[:, :, :])
                dve.drain()
                dve.tensor_tensor(biased[:, :, :], score[:, :, :], ebias[:, :].unsqueeze(1).to_broadcast(four), ALU.add)
                dve.drain()
                v = biased[:, :, :].rearrange("p t (g m) -> p (t g) m", m=GROUPS)
                dve.tensor_tensor(hi4[:, :, :], v[:, :, 0:4], v[:, :, 4:8], ALU.max)
                dve.tensor_tensor(lo4[:, :, :], v[:, :, 0:4], v[:, :, 4:8], ALU.min)
                dve.drain()
                dve.tensor_tensor(hi2[:, :, :], hi4[:, :, 0:2], hi4[:, :, 2:4], ALU.max)
                dve.tensor_tensor(mid2[:, :, :], hi4[:, :, 0:2], hi4[:, :, 2:4], ALU.min)
                dve.tensor_tensor(lo2[:, :, :], lo4[:, :, 0:2], lo4[:, :, 2:4], ALU.max)
                dve.drain()
                dve.tensor_tensor(lo2[:, :, :], lo2[:, :, :], mid2[:, :, :], ALU.max)
                dve.tensor_tensor(hi1[:, :], hi2[:, :, 0], hi2[:, :, 1], ALU.max)
                dve.tensor_tensor(mid1[:, :], hi2[:, :, 0], hi2[:, :, 1], ALU.min)
                dve.drain()
                dve.tensor_tensor(lo1[:, :], lo2[:, :, 0], lo2[:, :, 1], ALU.max)
                dve.drain()
                dve.tensor_tensor(lo1[:, :], lo1[:, :], mid1[:, :], ALU.max)
                dve.drain()
                gs = gsum[:, :, :]
                dve.tensor_tensor(gs.rearrange("p t g -> p (t g)"), hi1[:, :], lo1[:, :], ALU.add)
                dve.drain()
                other, own = gs.unsqueeze(2).to_broadcast(grp), gs.unsqueeze(3).to_broadcast(grp)
                dve.tensor_tensor(cmp_a[:, :, :, :], other, own, ALU.is_gt)
                dve.tensor_tensor(cmp_b[:, :, :, :], other, own, ALU.is_equal)
                dve.drain()
                dve.tensor_tensor(cmp_b[:, :, :, :], cmp_b[:, :, :, :], tri.unsqueeze(1).to_broadcast(grp), ALU.mult)
                dve.drain()
                dve.tensor_tensor(cmp_a[:, :, :, :], cmp_a[:, :, :, :], cmp_b[:, :, :, :], ALU.add)
                dve.drain()
                dve.reduce_sum(grank[:, :, :], cmp_a[:, :, :, :], AX.X)
                dve.drain()
                dve.tensor_scalar(grank[:, :, :], grank[:, :, :], float(TOPG), None, ALU.is_lt)
                dve.drain()
                dve.tensor_tensor(masked[:, :, :].rearrange("p t (g m) -> p t g m", m=GROUPS),
                                  biased[:, :, :].rearrange("p t (g m) -> p t g m", m=GROUPS),
                                  grank[:, :, :].unsqueeze(3).to_broadcast(grp), ALU.mult)
                dve.drain()
                for ii in range(TPC):
                    dve.max(top8[:, ii, :], masked[:, ii, :])
                dve.drain()
                for ii in range(TPC):
                    dve.match_replace(marked[:, ii, :], top8[:, ii, :], masked[:, ii, :], -3e38)
                dve.drain()
                dve.tensor_scalar(sel_b[:, :, :], marked[:, :, :], -3e38, None, ALU.is_equal).then_inc(s_sel, 1)
                dve.tensor_scalar(sel[:, :, :], marked[:, :, :], -3e38, None, ALU.is_equal)
                dve.drain()
                dve.tensor_tensor(wts[:, :, :], score[:, :, :], sel[:, :, :], ALU.mult)
                dve.reduce_sum(selsum[:, :], sel[:, :, :].rearrange("p t e -> p e t"), AX.X)
                dve.drain()
                dve.reduce_sum(wsum[:, :], wts[:, :, :], AX.X)
                dve.tensor_tensor(seen[:, :], seen[:, :], selsum[:, :], ALU.add)
                dve.drain()
                dve.tensor_scalar(wsum[:, :], wsum[:, :], 1e-20, None, ALU.add)
                dve.drain()
                dve.reciprocal(wrec[:, :], wsum[:, :])
                dve.drain()
                dve.tensor_tensor(wts[:, :, :], wts[:, :, :], wrec[:, :].unsqueeze(2).to_broadcast(four), ALU.mult)
                dve.wait_ge(s_pos, c + 1)
                pos = ps[:, 7, 0:TPC * E].rearrange("p (t e) -> p t e", e=E)
                dve.tensor_copy(seen_b[:, :], seen[:, :])
                dve.tensor_scalar(hv[:, :, :], pos, float(P), 1.0 - P * P, ALU.is_ge, ALU.mult)
                dve.scalar_tensor_tensor(valid[:, :, :], pos, float(CAP), sel[:, :, :], ALU.is_lt, ALU.mult)
                dve.drain()
                dve.scalar_tensor_tensor(key[:, :, :], pos, float(P), hv[:, :, :], ALU.mult, ALU.add)
                dve.drain()
                dve.tensor_tensor(key[:, :, :], key[:, :, :], erow.unsqueeze(1).to_broadcast(four), ALU.add)
                dve.drain()
                dve.tensor_tensor(key[:, :, :], key[:, :, :], valid[:, :, :], ALU.mult)
                dve.drain()
                for ii in range(TPC):
                    dve.max(key8[:, ii, :], key[:, ii, :])
                dve.drain()
                eight = [P, TOPK, E]
                for ii in range(TPC):
                    dve.tensor_tensor(eq8[:, :, :], key8[:, ii, :].unsqueeze(2).to_broadcast(eight),
                                      key[:, ii, :].unsqueeze(1).to_broadcast(eight), ALU.is_equal)
                    dve.drain()
                    dve.tensor_tensor(eq8[:, :, :], eq8[:, :, :], wts[:, ii, :].unsqueeze(1).to_broadcast(eight), ALU.mult)
                    dve.drain()
                    dve.reduce_sum(w8[:, ii, :], eq8[:, :, :], AX.X)
                    dve.drain()
                dve.wait_ge(s_slot, c * (16 * TPC * TOPK))
                dve.tensor_scalar(pay[:, :, :, 1].bitcast(f32), w8[:, :, :], ROUTED_SCALE, None, ALU.mult)
                dve.tensor_copy(pay[:, :, :, 0], tokid[:, ds(c * TPC, TPC)].unsqueeze(2).to_broadcast([P, TPC, TOPK]))
                dve.scalar_tensor_tensor(miss8[:, :, :], key8[:, :, :], 0.0, trash, ALU.is_equal, ALU.mult)
                dve.drain()
                dve.scalar_tensor_tensor(idx8[:, :, :], key8[:, :, :], -1.0, miss8[:, :, :], ALU.add, ALU.add)\
                   .then_inc(s_pay, 1)

            with dve.Fori(0, B) as b:
                for qc in range(QC):
                    i0 = qc * TPC
                    chunk_stats(b, i0, mv, ve, s_var)
                    normalise(b, i0)
                    rotate(b, i0)
                    for ii in range(TPC):
                        split(b, i0 + ii)
                        if ii + 1 < TPC:
                            normalise(b, i0 + ii + 1)
                            rotate(b, i0 + ii + 1)
                        row_max(b, i0 + ii)
                    divide(b, qc)
                    residual(b, qc)
                    route(b, qc)

            for p in range(2):
                dve.memset(hid_b[p][IB:IBP, :], 0.0)
                dve.memset(e_db[p][IB:IBP, :], 0.0)
            dve.memset(sh_db[IB:IBP, :], 0.0)
            dve.drain()
            dve.sem_inc(s_hid, 2)

            def x_out(n, p):
                dve.wait_ge(s_gu, n + 1)
                dve.wait_ge(s_T, n + 3)
                dve.tensor_copy(xgT[p][:, 2:4, :], ps[:, 1, :].rearrange("p (c t) -> p c t", t=CAP)).then_inc(s_xd, 1)

            def hidden(n, p):
                dve.wait_ge(s_dn, n + 1)
                dve.wait_ge(s_act, n + 1)
                dve.tensor_tensor(hid_a[p][:, :], gact_a[p][:, :], ps[0:IA, 2 + p, CAP:2 * CAP], ALU.mult)
                dve.tensor_tensor(hid_b[p][0:IB, :], gact_b[p][:, :], ps[IB:2 * IB, 4 + p, 0:CAP], ALU.mult)\
                   .then_inc(s_hid, 1)

            x_out(0, 0)
            with dve.Fori(0, NSH // 2) as i:
                for p in range(2):
                    n = i * 2 + p
                    hidden(n, p)
                    x_out(n + 1, 1 - p)
                    dve.wait_ge(s_dn, n + 3)
                    for h, done in enumerate((s_ya, s_yd)):
                        dve.tensor_tensor(y[p][:, h, :], ps[:, 6 + h, :], rows(i // (NSH // 2 // B), gb), ALU.mult)\
                           .then_inc(done, 1)
                    dve.drain()
                    for h in range(HALVES):
                        xt = xtile(n * HALVES + h)
                        dve.tensor_tensor(xt, xt, y[p][:, h, :], ALU.add)
                    dve.drain()

            def weighted(e, p):
                dve.wait_ge(s_yfree, e)
                dve.wait_ge(s_dn, e + NSH + 3)
                dve.tensor_scalar(y[p][:, 1, :], ps[:, 7, :], slots[:, ds(e * HALVES + 1, 1), 1].bitcast(f32), None,
                                  ALU.mult).then_inc(s_yd, 1)

            dve.wait_ge(s_slots_in, 16)
            with dve.Fori(0, E // 2 - 1) as i:
                for p in range(2):
                    hidden(i * 2 + (p + NSH), p)
                    x_out(i * 2 + (p + NSH + 1), 1 - p)
                    weighted(i * 2 + p, p)
            for p in range(2):
                e = E - 2 + p
                hidden(e + NSH, p)
                if p == 0:
                    x_out(e + NSH + 1, 1)
                weighted(e, p)

            for c in range(NT // TPC):
                dve.wait_ge(s_fin_in[c % 2], 16 * (c // 2 + 1))
                part = fin_acc[:, c % 2, :, :]
                dve.tensor_tensor(part, part, gb[:, c // QC, :].unsqueeze(1).to_broadcast([P, TPC, D]), ALU.mult)
                dve.drain()
                xc = xres[:, TPC * c:TPC * c + TPC, :]
                dve.tensor_tensor(xc, xc, part, ALU.add).then_inc(s_fin, 1)


def shape_constants(np):
    p = np.arange(P)
    con = np.zeros((P, NCONST), np.float32)
    con[:, C_ID:C_ID + P] = np.eye(P)
    con[:, C_BIAS:C_BIAS + P] = np.where(p[None, :] <= p[:, None], 0.0, -1e30)
    con[:, C_UP:C_UP + P] = p[:, None] < p[None, :]
    inv = np.float32(1.0) / np.float32(10000.0) ** (np.arange(0, HD, 2, dtype=np.float32) / np.float32(HD))
    ang = np.arange(S, dtype=np.float32)[:, None] * inv[None, :]
    c, s = np.cos(ang), np.sin(ang)
    tile = lambda a: a.reshape(TPB, P, HD).transpose(1, 0, 2).reshape(P, TPB * HD)
    con[:, C_COS:C_SIN] = tile(np.concatenate([c, c], 1))
    con[:, C_SIN:C_EROW] = tile(np.concatenate([-s, s], 1))
    con[:, C_EROW:C_TRI] = 2 * np.arange(E) + 1
    g = np.arange(GROUPS)
    con[:, C_TRI:C_TRASH] = (g[None, :] < g[:, None]).reshape(1, -1)
    con[:, C_TRASH:NCONST] = NSLOT + 1 + np.arange(TPC * TOPK)[None, :] * P + p[:, None]
    tokid = (np.arange(NT)[None, :] * P + p[:, None]).astype(np.int32)
    slot = np.zeros((P, E * HALVES, 2), np.int32)
    slot[:, :, 0] = NTOK + (np.arange(E * HALVES) % HALVES)[None, :] * P + p[:, None]
    return con, tokid, slot.reshape(P, -1)


def kernel(**inputs):
    import numpy as np
    import concourse.bacc as bacc
    from concourse.bass_utils import run_bass_kernel_spmd

    a = {k: np.asarray(v) for k, v in inputs.items()}
    chunks = lambda w: np.ascontiguousarray(w.reshape(KC, P, -1).transpose(1, 0, 2))
    con, tokid, slot = shape_constants(np)
    join = lambda g, u: np.concatenate([g, u[..., IA:], u[..., :IA]], axis=-1)
    gate_up = join(a["L0_ffn_w_gate"], a["L0_ffn_w_up"])
    arrays = {
        "x": np.ascontiguousarray(a["L0_attn_x"].reshape(NTOK, D)),
        "c_t": chunks(np.ascontiguousarray(a["L0_c"].T)),
        "wmod": np.ascontiguousarray(a["L0_wmod"]),
        "wq_t": chunks(np.ascontiguousarray(a["L0_attn_Wq"].T)),
        "wkv_t": chunks(np.concatenate([a["L0_attn_Wk"].T, a["L0_attn_Wv"].T], axis=1)),
        "wo_t": chunks(np.ascontiguousarray(a["L0_attn_Wo"].T)),
        "w_pre": np.ascontiguousarray(a["L0_attn_w_pre"].reshape(KC, P).T),
        "w_qn": np.ascontiguousarray(a["L0_attn_w_qn"]),
        "w_kn": np.ascontiguousarray(a["L0_attn_w_kn"]),
        "router_t": chunks(np.ascontiguousarray(a["L0_ffn_router_weight"].T)),
        "e_bias": np.ascontiguousarray(a["L0_ffn_e_bias"]),
        "gate_up": np.ascontiguousarray(gate_up.reshape(E, KC, P, 2 * EI).transpose(0, 2, 1, 3)),
        "w_down": np.ascontiguousarray(a["L0_ffn_w_down"]),
        "sh_gate_up": chunks(join(a["L0_ffn_sh_gate"], a["L0_ffn_sh_up"])),
        "sh_down": np.ascontiguousarray(a["L0_ffn_sh_down"]),
        "consts": con,
        "tokids": tokid,
        "slot_init": slot,
    }
    nc = bacc.Bacc("TRN2", target_bir_lowering=False, num_devices=1)
    args = [nc.dram_tensor(f"in_{n}", v.shape, mybir.dt.from_np(v.dtype), kind="ExternalInput").ap()
            for n, v in arrays.items()]
    out = nc.dram_tensor("out", (NTOK, D), mybir.dt.float32, kind="ExternalOutput").ap()
    build_program(nc, *args, out)
    r = run_bass_kernel_spmd(nc, [{f"in_{n}": v for n, v in arrays.items()}], core_ids=[0])
    return r.results[0]["out"].reshape(B, S, D)
```

```python
import concourse.bass as bass
from concourse import mybir
from contextlib import ExitStack

B, S, D = 2, 1024, 512
H, HD = 16, 32
P = 128
NTOK = B * S
TPB = S // P
NT = NTOK // P
CH = 512
TPC = CH // P
QC = S // CH
KC = D // P
GH = 4
NG = H // GH
E, EI, TOPK, GROUPS, TOPG = 64, 176, 8, 8, 4
CAP = 2 * 1024 * TOPK // E
HALVES = CAP // P
NSLOT = E * CAP
ROUTED_SCALE = 2.5
LN_EPS, RMS_EPS = 1e-5, 1e-6
EXTRA = CAP
IA = 112
IB = EI - IA
IBP = 96
NSH = NTOK // CAP
UNITS_B = sum(NG * 2 * TPC * (qc + 1) for qc in range(QC))
PVS_B = UNITS_B // 2

C_ID = 0
C_COS = P
C_SIN = C_COS + TPB * HD
C_EROW = C_SIN + TPB * HD
C_TRI = C_EROW + E
C_TRASH = C_TRI + GROUPS * GROUPS
NCONST = C_TRASH + TPB * TOPK


def build_program(nc, x, c_t, wmod, wq_t, wkv_t, wo_t, w_pre, w_qn, w_kn, router_t, e_bias,
                  gate_up, w_down, sh_gate_up, sh_down, consts, masks, tokids, slot_init, out):
    f32, f32r, bf16, i32 = mybir.dt.float32, mybir.dt.float32r, mybir.dt.bfloat16, mybir.dt.int32
    ALU, ACT, AX = mybir.AluOpType, mybir.ActivationFunctionType, mybir.AxisListType
    ds = bass.ds

    h2_dram = nc.dram_tensor("h2_dram", [NTOK + EXTRA, D], f32).ap()
    acc_dram = nc.dram_tensor("acc_dram", [NTOK + EXTRA, D], f32).ap()
    slot_dram = nc.dram_tensor("slot_dram", [NSLOT + TPB * TOPK * P, 2], i32).ap()

    ctx = ExitStack()
    with ctx:
        def sem(name):
            return ctx.enter_context(nc.semaphore(name))

        def sb(where, name, shape, dt=f32):
            return where.enter_context(nc.sbuf_tensor(name, shape, dt))

        xres = sb(ctx, "xres", [P, NT, D])
        con = sb(ctx, "con", [P, NCONST])
        ga = sb(ctx, "ga", [P, B, D])
        sbias = sb(ctx, "sbias", [P, B, D])
        cscale = sb(ctx, "cscale", [P, B, D])
        gb = sb(ctx, "gb", [P, B, D])
        mcol = sb(ctx, "mcol", [P, 2, KC, B])
        ident_b = sb(ctx, "ident_b", [P, P], bf16)
        bias_b = sb(ctx, "bias_b", [P, P], bf16)
        upper_b = sb(ctx, "upper_b", [P, P], bf16)
        ones_b = sb(ctx, "ones_b", [P, P], bf16)
        ones = sb(ctx, "ones", [P, HD])
        mhalf = sb(ctx, "mhalf", [P, NT + 1])
        tokid = sb(ctx, "tokid", [P, NT], i32)
        ebias = sb(ctx, "ebias", [P, E])
        wkq = sb(ctx, "wkq", [P, HD])
        rw = sb(ctx, "rw", [P, KC, E])
        wo = sb(ctx, "wo", [P, KC, D])

        mv = sb(ctx, "mv", [P, NT, 2])
        ve = sb(ctx, "ve", [P, NT])
        rstd = sb(ctx, "rstd", [P, NT])

        att = ExitStack()
        kpad = sb(att, "kpad", [P, GH, S], f32r)
        qs = sb(att, "qs", [P, 2, H, P])
        wq = sb(att, "wq", [P, KC, D])
        wkv = sb(att, "wkv", [P, KC, 2 * HD])
        ks = sb(att, "ks", [P, P])
        kh4 = sb(att, "kh4", [P, GH, HD])
        qh = sb(att, "qh", [P, H, HD])
        qpT = sb(att, "qpT", [P, NG, P], f32r)
        qk = sb(att, "qk", [P, H + 1, HD])
        t1 = sb(att, "t1", [P, H + 1, HD])
        t2 = sb(att, "t2", [P, H + 1, HD])
        qr = sb(att, "qr", [P, H + 1, HD])
        xn = sb(att, "xn", [P, 2, D])
        hT = sb(att, "hT", [P, 2, KC, P])
        pre = ExitStack()
        wmod_s = sb(pre, "wmod_s", [P, KC, 6 * D])
        ct_s = sb(pre, "ct_s", [P, KC, B])
        csb = sb(pre, "csb", [P, KC, B, P])
        gate_t = sb(pre, "gate_t", [P, D])
        gate_a = sb(pre, "gate_a", [P, D])
        mask_s = sb(pre, "mask_s", [P, 2 * P])
        wqn_s = sb(pre, "wqn_s", [P, HD])
        wkn_s = sb(pre, "wkn_s", [P, HD])
        wpre = sb(pre, "wpre", [P, KC])
        silu_c = sb(pre, "silu_c", [P, KC, B])
        st = sb(pre, "st", [P, NT, 6])
        pre.close()
        rout = ExitStack()
        RG = TPB * GROUPS
        ex = sb(rout, "ex", [P, TPB, E])
        score = sb(rout, "score", [P, TPB, E])
        biased = sb(rout, "biased", [P, TPB, E])
        hi4 = sb(rout, "hi4", [P, RG, 4])
        lo4 = sb(rout, "lo4", [P, RG, 4])
        hi2 = sb(rout, "hi2", [P, RG, 2])
        lo2 = sb(rout, "lo2", [P, RG, 2])
        mid2 = sb(rout, "mid2", [P, RG, 2])
        hi1 = sb(rout, "hi1", [P, RG])
        lo1 = sb(rout, "lo1", [P, RG])
        mid1 = sb(rout, "mid1", [P, RG])
        gsum = sb(rout, "gsum", [P, TPB, GROUPS])
        cmp_a = sb(rout, "cmp_a", [P, TPB, GROUPS, GROUPS])
        cmp_b = sb(rout, "cmp_b", [P, TPB, GROUPS, GROUPS])
        grank = sb(rout, "grank", [P, TPB, GROUPS])
        masked = sb(rout, "masked", [P, TPB, E])
        top8 = sb(rout, "top8", [P, TPB, TOPK])
        marked = sb(rout, "marked", [P, TPB, E])
        sel = sb(rout, "sel", [P, TPB, E])
        sel_b = sb(rout, "sel_b", [P, TPB, E], bf16)
        selsum = sb(rout, "selsum", [P, E])
        wts = sb(rout, "wts", [P, TPB, E])
        wsum = sb(rout, "wsum", [P, TPB])
        wrec = sb(rout, "wrec", [P, TPB])
        hv = sb(rout, "hv", [P, TPB, E])
        valid = sb(rout, "valid", [P, TPB, E])
        key = sb(rout, "key", [P, TPB, E])
        key8 = sb(rout, "key8", [P, TPB, TOPK])
        eq8 = sb(rout, "eq8", [P, TOPK, E])
        w8 = sb(rout, "w8", [P, TPB, TOPK])
        miss8 = sb(rout, "miss8", [P, TPB, TOPK])
        rout.close()
        qT = sb(att, "qT", [P, H, CH], f32r)
        probs = sb(att, "probs", [P, 2, GH, CH])
        h2 = sb(att, "h2", [P, 2, D])
        h2T = sb(att, "h2T", [P, 2, KC, P])
        kT = sb(att, "kT", [P, S], f32r)
        v_sb = sb(att, "v_sb", [P, TPB, HD])
        oT = sb(att, "oT", [P, QC, NG, CH])
        osq = sb(att, "osq", [P, CH])
        scratch = sb(att, "scratch", [P, CH])
        st2 = sb(att, "st2", [P, 2, 6])
        mv2 = sb(att, "mv2", [P, 2, 2])
        ve2 = sb(att, "ve2", [P, 2])
        rstd2 = sb(att, "rstd2", [P, 2])
        oms = sb(att, "oms", [P, TPC])
        orstd = sb(att, "orstd", [P, QC, TPC])
        ssq = sb(att, "ssq", [P, H + 1])
        ms = sb(att, "ms", [P, H + 1])
        rr = sb(att, "rr", [P, H + 1])
        nmax = sb(att, "nmax", [P, H])
        seen = sb(att, "seen", [P, E])
        seen_b = sb(att, "seen_b", [P, E], bf16)
        idx8 = sb(att, "idx8", [P, TPB, TOPK], i32)
        pay = sb(att, "pay", [P, TPB, TOPK, 2], i32)
        att.close()

        moe = ExitStack()
        sh_gu = sb(moe, "sh_gu", [P, KC, 2 * EI])
        sh_da = sb(moe, "sh_da", [IA, D])
        sh_db = sb(moe, "sh_db", [IBP, D])
        xg = [sb(moe, f"xg{p}", [P, HALVES, D]) for p in range(2)]
        xgT = [sb(moe, f"xgT{p}", [P, KC, CAP]) for p in range(2)]
        gact_a = [sb(moe, f"gact_a{p}", [IA, CAP]) for p in range(2)]
        gact_b = [sb(moe, f"gact_b{p}", [IB, CAP]) for p in range(2)]
        hid_a = [sb(moe, f"hid_a{p}", [IA, CAP]) for p in range(2)]
        hid_b = [sb(moe, f"hid_b{p}", [IBP, CAP]) for p in range(2)]
        y = [sb(moe, f"y{p}", [P, HALVES, D]) for p in range(2)]
        e_gu = [sb(moe, f"e_gu{p}", [P, KC, 2 * EI]) for p in range(2)]
        e_da = [sb(moe, f"e_da{p}", [IA, D]) for p in range(2)]
        e_db = [sb(moe, f"e_db{p}", [IBP, D]) for p in range(2)]
        slots = sb(moe, "slots", [P, E * HALVES, 2], i32)
        from_ix = [sb(moe, f"from_ix{q}", [P, HALVES], i32) for q in range(4)]
        to_ix = [sb(moe, f"to_ix{q}", [P, HALVES], i32) for q in range(4)]
        moe.close()
        fin = ExitStack()
        fin_acc = sb(fin, "fin_acc", [P, 2, TPC, D])
        fin.close()

        ps = ctx.enter_context(nc.psum_tensor("ps", [P, 8, 512], f32))

        def pair(n):
            return ps[:, 2 * n:2 * n + 2, :]

        o_tile = qh[:, :, :].rearrange("p (g j) d -> p g (j d)", j=GH)
        ident = con[:, C_ID:C_ID + P]
        cos = con[:, C_COS:C_SIN].rearrange("p (t d) -> p t d", d=HD)
        sin = con[:, C_SIN:C_EROW].rearrange("p (t d) -> p t d", d=HD)
        erow = con[:, C_EROW:C_TRI]
        tri = con[:, C_TRI:C_TRASH].rearrange("p (a b) -> p a b", b=GROUPS)
        trash = con[:, C_TRASH:NCONST].rearrange("p (t j) -> p t j", j=TOPK)

        s_mod_in = sem("s_mod_in")
        s_small = sem("s_small")
        s_x = sem("s_x")
        s_init = sem("s_init")
        s_h2_out = [sem(f"s_h2_out{p}") for p in range(2)]
        s_slot = sem("s_slot")
        s_slots_in = sem("s_slots_in")
        s_sh_w = sem("s_sh_w")
        s_wu = [sem(f"s_wu{p}") for p in range(2)]
        s_wd = [sem(f"s_wd{p}") for p in range(2)]
        s_xg = [sem(f"s_xg{p}") for p in range(2)]
        s_eg = [sem(f"s_eg{p}") for p in range(2)]
        s_added = sem("s_added")
        s_fin_in = [sem(f"s_fin_in{p}") for p in range(2)]
        s_out = sem("s_out")
        s_silu, s_csb, s_mod, s_modv, s_ready = (sem(n) for n in ("s_silu", "s_csb", "s_mod", "s_modv", "s_ready"))
        s_zero = sem("s_zero")
        (s_var, s_rstd, s_xn, s_xT, s_hT, s_q, s_qk, s_rope, s_ms, s_rr, s_parts, s_pack, s_packT, s_mm,
         s_max, s_nmax, s_st, s_qT) = (sem("s_" + n) for n in (
             "var", "rstd", "xn", "xT", "hT", "q", "qk", "rope", "ms", "rr", "parts", "pack", "packT", "mm",
             "max", "nmax", "st", "qT"))
        s_sc, s_exp, s_mask, s_pv, s_on, s_sq = (sem("s_" + n) for n in ("sc", "exp", "mask", "pv", "on", "sq"))
        (s_oss, s_oms, s_orstd, s_at, s_atd, s_var2, s_rstd2, s_h2, s_h2t, s_h2T, s_lg, s_ex, s_sel, s_pos,
         s_pay) = (sem("s_" + n) for n in (
             "oss", "oms", "orstd", "at", "atd", "var2", "rstd2", "h2", "h2t", "h2T", "lg", "ex", "sel", "pos",
             "pay"))
        s_T, s_xa, s_xd, s_gu, s_act, s_hid, s_dn, s_ya, s_yd = (sem("s_e" + n) for n in (
            "T", "xa", "xd", "gu", "act", "hid", "dn", "ya", "yd"))
        s_from, s_to, s_fin = sem("s_from"), sem("s_to"), sem("s_fin")
        s_ot = sem("s_ot")
        s_yfree = sem("s_yfree")
        s_step = sem("s_step")

        def hold(eng, semaphore, value):
            eng.wait_ge(semaphore, value)
            eng.sem_inc(s_step, 1)

        def xtile(t):
            return xres[:, ds(t, 1), :].rearrange("p a n -> p (a n)")

        def rows(b, tile):
            return tile[:, ds(b, 1), :].rearrange("p a n -> p (a n)")

        AT_PROJECT, AT_TURN, AT_LOGITS = 1, 5, 7
        STORED = (TPC + TPC // 2, TPC // 2)
        SLOTTED = 16 * TPB * TOPK

        block = ctx.enter_context(nc.Block())

        @block.sync
        def _(sp):
            sp.dma_start(ct_s[:, :, :], c_t).then_inc(s_mod_in, 16)
            sp.dma_start(wmod_s[:, :, :], wmod.rearrange("(c p) n -> p c n", p=P)).then_inc(s_mod_in, 16)
            xv = x.rearrange("(t p) n -> p t n", p=P)
            for c in range(4):
                sp.dma_start(xres[:, 4 * c:4 * c + 4, :], xv[:, 4 * c:4 * c + 4, :]).then_inc(s_x, 16)
            sp.wait_ge(s_zero, 1)
            zb = qs[:, 0, 0:D // P, :].rearrange("p h n -> p (h n)").unsqueeze(1)
            sp.dma_start(h2_dram[NTOK:NTOK + EXTRA, :].rearrange("(t p) n -> p t n", p=P),
                         zb.to_broadcast([P, EXTRA // P, D])).then_inc(s_init, 16)
            sp.dma_start(acc_dram.rearrange("(t p) n -> p t n", p=P),
                         zb.to_broadcast([P, (NTOK + EXTRA) // P, D])).then_inc(s_init, 16)
            sp.dma_start(slot_dram[0:NSLOT, :].rearrange("(p s) c -> p (s c)", p=P), slot_init).then_inc(s_init, 16)
            with sp.Fori(0, B) as b:
                with sp.Fori(0, TPC) as ii:
                    t = b * TPB + ii
                    sp.wait_ge(s_h2, t + 1)
                    sp.dma_start(h2_dram[ds(t * P, P), :], h2[:, 0, :]).then_inc(s_h2_out[0], 16)
                for ii in range(TPC):
                    t = b * TPB + (TPC + ii)
                    sp.wait_ge(s_h2, t + 1)
                    sp.dma_start(h2_dram[ds(t * P, P), :], h2[:, ii % 2, :]).then_inc(s_h2_out[ii % 2], 16)
            sp.wait_ge(s_lg, NT)
            sp.dma_start(sh_gu[:, :, :], sh_gate_up).then_inc(s_sh_w, 16)
            sp.dma_start(sh_da[:, :], sh_down[0:IA, :]).then_inc(s_sh_w, 16)
            sp.dma_start(sh_db[0:IB, :], sh_down[IA:EI, :]).then_inc(s_sh_w, 16)

            def load_up(e, p):
                sp.dma_start(e_gu[p][:, :, :], gate_up[ds(e, 1), :, :, :].rearrange("a p c n -> p (a c) n"))\
                  .then_inc(s_wu[p], 16)

            def load_down(e, p):
                sp.dma_start(e_da[p][:, :], w_down[ds(e, 1), 0:IA, :].rearrange("a i n -> (a i) n"))\
                  .then_inc(s_wd[p], 16)
                sp.dma_start(e_db[p][0:IB, :], w_down[ds(e, 1), IA:EI, :].rearrange("a i n -> (a i) n"))\
                  .then_inc(s_wd[p], 16)

            for p in range(2):
                sp.wait_ge(s_h2_out[p], 16 * B * STORED[p])
            with sp.Fori(0, NSH // 2) as i:
                for p in range(2):
                    n = i * 2 + p
                    sp.wait_ge(s_T, n + 1)
                    for h in range(HALVES):
                        sp.dma_start(xg[p][:, h, :], h2_dram[ds(n * CAP + h * P, P), :]).then_inc(s_xg[p], 16)
            for p in range(2):
                load_up(p, p)
                load_down(p, p)
            with sp.Fori(0, E // 2 - 1) as i:
                for p in range(2):
                    e = i * 2 + p
                    sp.wait_ge(s_gu, e + NSH + 3)
                    load_up(e + 2, p)
                    sp.wait_ge(s_dn, e + NSH + 3)
                    load_down(e + 2, p)
            sp.wait_ge(s_added, 16 * HALVES * E)
            av = acc_dram[0:NTOK, :].rearrange("(t p) n -> p t n", p=P)
            ov = out.rearrange("(t p) n -> p t n", p=P)
            for c in range(2):
                sp.dma_start(fin_acc[:, c, :, :], av[:, TPC * c:TPC * c + TPC, :]).then_inc(s_fin_in[c], 16)
            for c in range(NT // TPC):
                sp.wait_ge(s_fin, c + 1)
                sp.dma_start(ov[:, TPC * c:TPC * c + TPC, :], xres[:, TPC * c:TPC * c + TPC, :]).then_inc(s_out, 16)
                if c + 2 < NT // TPC:
                    sp.dma_start(fin_acc[:, c % 2, :, :], av[:, TPC * (c + 2):TPC * (c + 3), :])\
                      .then_inc(s_fin_in[c % 2], 16)
            sp.wait_ge(s_out, 16 * (NT // TPC))

        @block.gpsimd
        def _(pool):
            def inv_sqrt(dst, src, n):
                return pool.tensor_tensor(dst, src, mhalf[:, 0:n], ALU.pow)

            def fill_slots(ii):
                for j in range(TOPK):
                    pool.indirect_dma_start(
                        out=slot_dram, out_offset=bass.IndirectOffsetOnAxis(ap=idx8[:, ii, j:j + 1], axis=0),
                        in_=pay[:, ii, j, :], in_offset=None).then_inc(s_slot, 16)

            pool.wait_ge(s_ready, 1)
            pool.wait_ge(s_var, 1)
            inv_sqrt(rstd[:, :], ve[:, :], NT).then_inc(s_rstd, 1)
            pool.wait_ge(s_init, 48)
            def head_rms(b, i):
                hold(pool, s_ms, b * TPB + (i + 1))
                inv_sqrt(rr[:, :], ms[:, :], H + 1).then_inc(s_rr, 1)

            def tile_rstd(t, slot):
                hold(pool, s_var2, t + 1)
                inv_sqrt(rstd2[:, slot:slot + 1], ve2[:, slot:slot + 1], 1).then_inc(s_rstd2, 1)

            def causal(b, qc):
                kts = TPC * (qc + 1)
                if qc == 1:
                    hold(pool, s_pack, (b + 1) * TPB)
                with pool.Fori(0, NG) as g:
                    if qc == 1:
                        hold(pool, s_at, b * TPB + g)
                        pool.tensor_copy(o_tile[:, :, :], oT[:, 0, :, ds(g * P, P)]).then_inc(s_ot, 1)
                        tile_rstd(b * TPB + g, 0)
                    for dd in range(TPC):
                        kt = TPC * qc + dd
                        unit = b * UNITS_B + qc * (NG * 2 * TPC) + g * (2 * kts) + 2 * kt
                        hold(pool, s_exp, unit + 4)
                        tile = probs[:, kt % 2, :, dd * P:dd * P + P]
                        pool.affine_select(out=tile, in_=tile, compare_op=ALU.is_ge, fill=0.0, base=0,
                                           pattern=[[0, GH], [1, P]], channel_multiplier=-1).then_inc(s_mask, 1)

            def row_rms(b, qc):
                hold(pool, s_oms, b * QC + (qc + 1))
                inv_sqrt(orstd[:, qc, :], oms[:, :], TPC).then_inc(s_orstd, 1)

            with pool.Fori(0, B) as b:
                for i in range(TPC):
                    head_rms(b, i)
                    if i == 0:
                        hold(pool, s_pay, b + 1)
                    fill_slots(i)
                head_rms(b, TPC)
                causal(b, 0)
                row_rms(b, 0)
                fill_slots(TPC)
                for i in range(TPC + 1, TPB):
                    head_rms(b, i)
                    fill_slots(i)
                causal(b, 1)
                row_rms(b, 1)
                for ii in range(TPC):
                    tile_rstd(b * TPB + (TPC + ii), ii % 2)
            pool.wait_ge(s_pay, B + 1)
            for i in range(TPB):
                fill_slots(i)
            pool.wait_ge(s_slot, SLOTTED * (B + 1))
            pool.dma_start(slots[:, :, :], slot_dram[0:NSLOT, :].rearrange("(p s) c -> p s c", p=P))\
                .then_inc(s_slots_in, 16)
            pool.wait_ge(s_slots_in, 16)

            def gather(e, q):
                n = e + NSH
                hold(pool, s_T, n + 1)
                pool.tensor_copy(from_ix[q][:, :], slots[:, ds(e * HALVES, HALVES), 0]).then_inc(s_from, 1)
                hold(pool, s_from, e + 1)
                for h in range(HALVES):
                    pool.indirect_dma_start(
                        out=xg[q % 2][:, h, :], out_offset=None, in_=h2_dram,
                        in_offset=bass.IndirectOffsetOnAxis(ap=from_ix[q][:, h:h + 1], axis=0)).then_inc(s_eg[q % 2], 16)

            def add_rows(e, q):
                pool.tensor_copy(to_ix[q][:, :], slots[:, ds(e * HALVES, HALVES), 0]).then_inc(s_to, 1)
                hold(pool, s_to, e + 1)
                hold(pool, s_ya, e + NSH + 1)
                hold(pool, s_yd, e + NSH + 1)
                pool.wait_ge(s_added, e * (16 * HALVES))
                pool.sem_inc(s_yfree, 1)
                for h in range(HALVES):
                    pool.indirect_dma_start(
                        out=acc_dram, out_offset=bass.IndirectOffsetOnAxis(ap=to_ix[q][:, h:h + 1], axis=0),
                        in_=y[q % 2][:, h, :], in_offset=None, compute_op=ALU.add).then_inc(s_added, 16)

            gather(0, 0)
            gather(1, 1)
            gather(2, 2)
            with pool.Fori(0, E // 4 - 1) as i:
                for q in range(4):
                    gather(i * 4 + (q + 3), (q + 3) % 4)
                    add_rows(i * 4 + q, q)
            for q in range(4):
                e = E - 4 + q
                if q < 1:
                    gather(e + 3, q + 3)
                add_rows(e, q)

        @block.scalar
        def _(act):
            act.dma_start(con[:, :], consts).then_inc(s_small, 16)
            act.dma_start(mask_s[:, :], masks).then_inc(s_small, 16)
            act.dma_start(wq[:, :, :], wq_t).then_inc(s_small, 16)
            act.dma_start(wkv[:, :, :], wkv_t).then_inc(s_small, 16)
            act.dma_start(wo[:, :, :], wo_t).then_inc(s_small, 16)
            act.dma_start(rw[:, :, :], router_t).then_inc(s_small, 16)
            act.dma_start(wpre[:, :], w_pre).then_inc(s_small, 16)
            act.dma_start(tokid[:, :], tokids).then_inc(s_small, 16)
            act.dma_start(ebias[:, :], e_bias.unsqueeze(0).to_broadcast([P, E])).then_inc(s_small, 16)
            act.dma_start(wqn_s[:, :], w_qn.unsqueeze(0).to_broadcast([P, HD])).then_inc(s_small, 16)
            act.dma_start(wkn_s[:, :], w_kn.unsqueeze(0).to_broadcast([P, HD])).then_inc(s_small, 16)
            act.wait_ge(s_mod_in, 32)
            act.activation(silu_c[:, :, :], ct_s[:, :, :], ACT.Silu).then_inc(s_silu, 1)

            def modulate(b, i):
                t = b * TPB + i
                hold(act, s_xT, t + 1)
                hold(act, s_q, b * TPB + max(i - 1, 0))
                for cc in range(KC):
                    last = act.activation(hT[:, i % 2, cc, :], ps[:, 6, cc * P:(cc + 1) * P], ACT.Identity,
                                          bias=mcol[:, 0, cc, ds(b, 1)], scale=mcol[:, 1, cc, ds(b, 1)])
                last.then_inc(s_hT, 1)

            def project(b, i):
                t = b * TPB + i
                hold(act, s_rope, t)
                hold(act, s_on, b * (QC * NG))
                act.wait_ge(s_q, t + 1)
                act.activation(qk[:, 0:H, :], ps[:, 4, :].rearrange("p (h d) -> p h d", d=HD), ACT.Copy)
                act.activation(qk[:, H, :], ps[:, 7, 0:HD], ACT.Copy)
                act.activation(v_sb[:, i, :], ps[:, 7, HD:2 * HD], ACT.Copy).then_inc(s_qk, 1)

            def pack(b, i):
                t = b * TPB + i
                act.wait_ge(s_pack, t + 1)
                act.activation(qpT[:, :, :], ps[:, 5, :].rearrange("p (g t) -> p g t", t=P), ACT.Copy)
                act.activation(kT[:, i * P:i * P + P], ps[:, 7, 0:P], ACT.Copy)
                for j in range(GH):
                    r = slice(HD * j, HD * j + HD)
                    last = act.activation(kpad[r, j, i * P:i * P + P], ps[r, 7, P:2 * P], ACT.Copy)
                last.then_inc(s_packT, 1)

            def stack(b, i):
                ii = i % TPC
                for q4 in range(NG):
                    act.wait_ge(s_st, (b * TPB + i) * NG + q4 + 1)
                    act.activation(qT[:, GH * q4:GH * q4 + GH, ii * P:ii * P + P],
                                   ps[:, 5 + 2 * (q4 % 2), :].rearrange("p (g t) -> p g t", t=P), ACT.Copy)\
                       .then_inc(s_qT, 1)

            act.wait_ge(s_modv, 1)
            act.sem_inc(s_exp, 2)
            def exponentials(b, qc):
                kts = TPC * (qc + 1)
                with act.Fori(0, NG) as g:
                    for kt in range(kts):
                        off = max(0, kt - TPC * qc) * P
                        pv = b * PVS_B + qc * (NG * TPC) + g * kts + kt
                        hold(act, s_pv, pv + 1)
                        for pr in range(2):
                            unit = b * UNITS_B + qc * (NG * 2 * TPC) + g * (2 * kts) + (2 * kt + pr)
                            act.wait_ge(s_sc, unit + 1)
                            act.activation(probs[:, kt % 2, 2 * pr:2 * pr + 2, off:CH],
                                           pair(pr)[:, :, off:CH], ACT.Exp).then_inc(s_exp, 1)
                        if qc == 1 and kt == AT_TURN + 1:
                            rows_T(b * TPB + g, 6, 0, b * TPB + g)

            def rows_T(t, bank, slot, routed):
                hold(act, s_lg, routed)
                act.wait_ge(s_h2t, t + 1)
                act.activation(h2T[:, slot, :, :], ps[:, bank, :].rearrange("p (c t) -> p c t", t=P), ACT.Copy)\
                   .then_inc(s_h2T, 1)

            with act.Fori(0, B) as b:
                modulate(b, 0)
                modulate(b, 1)
                project(b, 0)
                for i in range(TPB):
                    if i == TPC:
                        exponentials(b, 0)
                    pack(b, i)
                    if i + 1 < TPB:
                        project(b, i + 1)
                    if i + 2 < TPB:
                        modulate(b, i + 2)
                    stack(b, i)
                exponentials(b, 1)
                for ii in range(TPC):
                    rows_T(b * TPB + (TPC + ii), ii % 2, ii % 2, b * TPB + (TPC + max(ii - 1, 0)))
                hold(act, s_lg, (b + 1) * TPB)
                act.activation(ex[:, :, :], ps[:, 7, :].rearrange("p (t e) -> p t e", e=E), ACT.Exp,
                               scale=-1.0).then_inc(s_ex, 1)

            def x_out(n, p):
                hold(act, s_gu, n + 1)
                act.wait_ge(s_T, n + 3)
                act.activation(xgT[p][:, 0:2, :], ps[:, 0, :].rearrange("p (c t) -> p c t", t=CAP), ACT.Copy)\
                   .then_inc(s_xa, 1)

            def gates(n, p):
                hold(act, s_hid, n + 1)
                act.wait_ge(s_gu, n + 3)
                act.activation(gact_a[p][:, :], ps[0:IA, 2 + p, 0:CAP], ACT.Silu)
                act.activation(gact_b[p][:, :], ps[0:IB, 4 + p, 0:CAP], ACT.Silu).then_inc(s_act, 1)

            x_out(0, 0)
            gates(0, 0)
            x_out(1, 1)
            with act.Fori(0, NSH // 2) as i:
                for p in range(2):
                    n = i * 2 + p
                    gates(n + 1, 1 - p)
                    x_out(n + 2, p)

            def weighted(e, p):
                hold(act, s_yfree, e)
                act.wait_ge(s_slots_in, 16)
                hold(act, s_dn, e + NSH + 3)
                act.activation(y[p][:, 0, :], ps[:, 6, :], ACT.Copy,
                               scale=slots[:, ds(e * HALVES, 1), 1].bitcast(f32)).then_inc(s_ya, 1)

            with act.Fori(0, E // 2 - 1) as i:
                for p in range(2):
                    gates(i * 2 + (p + NSH + 1), 1 - p)
                    x_out(i * 2 + (p + NSH + 2), p)
                    weighted(i * 2 + p, p)
            gates(E + NSH - 1, 1)
            for p in range(2):
                weighted(E - 2 + p, p)

        @block.tensor
        def _(pe):
            pe.wait_ge(s_silu, 1)
            for m in range(2):
                for cc in range(KC):
                    for k in range(KC):
                        col = (m * KC + cc) * B
                        last = pe.matmul(ps[:, 0, col:col + B], wmod_s[:, k, m * D + cc * P:m * D + (cc + 1) * P],
                                         silu_c[:, k, :], start=(k == 0), stop=(k == KC - 1))
            last.then_inc(s_mod, 1)
            pe.wait_ge(s_csb, 1)
            for n, m in enumerate((2, 3, 4, 5)):
                for b in range(B):
                    u = n * B + b
                    if u >= 4:
                        pe.wait_ge(s_modv, u - 2)
                    for k in range(KC):
                        last = pe.matmul(ps[:, 1 + u % 4, :], csb[:, k, b, :], wmod_s[:, k, m * D:(m + 1) * D],
                                         start=(k == 0), stop=(k == KC - 1))
                    last.then_inc(s_mod, 1)
            pe.wait_ge(s_modv, 9)
            pe.wait_ge(s_small, 176)
            pe.wait_ge(s_ready, 1)
            pe.sem_inc(s_pv, 2)

            def turn_x(b, i):
                t = b * TPB + i
                pe.wait_ge(s_hT, t)
                pe.wait_ge(s_xn, t + 1)
                for cc in range(KC):
                    last = pe.transpose(ps[:, 6, cc * P:(cc + 1) * P], xn[:, i % 2, cc * P:(cc + 1) * P], ident)
                last.then_inc(s_xT, 1)

            def project(b, i, step):
                t = b * TPB + i
                cc = step % KC
                if step == 0:
                    pe.wait_ge(s_hT, t + 1)
                if step < KC:
                    pe.matmul(ps[:, 4, :], hT[:, i % 2, cc, :], wq[:, cc, :], start=(cc == 0), stop=(cc == KC - 1))
                else:
                    last = pe.matmul(ps[:, 7, 0:2 * HD], hT[:, i % 2, cc, :], wkv[:, cc, :],
                                     start=(cc == 0), stop=(cc == KC - 1))
                    if step == 2 * KC - 1:
                        last.then_inc(s_q, 1)

            def pack(b, i):
                t = b * TPB + i
                pe.wait_ge(s_parts, t + 1)
                pe.wait_ge(s_qk, t + 1)
                pe.wait_ge(s_qT, t * NG)
                pe.transpose(ps[:, 7, 0:P], ks[:, :], ident)
                pe.transpose(ps[:, 7, P:2 * P], kh4[:, :, :].rearrange("p j d -> p (j d)"), ident)
                for g in range(NG):
                    last = pe.transpose(ps[:, 5, g * P:(g + 1) * P], qh[:, GH * g:GH * g + GH, :].rearrange("p j d -> p (j d)"), ident)
                last.then_inc(s_pack, 1)

            def row_max(b, i):
                t = b * TPB + i
                pe.wait_ge(s_packT, t + 1)
                for h in range(H):
                    if h < 2:
                        pe.wait_ge(s_max, t * H)
                    else:
                        pe.wait_ge(s_max, t * H + (h - 1))
                    flat = pair(h % 2).rearrange("p a n -> p (a n)")
                    width = (i + 1) * P
                    if i < TPB - 1 and 2 <= h < 2 + 2 * KC:
                        project(b, i + 1, h - 2)
                    for lo in range(0, width, 512):
                        hi = min(lo + 512, width)
                        pe.matmul(flat[:, lo:hi], qpT[:, h // GH, :], kpad[:, h % GH, lo:hi], start=True,
                                  stop=(hi < width))
                    pe.matmul(flat[:, width - P:width], ident_b[:, :], bias_b[:, :], start=False, stop=True)\
                      .then_inc(s_mm, 1)

            def stack(b, i):
                t = b * TPB + i
                pe.wait_ge(s_nmax, t + 1)
                if i < TPB - 1:
                    pe.wait_ge(s_qk, t + 2)
                for q4 in range(NG):
                    if q4 >= 2:
                        pe.wait_ge(s_qT, t * NG + (q4 - 1))
                    for j in range(GH):
                        last = pe.transpose(ps[:, 5 + 2 * (q4 % 2), j * P:(j + 1) * P], qs[:, i % 2, GH * q4 + j, :], ident)
                    last.then_inc(s_st, 1)

            def attend(b, qc):
                kts = TPC * (qc + 1)
                hold(pe, s_qT, (b * TPB + (qc + 1) * TPC) * NG)

                def scores(g, kt):
                    off = max(0, kt - TPC * qc) * P
                    for pr in range(2):
                        unit = b * UNITS_B + qc * (NG * 2 * TPC) + g * (2 * kts) + (2 * kt + pr)
                        hold(pe, s_exp, unit + 1)
                        for jj in range(2):
                            last = pe.matmul(ps[:, 2 * pr + jj, off:CH], kT[:, kt * P:kt * P + P],
                                             qT[:, ds(g * GH + (2 * pr + jj), 1), off:CH], start=True, stop=True)
                        last.then_inc(s_sc, 1)

                def values(g, kt):
                    off = max(0, kt - TPC * qc) * P
                    unit = b * UNITS_B + qc * (NG * 2 * TPC) + g * (2 * kts) + 2 * kt
                    if kt == 0:
                        pe.wait_ge(s_on, b * (QC * NG) + qc * NG + g)
                    if kt >= TPC * qc:
                        pe.wait_ge(s_mask, b * (QC * NG * TPC) + qc * (NG * TPC) + g * TPC + (kt - TPC * qc + 1))
                    else:
                        pe.wait_ge(s_exp, unit + 4)
                    for bank, left in ((4, v_sb[:, kt, :]), (5, ones[:, :])):
                        for j in range(GH):
                            last = pe.matmul(ps[HD * j:HD * j + HD, bank, off:CH], left, probs[:, kt % 2, j, off:CH],
                                             start=(kt == 0), stop=(kt == kts - 1))
                    last.then_inc(s_pv, 1)

                with pe.Fori(0, NG) as g:
                    for kt in range(kts):
                        scores(g, kt)
                        if kt:
                            values(g, kt - 1)
                        if qc == 1 and kt == AT_PROJECT:
                            pe.wait_ge(s_ot, b * NG + (g + 1))
                            out_project(o_tile, 6)
                        if qc == 1 and kt == AT_TURN:
                            turn(b * TPB + g, 6, 0)
                        if qc == 1 and kt == AT_LOGITS:
                            logits(b * TPB + g, g, 0)
                    values(g, kts - 1)

            def square_sums(b, qc):
                pe.wait_ge(s_sq, b * (QC * NG) + (qc + 1) * NG)
                for ii in range(TPC):
                    last = pe.matmul(ps[:, 6 - 4 * qc, ii:ii + 1], osq[:, ii * P:ii * P + P], ones[:, 0:1],
                                     start=True, stop=True)
                last.then_inc(s_oss, 1)

            def out_project(rows_t, bank):
                for g in range(NG):
                    last = pe.matmul(ps[:, bank, :], rows_t[:, g, :], wo[:, g, :], start=(g == 0), stop=(g == NG - 1))
                last.then_inc(s_at, 1)

            def turn(t, bank, slot):
                pe.wait_ge(s_h2, t + 1)
                for cc in range(KC):
                    last = pe.transpose(ps[:, bank, cc * P:(cc + 1) * P], h2[:, slot, cc * P:(cc + 1) * P], ident)
                last.then_inc(s_h2t, 1)

            def logits(t, i, slot):
                pe.wait_ge(s_h2T, t + 1)
                for cc in range(KC):
                    last = pe.matmul(ps[:, 7, ds(i * E, E)], h2T[:, slot, cc, :], rw[:, cc, :],
                                     start=(cc == 0), stop=(cc == KC - 1))
                last.then_inc(s_lg, 1)

            def finish_chunk(b):
                def project_tile(ii):
                    if ii >= 2:
                        pe.wait_ge(s_atd, b * TPB + (TPC + ii - 1))
                    out_project(oT[:, 1, :, ii * P:ii * P + P], 4 + 2 * (ii % 2))

                project_tile(0)
                for ii in range(TPC):
                    if ii + 1 < TPC:
                        project_tile(ii + 1)
                    if ii:
                        logits(b * TPB + (TPC + ii - 1), TPC + ii - 1, (ii - 1) % 2)
                    turn(b * TPB + (TPC + ii), ii % 2, ii % 2)
                logits(b * TPB + (TPB - 1), TPB - 1, 1)

            def count(b):
                pe.wait_ge(s_sel, b + 1)
                for i in range(TPB):
                    dst = ps[:, 7, i * E:(i + 1) * E]
                    pe.matmul(dst, ones_b[:, :], seen_b[:, :], start=True, stop=False)
                    for before in range(i):
                        pe.matmul(dst, ones_b[:, :], sel_b[:, before, :], start=False, stop=False)
                    last = pe.matmul(dst, upper_b[:, :], sel_b[:, i, :], start=False, stop=True)
                last.then_inc(s_pos, 1)

            with pe.Fori(0, B) as b:
                turn_x(b, 0)
                turn_x(b, 1)
                pe.wait_ge(s_pay, b + 1)
                for step in range(2 * KC):
                    project(b, 0, step)
                for i in range(TPB):
                    if i == TPC:
                        attend(b, 0)
                        square_sums(b, 0)
                    pack(b, i)
                    row_max(b, i)
                    if i + 2 < TPB:
                        turn_x(b, i + 2)
                    stack(b, i)
                attend(b, 1)
                square_sums(b, 1)
                finish_chunk(b)
                count(b)

            pe.sem_inc(s_T, 2)
            pe.sem_inc(s_gu, 2)
            pe.sem_inc(s_dn, 2)

            def turn_rows(n, p, arrived, loads):
                pe.wait_ge(s_xa, n)
                pe.wait_ge(s_xd, n)
                pe.wait_ge(arrived[p], loads * 32)
                for cc in range(KC):
                    for h in range(HALVES):
                        col = (cc % 2) * CAP + h * P
                        last = pe.transpose(ps[:, cc // 2, col:col + P], xg[p][:, h, cc * P:(cc + 1) * P], ident)
                last.then_inc(s_T, 1)

            def up(n, p, w):
                pe.wait_ge(s_xa, n + 1)
                pe.wait_ge(s_xd, n + 1)
                pe.wait_ge(s_hid, n + 1)
                for s, col in enumerate((0, IA + 2 * IB)):
                    for cc in range(KC):
                        pe.matmul(ps[0:IA, 2 + p, s * CAP:(s + 1) * CAP], w[:, cc, col:col + IA], xgT[p][:, cc, :],
                                  start=(cc == 0), stop=(cc == KC - 1))
                for cc in range(KC):
                    last = pe.matmul(ps[:, 4 + p, 0:CAP], w[:, cc, IA:IA + 2 * IB], xgT[p][:, cc, :],
                                     start=(cc == 0), stop=(cc == KC - 1))
                last.then_inc(s_gu, 1)

            def down(n, p, wa, wb):
                pe.wait_ge(s_hid, n + 3)
                pe.wait_ge(s_ya, n)
                pe.wait_ge(s_yd, n)
                for h in range(HALVES):
                    pe.matmul(ps[:, 6 + h, :], hid_a[p][:, h * P:(h + 1) * P], wa[:, :], start=True, stop=False)
                    last = pe.matmul(ps[:, 6 + h, :], hid_b[p][:, h * P:(h + 1) * P], wb[:, :], start=False, stop=True)
                last.then_inc(s_dn, 1)

            turn_rows(0, 0, s_xg, 1)
            pe.wait_ge(s_sh_w, 48)
            up(0, 0, sh_gu)
            turn_rows(1, 1, s_xg, 1)
            with pe.Fori(0, NSH // 2 - 1) as i:
                for p in range(2):
                    n = i * 2 + p
                    up(n + 1, 1 - p, sh_gu)
                    turn_rows(n + 2, p, s_xg, i + 2)
                    down(n, p, sh_da, sh_db)

            def expert_up(e, p, loads):
                pe.wait_ge(s_wu[p], loads * 16)
                up(e + NSH, p, e_gu[p])

            def expert_down(e, p, loads):
                pe.wait_ge(s_wd[p], loads * 32)
                down(e + NSH, p, e_da[p], e_db[p])

            up(NSH - 1, 1, sh_gu)
            turn_rows(NSH, 0, s_eg, 1)
            down(NSH - 2, 0, sh_da, sh_db)
            expert_up(0, 0, 1)
            turn_rows(NSH + 1, 1, s_eg, 1)
            down(NSH - 1, 1, sh_da, sh_db)
            with pe.Fori(0, E // 2 - 1) as i:
                for p in range(2):
                    e = i * 2 + p
                    expert_up(e + 1, 1 - p, i + (1 + p))
                    turn_rows(e + (NSH + 2), p, s_eg, i + 2)
                    expert_down(e, p, i + 1)
            expert_up(E - 1, 1, E // 2)
            for p in range(2):
                expert_down(E - 2 + p, p, E // 2)

        @block.vector
        def _(dve):
            dve.memset(qs[:, :, :, :], 0.0).then_inc(s_zero, 1)
            dve.memset(ones[:, :], 1.0)
            dve.memset(ones_b[:, :], 1.0)
            dve.memset(mhalf[:, :], -0.5)
            dve.memset(ks[:, :], 0.0)
            dve.memset(seen[:, :], 0.0)
            dve.memset(seen_b[:, :], 0.0)
            dve.wait_ge(s_small, 176)
            dve.tensor_copy(ident_b[:, :], ident)
            dve.tensor_copy(bias_b[:, :], mask_s[:, 0:P])
            dve.tensor_copy(upper_b[:, :], mask_s[:, P:2 * P])
            dve.drain()
            dve.memset(ks[:, 3 * HD:3 * HD + 2], 1.0)
            dve.scalar_tensor_tensor(wkq[:, :], wqn_s[:, :], float(HD) ** -0.5, wkn_s[:, :], ALU.mult, ALU.mult)
            for cc in range(KC):
                dve.tensor_scalar(wo[:, cc, :], wo[:, cc, :], wpre[:, cc:cc + 1], None, ALU.mult)
            dve.wait_ge(s_silu, 1)
            for k in range(KC):
                last = dve.tensor_copy(csb[:, k, :, :], silu_c[:, k, :].unsqueeze(2).to_broadcast([P, B, P]))
            last.then_inc(s_csb, 1)
            dve.wait_ge(s_mod, 1)
            cols = ps[:, 0, 0:2 * KC * B].rearrange("p (m c b) -> p m c b", m=2, c=KC)
            dve.tensor_copy(mcol[:, 0, :, :], cols[:, 0, :, :])
            dve.tensor_scalar(mcol[:, 1, :, :], cols[:, 1, :, :], 1.0, None, ALU.add).then_inc(s_modv, 1)
            for n, dst in enumerate((ga, sbias, cscale, gb)):
                for b in range(B):
                    u = n * B + b
                    dve.wait_ge(s_mod, u + 2)
                    src = ps[:, 1 + u % 4, :]
                    if dst is sbias:
                        dve.tensor_copy(dst[:, b, :], src).then_inc(s_modv, 1)
                    elif dst is cscale:
                        dve.tensor_scalar(dst[:, b, :], src, 1.0, None, ALU.add).then_inc(s_modv, 1)
                    else:
                        dve.drain()
                        dve.tensor_scalar(gate_t[:, :], src, 0.0, 0.5, ALU.is_ge, ALU.subtract)
                        dve.drain()
                        dve.scalar_tensor_tensor(gate_a[:, :], gate_t[:, :], 2.0, src, ALU.mult, ALU.mult)\
                           .then_inc(s_modv, 1)
                        dve.drain()
                        dve.tensor_scalar(gate_a[:, :], gate_a[:, :], 0.25, 2.0, ALU.max, ALU.mult)
                        dve.drain()
                        dve.tensor_tensor(dst[:, b, :], gate_t[:, :], gate_a[:, :], ALU.mult)
            dve.memset(kpad[:, :, :].bitcast(f32), 0.0)
            dve.drain()
            dve.sem_inc(s_ready, 1)
            dve.wait_ge(s_init, 48)
            dve.wait_ge(s_x, 64)
            for t in range(NT):
                dve.bn_stats(st[:, t, :], xres[:, t, :])
            dve.memset(pay[:, :, :, :], 0)
            dve.tensor_scalar(idx8[:, :, :], trash, -1.0, None, ALU.add).then_inc(s_pay, 1)
            dve.drain()
            for t in range(NT):
                dve.bn_aggr(mv[:, t, :], st[:, t, :])
            dve.drain()
            dve.tensor_scalar(ve[:, :], mv[:, :, 1], LN_EPS, None, ALU.add).then_inc(s_var, 1)

            def normalise(b, i):
                dve.wait_ge(s_xT, b * TPB + max(i - 1, 0))
                t = b * TPB + i
                dve.tensor_scalar(xn[:, i % 2, :], xtile(t), mv[:, ds(t, 1), 0], rstd[:, ds(t, 1)],
                                  ALU.subtract, ALU.mult).then_inc(s_xn, 1)

            def rotate(b, i):
                t = b * TPB + i
                half = HD // 2
                shape = [P, H + 1, half]
                dve.wait_ge(s_qk, t + 1)
                dve.tensor_tensor(t1[:, :, :], qk[:, :, :], cos[:, i, :].unsqueeze(1).to_broadcast([P, H + 1, HD]), ALU.mult)
                dve.tensor_tensor(t2[:, :, 0:half], qk[:, :, half:HD],
                                  sin[:, i, 0:half].unsqueeze(1).to_broadcast(shape), ALU.mult)
                dve.tensor_tensor(t2[:, :, half:HD], qk[:, :, 0:half],
                                  sin[:, i, half:HD].unsqueeze(1).to_broadcast(shape), ALU.mult).then_inc(s_rope, 1)
                dve.drain()
                dve.tensor_tensor(qr[:, :, :], t1[:, :, :], t2[:, :, :], ALU.add)
                dve.drain()
                dve.tensor_tensor(t1[:, :, :], qr[:, :, :], qr[:, :, :], ALU.mult)
                dve.drain()
                dve.reduce_sum(ssq[:, :], t1[:, :, :], AX.X)
                dve.drain()
                dve.tensor_scalar(ms[:, :], ssq[:, :], 1.0 / HD, RMS_EPS, ALU.mult, ALU.add).then_inc(s_ms, 1)

            def split(b, i):
                t = b * TPB + i
                q_parts = qs[:, i % 2, :, :]
                dve.wait_ge(s_rr, t + 1)
                dve.tensor_tensor(t2[:, :, :], qr[:, :, :], rr[:, :].unsqueeze(2).to_broadcast([P, H + 1, HD]), ALU.mult)
                dve.drain()
                dve.wait_ge(s_st, (b * TPB + max(i - 1, 0)) * NG)
                dve.tensor_copy(q_parts[:, :, 0:HD].bitcast(f32r), t2[:, 0:H, :])
                dve.tensor_copy(q_parts[:, :, HD:2 * HD].bitcast(f32r), t2[:, 0:H, :])
                dve.tensor_tensor(t1[:, H, :], t2[:, H, :], wkq[:, :], ALU.mult)
                dve.drain()
                dve.wait_ge(s_pack, t)
                dve.tensor_copy(qh[:, :, :].bitcast(f32r), t2[:, 0:H, :])
                dve.tensor_copy(ks[:, 0:HD].bitcast(f32r), t1[:, H, :])
                dve.tensor_copy(ks[:, 2 * HD:3 * HD].bitcast(f32r), t1[:, H, :])
                dve.tensor_copy(kh4[:, :, :].bitcast(f32r), t1[:, H, :].unsqueeze(1).to_broadcast([P, GH, HD]))
                dve.tensor_tensor(q_parts[:, :, 2 * HD:3 * HD].bitcast(f32r), t2[:, 0:H, :], q_parts[:, :, 0:HD],
                                  ALU.subtract)
                dve.drain()
                dve.tensor_tensor(ks[:, HD:2 * HD].bitcast(f32r), t1[:, H, :], ks[:, 0:HD], ALU.subtract)\
                   .then_inc(s_parts, 1)

            def row_max(b, i):
                t = b * TPB + i
                q_parts = qs[:, i % 2, :, :]
                for h in range(H):
                    if h == 12 and i + 1 < TPB:
                        rotate(b, i + 1)
                        if i + 2 < TPB:
                            normalise(b, i + 2)
                    dve.wait_ge(s_mm, t * H + (h + 1))
                    dve.tensor_reduce(nmax[:, h:h + 1], pair(h % 2).rearrange("p a n -> p (a n)")[:, 0:(i + 1) * P],
                                      AX.X, ALU.max, negate=True).then_inc(s_max, 1)
                dve.drain()
                dve.tensor_copy(q_parts[:, :, 3 * HD].bitcast(f32r), nmax[:, :])
                dve.drain()
                dve.tensor_tensor(q_parts[:, :, 3 * HD + 1].bitcast(f32r), nmax[:, :], q_parts[:, :, 3 * HD],
                                  ALU.subtract).then_inc(s_nmax, 1)

            def divide(b, qc):
                kts = TPC * (qc + 1)
                dve.wait_ge(s_oss, b * QC + qc)
                dve.memset(osq[:, :], 0.0)
                dve.drain()
                with dve.Fori(0, NG) as g:
                    if qc == 1:
                        residual(b, 0, g, 6, 0)
                        shift(b, 0, g, 0)
                    dve.wait_ge(s_pv, b * PVS_B + qc * (NG * TPC) + g * kts + (kts + 2))
                    dve.reciprocal(scratch[:, :], ps[:, 5, :])
                    dve.drain()
                    row = oT[:, qc, ds(g, 1), :].rearrange("p a n -> p (a n)")
                    dve.tensor_tensor(row, ps[:, 4, :], scratch[:, :], ALU.mult).then_inc(s_on, 1)
                    dve.drain()
                    dve.tensor_tensor(scratch[:, :], row, row, ALU.mult)
                    dve.drain()
                    dve.tensor_tensor(osq[:, :], osq[:, :], scratch[:, :], ALU.add).then_inc(s_sq, 1)
                    dve.drain()
                dve.wait_ge(s_oss, b * QC + (qc + 1))
                dve.tensor_scalar(oms[:, :], ps[:, 6 - 4 * qc, 0:TPC], 1.0 / D, RMS_EPS, ALU.mult, ALU.add)\
                   .then_inc(s_oms, 1)

            def residual(b, qc, ii, bank, slot):
                t = b * TPB + (ii + qc * TPC)
                dve.wait_ge(s_orstd, b * QC + (qc + 1))
                dve.wait_ge(s_at, t + 1)
                dve.scalar_tensor_tensor(scratch[:, :], ps[:, bank, :], orstd[:, qc, ds(ii, 1)], rows(b, ga),
                                         ALU.mult, ALU.mult).then_inc(s_atd, 1)
                dve.drain()
                xt = xtile(t)
                dve.tensor_tensor(xt, xt, scratch[:, :], ALU.add)
                dve.drain()
                dve.bn_stats(st2[:, slot, :], xt)
                dve.drain()
                dve.bn_aggr(mv2[:, slot, :], st2[:, slot, :])
                dve.drain()
                dve.tensor_scalar(ve2[:, slot:slot + 1], mv2[:, slot, 1:2], LN_EPS, None, ALU.add).then_inc(s_var2, 1)

            def shift(b, qc, ii, slot):
                t = b * TPB + (ii + qc * TPC)
                row = h2[:, slot, :]
                dve.wait_ge(s_rstd2, t + 1)
                dve.wait_ge(s_h2_out[slot], (b * STORED[slot] + (ii if qc == 0 else TPC * (1 - slot) + ii // 2)) * 16)
                dve.wait_ge(s_h2t, b * TPB + (ii if qc == 0 else TPC + max(ii - 1, 0)))
                dve.tensor_scalar(row, xtile(t), mv2[:, slot, 0:1], rstd2[:, slot:slot + 1], ALU.subtract, ALU.mult)
                dve.drain()
                dve.tensor_tensor(row, row, rows(b, cscale), ALU.mult)
                dve.drain()
                dve.tensor_tensor(row, row, rows(b, sbias), ALU.add).then_inc(s_h2, 1)

            def route(b):
                all_e = [P, TPB, E]
                grp = [P, TPB, GROUPS, GROUPS]
                dve.wait_ge(s_ex, b + 1)
                dve.tensor_scalar(biased[:, :, :], ex[:, :, :], 1.0, None, ALU.add)
                dve.drain()
                dve.reciprocal(score[:, :, :], biased[:, :, :])
                dve.drain()
                dve.tensor_tensor(biased[:, :, :], score[:, :, :], ebias[:, :].unsqueeze(1).to_broadcast(all_e), ALU.add)
                dve.drain()
                v = biased[:, :, :].rearrange("p t (g m) -> p (t g) m", m=GROUPS)
                dve.tensor_tensor(hi4[:, :, :], v[:, :, 0:4], v[:, :, 4:8], ALU.max)
                dve.tensor_tensor(lo4[:, :, :], v[:, :, 0:4], v[:, :, 4:8], ALU.min)
                dve.drain()
                dve.tensor_tensor(hi2[:, :, :], hi4[:, :, 0:2], hi4[:, :, 2:4], ALU.max)
                dve.tensor_tensor(mid2[:, :, :], hi4[:, :, 0:2], hi4[:, :, 2:4], ALU.min)
                dve.tensor_tensor(lo2[:, :, :], lo4[:, :, 0:2], lo4[:, :, 2:4], ALU.max)
                dve.drain()
                dve.tensor_tensor(lo2[:, :, :], lo2[:, :, :], mid2[:, :, :], ALU.max)
                dve.tensor_tensor(hi1[:, :], hi2[:, :, 0], hi2[:, :, 1], ALU.max)
                dve.tensor_tensor(mid1[:, :], hi2[:, :, 0], hi2[:, :, 1], ALU.min)
                dve.drain()
                dve.tensor_tensor(lo1[:, :], lo2[:, :, 0], lo2[:, :, 1], ALU.max)
                dve.drain()
                dve.tensor_tensor(lo1[:, :], lo1[:, :], mid1[:, :], ALU.max)
                dve.drain()
                gs = gsum[:, :, :]
                dve.tensor_tensor(gs.rearrange("p t g -> p (t g)"), hi1[:, :], lo1[:, :], ALU.add)
                dve.drain()
                other, own = gs.unsqueeze(2).to_broadcast(grp), gs.unsqueeze(3).to_broadcast(grp)
                dve.tensor_tensor(cmp_a[:, :, :, :], other, own, ALU.is_gt)
                dve.tensor_tensor(cmp_b[:, :, :, :], other, own, ALU.is_equal)
                dve.drain()
                dve.tensor_tensor(cmp_b[:, :, :, :], cmp_b[:, :, :, :], tri.unsqueeze(1).to_broadcast(grp), ALU.mult)
                dve.drain()
                dve.tensor_tensor(cmp_a[:, :, :, :], cmp_a[:, :, :, :], cmp_b[:, :, :, :], ALU.add)
                dve.drain()
                dve.reduce_sum(grank[:, :, :], cmp_a[:, :, :, :], AX.X)
                dve.drain()
                dve.tensor_scalar(grank[:, :, :], grank[:, :, :], float(TOPG), None, ALU.is_lt)
                dve.drain()
                dve.tensor_tensor(masked[:, :, :].rearrange("p t (g m) -> p t g m", m=GROUPS),
                                  biased[:, :, :].rearrange("p t (g m) -> p t g m", m=GROUPS),
                                  grank[:, :, :].unsqueeze(3).to_broadcast(grp), ALU.mult)
                dve.drain()
                for ii in range(TPB):
                    dve.max(top8[:, ii, :], masked[:, ii, :])
                dve.drain()
                for ii in range(TPB):
                    dve.match_replace(marked[:, ii, :], top8[:, ii, :], masked[:, ii, :], -3e38)
                dve.drain()
                dve.tensor_scalar(sel_b[:, :, :], marked[:, :, :], -3e38, None, ALU.is_equal).then_inc(s_sel, 1)
                dve.tensor_scalar(sel[:, :, :], marked[:, :, :], -3e38, None, ALU.is_equal)
                dve.drain()
                dve.tensor_tensor(wts[:, :, :], score[:, :, :], sel[:, :, :], ALU.mult)
                dve.reduce_sum(selsum[:, :], sel[:, :, :].rearrange("p t e -> p e t"), AX.X)
                dve.drain()
                dve.reduce_sum(wsum[:, :], wts[:, :, :], AX.X)
                dve.tensor_tensor(seen[:, :], seen[:, :], selsum[:, :], ALU.add)
                dve.drain()
                dve.tensor_scalar(wsum[:, :], wsum[:, :], 1e-20, None, ALU.add)
                dve.drain()
                dve.reciprocal(wrec[:, :], wsum[:, :])
                dve.drain()
                dve.tensor_tensor(wts[:, :, :], wts[:, :, :], wrec[:, :].unsqueeze(2).to_broadcast(all_e), ALU.mult)
                dve.wait_ge(s_pos, b + 1)
                pos = ps[:, 7, :].rearrange("p (t e) -> p t e", e=E)
                dve.tensor_copy(seen_b[:, :], seen[:, :])
                dve.tensor_scalar(hv[:, :, :], pos, float(P), 1.0 - P * P, ALU.is_ge, ALU.mult)
                dve.scalar_tensor_tensor(valid[:, :, :], pos, float(CAP), sel[:, :, :], ALU.is_lt, ALU.mult)
                dve.drain()
                dve.scalar_tensor_tensor(key[:, :, :], pos, float(P), hv[:, :, :], ALU.mult, ALU.add)
                dve.drain()
                dve.tensor_tensor(key[:, :, :], key[:, :, :], erow.unsqueeze(1).to_broadcast(all_e), ALU.add)
                dve.drain()
                dve.tensor_tensor(key[:, :, :], key[:, :, :], valid[:, :, :], ALU.mult)
                dve.drain()
                for ii in range(TPB):
                    dve.max(key8[:, ii, :], key[:, ii, :])
                dve.drain()
                eight = [P, TOPK, E]
                for ii in range(TPB):
                    dve.tensor_tensor(eq8[:, :, :], key8[:, ii, :].unsqueeze(2).to_broadcast(eight),
                                      key[:, ii, :].unsqueeze(1).to_broadcast(eight), ALU.is_equal)
                    dve.drain()
                    dve.tensor_tensor(eq8[:, :, :], eq8[:, :, :], wts[:, ii, :].unsqueeze(1).to_broadcast(eight), ALU.mult)
                    dve.drain()
                    dve.reduce_sum(w8[:, ii, :], eq8[:, :, :], AX.X)
                    dve.drain()
                dve.wait_ge(s_slot, (b + 1) * SLOTTED)
                dve.tensor_scalar(pay[:, :, :, 1].bitcast(f32), w8[:, :, :], ROUTED_SCALE, None, ALU.mult)
                dve.tensor_copy(pay[:, :, :, 0], tokid[:, ds(b * TPB, TPB)].unsqueeze(2).to_broadcast([P, TPB, TOPK]))
                dve.scalar_tensor_tensor(miss8[:, :, :], key8[:, :, :], 0.0, trash, ALU.is_equal, ALU.mult)
                dve.drain()
                dve.scalar_tensor_tensor(idx8[:, :, :], key8[:, :, :], -1.0, miss8[:, :, :], ALU.add, ALU.add)\
                   .then_inc(s_pay, 1)

            dve.wait_ge(s_rstd, 1)
            with dve.Fori(0, B) as b:
                normalise(b, 0)
                normalise(b, 1)
                rotate(b, 0)
                for i in range(TPB):
                    split(b, i)
                    if i == TPC:
                        divide(b, 0)
                    row_max(b, i)
                divide(b, 1)
                residual(b, 1, 0, 4, 0)
                for ii in range(TPC):
                    if ii + 1 < TPC:
                        residual(b, 1, ii + 1, 4 + 2 * ((ii + 1) % 2), (ii + 1) % 2)
                    shift(b, 1, ii, ii % 2)
                route(b)

            for p in range(2):
                dve.memset(hid_b[p][IB:IBP, :], 0.0)
                dve.memset(e_db[p][IB:IBP, :], 0.0)
            dve.memset(sh_db[IB:IBP, :], 0.0)
            dve.drain()
            dve.sem_inc(s_hid, 2)

            def x_out(n, p):
                dve.wait_ge(s_gu, n + 1)
                dve.wait_ge(s_T, n + 3)
                dve.tensor_copy(xgT[p][:, 2:4, :], ps[:, 1, :].rearrange("p (c t) -> p c t", t=CAP)).then_inc(s_xd, 1)

            def hidden(n, p):
                dve.wait_ge(s_dn, n + 1)
                dve.wait_ge(s_act, n + 1)
                dve.tensor_tensor(hid_a[p][:, :], gact_a[p][:, :], ps[0:IA, 2 + p, CAP:2 * CAP], ALU.mult)
                dve.tensor_tensor(hid_b[p][0:IB, :], gact_b[p][:, :], ps[IB:2 * IB, 4 + p, 0:CAP], ALU.mult)\
                   .then_inc(s_hid, 1)

            x_out(0, 0)
            hidden(0, 0)
            x_out(1, 1)
            with dve.Fori(0, NSH // 2) as i:
                for p in range(2):
                    n = i * 2 + p
                    hidden(n + 1, 1 - p)
                    x_out(n + 2, p)
                    dve.wait_ge(s_dn, n + 3)
                    for h, done in enumerate((s_ya, s_yd)):
                        dve.tensor_tensor(y[p][:, h, :], ps[:, 6 + h, :], rows(i // (NSH // 2 // B), gb), ALU.mult)\
                           .then_inc(done, 1)
                    dve.drain()
                    for h in range(HALVES):
                        xt = xtile(n * HALVES + h)
                        dve.tensor_tensor(xt, xt, y[p][:, h, :], ALU.add)
                    dve.drain()

            def weighted(e, p):
                dve.wait_ge(s_yfree, e)
                dve.wait_ge(s_dn, e + NSH + 3)
                dve.tensor_scalar(y[p][:, 1, :], ps[:, 7, :], slots[:, ds(e * HALVES + 1, 1), 1].bitcast(f32), None,
                                  ALU.mult).then_inc(s_yd, 1)

            dve.wait_ge(s_slots_in, 16)
            with dve.Fori(0, E // 2 - 1) as i:
                for p in range(2):
                    hidden(i * 2 + (p + NSH + 1), 1 - p)
                    x_out(i * 2 + (p + NSH + 2), p)
                    weighted(i * 2 + p, p)
            hidden(E + NSH - 1, 1)
            for p in range(2):
                weighted(E - 2 + p, p)

            for c in range(NT // TPC):
                dve.wait_ge(s_fin_in[c % 2], 16 * (c // 2 + 1))
                part = fin_acc[:, c % 2, :, :]
                dve.tensor_tensor(part, part, gb[:, c // QC, :].unsqueeze(1).to_broadcast([P, TPC, D]), ALU.mult)
                dve.drain()
                xc = xres[:, TPC * c:TPC * c + TPC, :]
                dve.tensor_tensor(xc, xc, part, ALU.add).then_inc(s_fin, 1)


def shape_constants(np):
    p = np.arange(P)
    con = np.zeros((P, NCONST), np.float32)
    con[:, C_ID:C_ID + P] = np.eye(P)
    masks = np.zeros((P, 2 * P), np.float32)
    masks[:, 0:P] = np.where(p[None, :] <= p[:, None], 0.0, -1e30)
    masks[:, P:2 * P] = p[:, None] < p[None, :]
    inv = np.float32(1.0) / np.float32(10000.0) ** (np.arange(0, HD, 2, dtype=np.float32) / np.float32(HD))
    ang = np.arange(S, dtype=np.float32)[:, None] * inv[None, :]
    c, s = np.cos(ang), np.sin(ang)
    tile = lambda a: a.reshape(TPB, P, HD).transpose(1, 0, 2).reshape(P, TPB * HD)
    con[:, C_COS:C_SIN] = tile(np.concatenate([c, c], 1))
    con[:, C_SIN:C_EROW] = tile(np.concatenate([-s, s], 1))
    con[:, C_EROW:C_TRI] = 2 * np.arange(E) + 1
    g = np.arange(GROUPS)
    con[:, C_TRI:C_TRASH] = (g[None, :] < g[:, None]).reshape(1, -1)
    con[:, C_TRASH:NCONST] = NSLOT + 1 + np.arange(TPB * TOPK)[None, :] * P + p[:, None]
    tokid = (np.arange(NT)[None, :] * P + p[:, None]).astype(np.int32)
    slot = np.zeros((P, E * HALVES, 2), np.int32)
    slot[:, :, 0] = NTOK + (np.arange(E * HALVES) % HALVES)[None, :] * P + p[:, None]
    return con, masks, tokid, slot.reshape(P, -1)


def kernel(**inputs):
    import numpy as np
    import concourse.bacc as bacc
    from concourse.bass_utils import run_bass_kernel_spmd

    a = {k: np.asarray(v) for k, v in inputs.items()}
    chunks = lambda w: np.ascontiguousarray(w.reshape(KC, P, -1).transpose(1, 0, 2))
    con, masks, tokid, slot = shape_constants(np)
    join = lambda g, u: np.concatenate([g, u[..., IA:], u[..., :IA]], axis=-1)
    gate_up = join(a["L0_ffn_w_gate"], a["L0_ffn_w_up"])
    arrays = {
        "x": np.ascontiguousarray(a["L0_attn_x"].reshape(NTOK, D)),
        "c_t": chunks(np.ascontiguousarray(a["L0_c"].T)),
        "wmod": np.ascontiguousarray(a["L0_wmod"]),
        "wq_t": chunks(np.ascontiguousarray(a["L0_attn_Wq"].T)),
        "wkv_t": chunks(np.concatenate([a["L0_attn_Wk"].T, a["L0_attn_Wv"].T], axis=1)),
        "wo_t": chunks(np.ascontiguousarray(a["L0_attn_Wo"].T)),
        "w_pre": np.ascontiguousarray(a["L0_attn_w_pre"].reshape(KC, P).T),
        "w_qn": np.ascontiguousarray(a["L0_attn_w_qn"]),
        "w_kn": np.ascontiguousarray(a["L0_attn_w_kn"]),
        "router_t": chunks(np.ascontiguousarray(a["L0_ffn_router_weight"].T)),
        "e_bias": np.ascontiguousarray(a["L0_ffn_e_bias"]),
        "gate_up": np.ascontiguousarray(gate_up.reshape(E, KC, P, 2 * EI).transpose(0, 2, 1, 3)),
        "w_down": np.ascontiguousarray(a["L0_ffn_w_down"]),
        "sh_gate_up": chunks(join(a["L0_ffn_sh_gate"], a["L0_ffn_sh_up"])),
        "sh_down": np.ascontiguousarray(a["L0_ffn_sh_down"]),
        "consts": con,
        "masks": masks,
        "tokids": tokid,
        "slot_init": slot,
    }
    nc = bacc.Bacc("TRN2", target_bir_lowering=False, num_devices=1)
    args = [nc.dram_tensor(f"in_{n}", v.shape, mybir.dt.from_np(v.dtype), kind="ExternalInput").ap()
            for n, v in arrays.items()]
    out = nc.dram_tensor("out", (NTOK, D), mybir.dt.float32, kind="ExternalOutput").ap()
    build_program(nc, *args, out)
    r = run_bass_kernel_spmd(nc, [{f"in_{n}": v for n, v in arrays.items()}], core_ids=[0])
    return r.results[0]["out"].reshape(B, S, D)
```

```python
import concourse.bass as bass
from concourse import mybir
from contextlib import ExitStack

B, S, D = 2, 1024, 512
H, HD = 16, 32
P = 128
NTOK = B * S
TPB = S // P
NT = NTOK // P
CH = 512
TPC = CH // P
QC = S // CH
KC = D // P
GH = 4
NG = H // GH
E, EI, TOPK, GROUPS, TOPG = 64, 176, 8, 8, 4
CAP = 2 * 1024 * TOPK // E
HALVES = CAP // P
NSLOT = E * CAP
ROUTED_SCALE = 2.5
LN_EPS, RMS_EPS = 1e-5, 1e-6
EXTRA = CAP
IA = 112
IB = EI - IA
NSH = NTOK // CAP
UNITS_B = sum(NG * 2 * TPC * (qc + 1) for qc in range(QC))
PVS_B = UNITS_B // 2

C_ID = 0
C_COS = P
C_SIN = C_COS + TPB * HD
C_EROW = C_SIN + TPB * HD
C_TRI = C_EROW + E
C_TRASH = C_TRI + GROUPS * GROUPS
NCONST = C_TRASH + TPB * TOPK


def build_program(nc, x, c_t, wmod, wq_t, wkv_t, wo_t, w_pre, w_qn, w_kn, router_t, e_bias,
                  gate_up, w_down, sh_gate_up, sh_down, consts, masks, tokids, slot_init, out):
    f32, f32r, bf16, i32 = mybir.dt.float32, mybir.dt.float32r, mybir.dt.bfloat16, mybir.dt.int32
    ALU, ACT, AX = mybir.AluOpType, mybir.ActivationFunctionType, mybir.AxisListType
    ds = bass.ds

    h2_dram = nc.dram_tensor("h2_dram", [NTOK + EXTRA, D + E], f32).ap()
    acc_dram = nc.dram_tensor("acc_dram", [NTOK + EXTRA, D], f32).ap()
    rows_dram = nc.dram_tensor("rows_dram", [B, 4 * D], f32).ap()
    slot_dram = nc.dram_tensor("slot_dram", [NSLOT + TPB * TOPK * P, 1], i32).ap()

    ctx = ExitStack()
    with ctx:
        def sem(name):
            return ctx.enter_context(nc.semaphore(name))

        def sb(where, name, shape, dt=f32):
            return where.enter_context(nc.sbuf_tensor(name, shape, dt))

        xres = sb(ctx, "xres", [P, NT, D])
        con = sb(ctx, "con", [P, NCONST])
        mods = sb(ctx, "mods", [P, 4, B, D])
        mcol = sb(ctx, "mcol", [P, 2, KC, B])
        ident_b = sb(ctx, "ident_b", [P, P], bf16)
        bias_b = sb(ctx, "bias_b", [P, P], bf16)
        upper_b = sb(ctx, "upper_b", [P, P], bf16)
        ones_b = sb(ctx, "ones_b", [P, P], bf16)
        ones = sb(ctx, "ones", [P, HD])
        mhalf = sb(ctx, "mhalf", [P, NT + 1])
        tokid = sb(ctx, "tokid", [P, NT], i32)
        ebias = sb(ctx, "ebias", [P, E])
        wkq = sb(ctx, "wkq", [P, HD])
        rw = sb(ctx, "rw", [P, KC, E])
        wo = sb(ctx, "wo", [P, KC, D])

        mv = sb(ctx, "mv", [P, NT, 2])
        ve = sb(ctx, "ve", [P, NT])
        rstd = sb(ctx, "rstd", [P, NT])

        att = ExitStack()
        kpad = sb(att, "kpad", [P, GH, S], f32r)
        qs = sb(att, "qs", [P, 2, H, P])
        wq = sb(att, "wq", [P, KC, D])
        wkv = sb(att, "wkv", [P, KC, 2 * HD])
        ks = sb(att, "ks", [P, P])
        kh4 = sb(att, "kh4", [P, GH, HD])
        qh = sb(att, "qh", [P, H, HD])
        qpT = sb(att, "qpT", [P, NG, P], f32r)
        qk = sb(att, "qk", [P, H + 1, HD])
        t1 = sb(att, "t1", [P, H + 1, HD])
        t2 = sb(att, "t2", [P, H + 1, HD])
        qr = sb(att, "qr", [P, H + 1, HD])
        xn = sb(att, "xn", [P, 2, D])
        hT = sb(att, "hT", [P, 2, KC, P])
        pre = ExitStack()
        wmod_s = sb(pre, "wmod_s", [P, KC, 6 * D])
        ct_s = sb(pre, "ct_s", [P, KC, B])
        gate_t = sb(pre, "gate_t", [B, D])
        gate_a = sb(pre, "gate_a", [B, D])
        mod_rows = sb(pre, "mod_rows", [B, 4, D])
        mask_s = sb(pre, "mask_s", [P, 2 * P])
        wqn_s = sb(pre, "wqn_s", [P, HD])
        wkn_s = sb(pre, "wkn_s", [P, HD])
        wpre = sb(pre, "wpre", [P, KC])
        silu_c = sb(pre, "silu_c", [P, KC, B])
        st = sb(pre, "st", [P, NT, 6])
        pre.close()
        rout = ExitStack()
        RG = TPB * GROUPS
        ex = sb(rout, "ex", [P, TPB, E])
        score = sb(rout, "score", [P, TPB, E])
        biased = sb(rout, "biased", [P, TPB, E])
        hi4 = sb(rout, "hi4", [P, RG, 4])
        lo4 = sb(rout, "lo4", [P, RG, 4])
        hi2 = sb(rout, "hi2", [P, RG, 2])
        lo2 = sb(rout, "lo2", [P, RG, 2])
        mid2 = sb(rout, "mid2", [P, RG, 2])
        hi1 = sb(rout, "hi1", [P, RG])
        lo1 = sb(rout, "lo1", [P, RG])
        mid1 = sb(rout, "mid1", [P, RG])
        gsum = sb(rout, "gsum", [P, TPB, GROUPS])
        cmp_a = sb(rout, "cmp_a", [P, TPB, GROUPS, GROUPS])
        cmp_b = sb(rout, "cmp_b", [P, TPB, GROUPS, GROUPS])
        grank = sb(rout, "grank", [P, TPB, GROUPS])
        masked = sb(rout, "masked", [P, TPB, E])
        top8 = sb(rout, "top8", [P, TPB, TOPK])
        marked = sb(rout, "marked", [P, TPB, E])
        sel = sb(rout, "sel", [P, TPB, E])
        sel_b = sb(rout, "sel_b", [P, TPB, E], bf16)
        selsum = sb(rout, "selsum", [P, E])
        wts = sb(rout, "wts", [P, TPB, E])
        wsum = sb(rout, "wsum", [P, TPB])
        wrec = sb(rout, "wrec", [P, TPB])
        hv = sb(rout, "hv", [P, TPB, E])
        valid = sb(rout, "valid", [P, TPB, E])
        key = sb(rout, "key", [P, TPB, E])
        key8 = sb(rout, "key8", [P, TPB, TOPK])
        miss8 = sb(rout, "miss8", [P, TPB, TOPK])
        rout.close()
        qT = sb(att, "qT", [P, H, CH], f32r)
        probs = sb(att, "probs", [P, 2, GH, CH])
        oT = sb(att, "oT", [P, QC, NG, CH])
        h2 = sb(att, "h2", [P, 2, D])
        h2T = sb(att, "h2T", [P, 2, KC, P])
        kT = sb(att, "kT", [P, S], f32r)
        v_sb = sb(att, "v_sb", [P, TPB, HD])
        osq = sb(att, "osq", [P, CH])
        scratch = sb(att, "scratch", [P, CH])
        st2 = sb(att, "st2", [P, 2, 6])
        mv2 = sb(att, "mv2", [P, 2, 2])
        ve2 = sb(att, "ve2", [P, 2])
        rstd2 = sb(att, "rstd2", [P, 2])
        oms = sb(att, "oms", [P, TPC])
        orstd = sb(att, "orstd", [P, QC, TPC])
        ssq = sb(att, "ssq", [P, H + 1])
        ms = sb(att, "ms", [P, H + 1])
        rr = sb(att, "rr", [P, H + 1])
        nmax = sb(att, "nmax", [P, 2, H])
        seen = sb(att, "seen", [P, E])
        seen_b = sb(att, "seen_b", [P, E], bf16)
        idx8 = sb(att, "idx8", [P, TPB, TOPK], i32)
        pay = sb(att, "pay", [P, TPB], i32)
        att.close()

        moe = ExitStack()
        sh_gu = sb(moe, "sh_gu", [P, KC, 2 * EI])
        sh_d = sb(moe, "sh_d", [IA, 2, D])
        xg = [sb(moe, f"xg{p}", [P, HALVES, D + E]) for p in range(2)]
        x_hi = [sb(moe, f"x_hi{p}", [P, KC, CAP], f32r) for p in range(2)]
        x_lo = [sb(moe, f"x_lo{p}", [P, KC, CAP], f32r) for p in range(2)]
        sh_gu_hi = sb(moe, "sh_gu_hi", [P, KC, 2 * EI], f32r)
        sh_gu_lo = sb(moe, "sh_gu_lo", [P, KC, 2 * EI], f32r)
        sh_d_hi = sb(moe, "sh_d_hi", [P, 2, D], f32r)
        sh_d_lo = sb(moe, "sh_d_lo", [IA, D], f32r)
        gact_a = [sb(moe, f"gact_a{p}", [IA, CAP]) for p in range(2)]
        gact_b = [sb(moe, f"gact_b{p}", [IB, CAP]) for p in range(2)]
        hid = sb(moe, "hid", [IA, 2, CAP])
        hid_hi = [sb(moe, f"hid_hi{p}", [P, 2, CAP], f32r) for p in range(2)]
        hid_lo = [sb(moe, f"hid_lo{p}", [P, 2, CAP], f32r) for p in range(2)]
        y = [sb(moe, f"y{p}", [P, HALVES, D]) for p in range(2)]
        e_gu = [sb(moe, f"e_gu{p}", [P, KC, 2 * EI]) for p in range(2)]
        e_d = [sb(moe, f"e_d{p}", [IA, 2, D]) for p in range(2)]
        e_gu_hi = [sb(moe, f"e_gu_hi{p}", [P, KC, 2 * EI], f32r) for p in range(2)]
        e_gu_lo = [sb(moe, f"e_gu_lo{p}", [P, KC, 2 * EI], f32r) for p in range(2)]
        e_d_hi = [sb(moe, f"e_d_hi{p}", [P, 2, D], f32r) for p in range(2)]
        e_d_lo = [sb(moe, f"e_d_lo{p}", [IA, D], f32r) for p in range(2)]
        slots = sb(moe, "slots", [P, E * HALVES], i32)
        weight = sb(moe, "weight", [P, E * HALVES])
        from_ix = [sb(moe, f"from_ix{q}", [P, HALVES], i32) for q in range(4)]
        to_ix = [sb(moe, f"to_ix{q}", [P, HALVES], i32) for q in range(4)]
        moe.close()
        fin = ExitStack()
        fin_acc = sb(fin, "fin_acc", [P, NT // TPC, TPC, D])
        fin.close()

        ps = ctx.enter_context(nc.psum_tensor("ps", [P, 8, 512], f32))

        def pair(n):
            return ps[:, 2 * n:2 * n + 2, :]

        sq = h2T[:, :, :, :].rearrange("p a c t -> p (a c t)")[:, 0:(H + 1) * HD].rearrange("p (h d) -> p h d", d=HD)
        o_tile = qh[:, :, :].rearrange("p (g j) d -> p g (j d)", j=GH)
        ga, sbias, cscale, gb = (mods[:, n, :, :] for n in range(4))
        ident = con[:, C_ID:C_ID + P]
        cos = con[:, C_COS:C_SIN].rearrange("p (t d) -> p t d", d=HD)
        sin = con[:, C_SIN:C_EROW].rearrange("p (t d) -> p t d", d=HD)
        erow = con[:, C_EROW:C_TRI]
        tri = con[:, C_TRI:C_TRASH].rearrange("p (a b) -> p a b", b=GROUPS)
        trash = con[:, C_TRASH:NCONST].rearrange("p (t j) -> p t j", j=TOPK)

        s_mod_in = sem("s_mod_in")
        s_rows_in = [sem(f"s_rows_in{k}") for k in range(2)]
        s_small = sem("s_small")
        s_x = [sem(f"s_x{b}") for b in range(B)]
        s_slot_init = sem("s_slot_init")
        s_init = sem("s_init")
        s_weights = sem("s_weights")
        s_h2_out = [sem(f"s_h2_out{p}") for p in range(2)]
        s_wts, s_wts_out = sem("s_wts"), sem("s_wts_out")
        s_slot = sem("s_slot")
        s_slots_in = sem("s_slots_in")
        s_sh_w = sem("s_sh_w")
        s_wu = [sem(f"s_wu{p}") for p in range(2)]
        s_wd = [sem(f"s_wd{p}") for p in range(2)]
        s_xg = [sem(f"s_xg{p}") for p in range(2)]
        s_eg = [sem(f"s_eg{p}") for p in range(2)]
        s_added = sem("s_added")
        s_fin_in = [sem(f"s_fin_in{c}") for c in range(NT // TPC)]
        s_out = sem("s_out")
        s_silu, s_mod, s_modv, s_ready = (sem(n) for n in ("s_silu", "s_mod", "s_modv", "s_ready"))
        s_zero = sem("s_zero")
        s_rows, s_rows_out, s_gates = sem("s_rows"), sem("s_rows_out"), sem("s_gates")
        (s_var, s_rstd, s_xn, s_xT, s_hT, s_q, s_qk, s_square, s_rope, s_ms, s_rr, s_parts, s_pack, s_packT, s_mm,
         s_max, s_nmax, s_st, s_qT) = (sem("s_" + n) for n in (
             "var", "rstd", "xn", "xT", "hT", "q", "qk", "square", "rope", "ms", "rr", "parts", "pack", "packT", "mm",
             "max", "nmax", "st", "qT"))
        s_sc, s_exp, s_mask, s_pv, s_on, s_sq = (sem("s_" + n) for n in ("sc", "exp", "mask", "pv", "on", "sq"))
        (s_oss, s_oms, s_orstd, s_at, s_atd, s_var2, s_rstd2, s_h2, s_h2t, s_h2T, s_lg, s_ex, s_sel, s_pos,
         s_pay) = (sem("s_" + n) for n in (
             "oss", "oms", "orstd", "at", "atd", "var2", "rstd2", "h2", "h2t", "h2T", "lg", "ex", "sel", "pos",
             "pay"))
        s_T, s_xa, s_xd, s_gu, s_act, s_hidden, s_hh, s_hid, s_dn, s_ya, s_yd = (sem("s_e" + n) for n in (
            "T", "xa", "xd", "gu", "act", "hidden", "hh", "hid", "dn", "ya", "yd"))
        s_guh, s_gul, s_dh, s_dl, s_dp, s_shh, s_shl = (sem("s_" + n) for n in (
            "guh", "gul", "dh", "dl", "dp", "shh", "shl"))
        s_from, s_to, s_fin = sem("s_from"), sem("s_to"), sem("s_fin")
        s_ot = sem("s_ot")
        s_yfree = sem("s_yfree")
        s_step = sem("s_step")

        def hold(eng, semaphore, value):
            eng.wait_ge(semaphore, value)
            eng.sem_inc(s_step, 1)

        def xtile(t):
            return xres[:, ds(t, 1), :].rearrange("p a n -> p (a n)")

        def rows(b, tile):
            return tile[:, ds(b, 1), :].rearrange("p a n -> p (a n)")

        BESIDE = (TPC, TPC + 1)
        KEYS = NG * TPC
        MAXES = [sum(2 * H if j in BESIDE else H for j in range(i)) for i in range(TPB + 1)]

        def unit_of(b, qc, g, kt, pr):
            return b * UNITS_B + qc * (NG * 2 * TPC) + g * (2 * TPC * (qc + 1)) + (2 * kt + pr)

        def stack_bank(i, q4):
            return 7 - q4 % 2 if i in BESIDE else 5 + 2 * (q4 % 2)

        EARLY, LATER = (1, 2, 3, 4, 7), (0, 1, 2, 3, 6)

        def kv_bank(i):
            return 5 if i < 2 else 7

        def beside(i, slot):
            return (i - TPC) * (H // 2) + slot // 2

        DIVIDE_STEPS = TPC + 2
        SQUARED = BESIDE[1] + 1

        def divided_from(g):
            return 2 * ((g + 1) * TPC + 2)

        AT_PROJECT, AT_TURN, AT_LOGITS = 1, 5, 7
        OUT_BANKS = (4, 6, 2, 3)
        STORED = (TPC + TPC // 2, TPC // 2)
        SLOTTED = 16 * TPB * TOPK

        block = ctx.enter_context(nc.Block())

        @block.sync
        def _(sp):
            sp.dma_start(ct_s[:, :, :], c_t).then_inc(s_mod_in, 16)
            wv = wmod.rearrange("(c p) n -> p c n", p=P)
            xv = x.rearrange("(t p) n -> p t n", p=P)
            sp.dma_start(wmod_s[:, :, 0:2 * D], wv[:, :, 0:2 * D]).then_inc(s_mod_in, 16)
            def load_x(c):
                sp.dma_start(xres[:, TPC * c:TPC * c + TPC, :], xv[:, TPC * c:TPC * c + TPC, :])\
                  .then_inc(s_x[c * TPC // TPB], 16)

            for c in range(TPB // TPC):
                load_x(c)
            sp.wait_ge(s_weights, 64)
            sp.dma_start(slot_dram[0:NSLOT, :].rearrange("(p s) c -> p (s c)", p=P), slot_init).then_inc(s_slot_init, 16)
            for c in range(TPB // TPC, NT // TPC):
                load_x(c)
            for k in range(2):
                cols = slice((2 + 2 * k) * D, (4 + 2 * k) * D)
                sp.dma_start(wmod_s[:, :, cols], wv[:, :, cols]).then_inc(s_rows_in[k], 16)
            sp.wait_ge(s_rows, 1)
            sp.dma_start(rows_dram, mod_rows[:, :, :].rearrange("b n d -> b (n d)")).then_inc(s_rows_out, 16)
            sp.wait_ge(s_rows_out, 16)
            for b in range(B):
                sp.dma_start(mods[:, :, b, :], rows_dram[b, :].rearrange("(n d) -> n d", d=D).unsqueeze(0)
                             .to_broadcast([P, 4, D])).then_inc(s_gates, 16)
            sp.wait_ge(s_zero, 1)
            zeros = h2[:, :, :].rearrange("p a n -> p (a n)")
            sp.dma_start(h2_dram[NTOK:NTOK + EXTRA, :].rearrange("(t p) n -> p t n", p=P),
                         zeros[:, 0:D + E].unsqueeze(1).to_broadcast([P, EXTRA // P, D + E])).then_inc(s_init, 16)
            sp.dma_start(acc_dram.rearrange("(t p) n -> p t n", p=P),
                         zeros[:, 0:D].unsqueeze(1).to_broadcast([P, (NTOK + EXTRA) // P, D])).then_inc(s_init, 16)
            with sp.Fori(0, B) as b:
                with sp.Fori(0, TPC) as ii:
                    t = b * TPB + ii
                    sp.wait_ge(s_h2, t + 1)
                    sp.dma_start(h2_dram[ds(t * P, P), 0:D], h2[:, 0, :]).then_inc(s_h2_out[0], 16)
                for ii in range(TPC):
                    t = b * TPB + (TPC + ii)
                    sp.wait_ge(s_h2, t + 1)
                    sp.dma_start(h2_dram[ds(t * P, P), 0:D], h2[:, ii % 2, :]).then_inc(s_h2_out[ii % 2], 16)
                sp.wait_ge(s_wts, b + 1)
                sp.dma_start(h2_dram[ds(b * S, S), D:D + E].rearrange("(t p) e -> p t e", p=P), wts[:, :, :])\
                  .then_inc(s_wts_out, 16)
            sp.wait_ge(s_lg, NT)
            sp.dma_start(sh_gu[:, :, :], sh_gate_up).then_inc(s_sh_w, 16)
            sp.dma_start(sh_d[:, 0, :], sh_down[0:IA, :]).then_inc(s_sh_w, 16)
            sp.dma_start(sh_d[0:IB, 1, :], sh_down[IA:EI, :]).then_inc(s_sh_w, 16)

            def load_up(e, p):
                sp.dma_start(e_gu[p][:, :, :], gate_up[ds(e, 1), :, :, :].rearrange("a p c n -> p (a c) n"))\
                  .then_inc(s_wu[p], 16)

            def load_down(e, p):
                sp.dma_start(e_d[p][:, 0, :], w_down[ds(e, 1), 0:IA, :].rearrange("a i n -> (a i) n"))\
                  .then_inc(s_wd[p], 16)
                sp.dma_start(e_d[p][0:IB, 1, :], w_down[ds(e, 1), IA:EI, :].rearrange("a i n -> (a i) n"))\
                  .then_inc(s_wd[p], 16)

            for p in range(2):
                sp.wait_ge(s_h2_out[p], 16 * B * STORED[p])
            with sp.Fori(0, NSH // 2) as i:
                for p in range(2):
                    n = i * 2 + p
                    sp.wait_ge(s_T, n + 1)
                    for h in range(HALVES):
                        sp.dma_start(xg[p][:, h, 0:D], h2_dram[ds(n * CAP + h * P, P), 0:D]).then_inc(s_xg[p], 16)
            sp.wait_ge(s_pay, B + 1)
            for p in range(2):
                load_up(p, p)
                load_down(p, p)
            with sp.Fori(0, E // 2 - 1) as i:
                for p in range(2):
                    e = i * 2 + p
                    sp.wait_ge(s_gul, e + 1)
                    load_up(e + 2, p)
                    sp.wait_ge(s_dl, e + 1)
                    sp.wait_ge(s_dp, e + 1)
                    load_down(e + 2, p)
            sp.wait_ge(s_added, 16 * HALVES * E)
            av = acc_dram[0:NTOK, :].rearrange("(t p) n -> p t n", p=P)
            for c in range(NT // TPC):
                sp.dma_start(fin_acc[:, c, :, :], av[:, TPC * c:TPC * c + TPC, :]).then_inc(s_fin_in[c], 16)
            sp.wait_ge(s_out, 16 * (NT // TPC))

        @block.gpsimd
        def _(pool):
            def inv_sqrt(dst, src, n):
                return pool.tensor_tensor(dst, src, mhalf[:, 0:n], ALU.pow)

            def fill_slots(ii):
                for j in range(TOPK):
                    pool.indirect_dma_start(
                        out=slot_dram, out_offset=bass.IndirectOffsetOnAxis(ap=idx8[:, ii, j:j + 1], axis=0),
                        in_=pay[:, ii:ii + 1], in_offset=None).then_inc(s_slot, 16)

            pool.memset(h2[:, :, :], 0.0).then_inc(s_zero, 1)
            for b in range(B):
                tiles = slice(b * TPB, (b + 1) * TPB)
                pool.wait_ge(s_var, b + 1)
                inv_sqrt(rstd[:, tiles], ve[:, tiles], TPB).then_inc(s_rstd, 1)
            pool.wait_ge(s_slot_init, 16)
            def head_rms(b, i):
                hold(pool, s_ms, b * TPB + (i + 1))
                inv_sqrt(rr[:, :], ms[:, :], H + 1).then_inc(s_rr, 1)

            def tile_rstd(t, slot):
                hold(pool, s_var2, t + 1)
                inv_sqrt(rstd2[:, slot:slot + 1], ve2[:, slot:slot + 1], 1).then_inc(s_rstd2, 1)

            def causal(b, qc, g, kt):
                hold(pool, s_exp, unit_of(b, qc, g, kt, 0) + 4)
                dd = kt - TPC * qc
                tile = probs[:, kt % 2, :, dd * P:dd * P + P]
                pool.affine_select(out=tile, in_=tile, compare_op=ALU.is_ge, fill=0.0, base=0,
                                   pattern=[[0, GH], [1, P]], channel_multiplier=-1).then_inc(s_mask, 1)

            def row_rms(b, qc):
                hold(pool, s_oms, b * QC + (qc + 1))
                inv_sqrt(orstd[:, qc, :], oms[:, :], TPC).then_inc(s_orstd, 1)

            with pool.Fori(0, B) as b:
                head_rms(b, 0)
                hold(pool, s_pay, b + 1)
                for i in range(TPB):
                    if i + 1 < TPB:
                        head_rms(b, i + 1)
                    if i in BESIDE:
                        for k in range(beside(i, 0), beside(i, H)):
                            causal(b, 0, k // TPC, k % TPC)
                    if i == SQUARED:
                        row_rms(b, 0)
                    fill_slots(i)
                hold(pool, s_pack, (b + 1) * TPB)
                with pool.Fori(0, NG) as g:
                    hold(pool, s_at, b * TPB + g)
                    pool.tensor_copy(o_tile[:, :, :], oT[:, 0, :, ds(g * P, P)]).then_inc(s_ot, 1)
                    tile_rstd(b * TPB + g, 0)
                    for kt in range(TPC, 2 * TPC):
                        causal(b, 1, g, kt)
                row_rms(b, 1)
                for ii in range(TPC):
                    tile_rstd(b * TPB + (TPC + ii), ii % 2)
            pool.wait_ge(s_pay, B + 1)
            for i in range(TPB):
                fill_slots(i)
            pool.wait_ge(s_slot, SLOTTED * (B + 1))
            for p in range(2):
                pool.wait_ge(s_h2_out[p], 16 * B * STORED[p])
            pool.dma_start(slots[:, :], slot_dram[0:NSLOT, :].rearrange("(p s) c -> p (s c)", p=P))\
                .then_inc(s_slots_in, 16)
            pool.wait_ge(s_slots_in, 16)
            pool.wait_ge(s_wts_out, 16 * B)
            pool.wait_ge(s_init, 32)

            def gather(e, q):
                hold(pool, s_xd, e + (NSH - 1))
                pool.tensor_copy(from_ix[q][:, :], slots[:, ds(e * HALVES, HALVES)]).then_inc(s_from, 1)
                hold(pool, s_from, e + 1)
                for h in range(HALVES):
                    pool.indirect_dma_start(
                        out=xg[q % 2][:, h, :], out_offset=None, in_=h2_dram,
                        in_offset=bass.IndirectOffsetOnAxis(ap=from_ix[q][:, h:h + 1], axis=0)).then_inc(s_eg[q % 2], 16)

            def down_lo(e, p):
                hold(pool, s_dh, e + 1)
                pool.tensor_tensor(e_d_lo[p][:, :], e_d[p][:, 0, :], e_d_hi[p][0:IA, 0, :].bitcast(f32), ALU.subtract)\
                    .then_inc(s_dp, 1)

            def add_rows(e, q):
                pool.tensor_copy(to_ix[q][:, :], slots[:, ds(e * HALVES, HALVES)]).then_inc(s_to, 1)
                hold(pool, s_to, e + 1)
                hold(pool, s_ya, e + NSH + 1)
                hold(pool, s_yd, e + NSH + 1)
                pool.wait_ge(s_added, e * (16 * HALVES))
                pool.sem_inc(s_yfree, 1)
                for h in range(HALVES):
                    pool.indirect_dma_start(
                        out=acc_dram, out_offset=bass.IndirectOffsetOnAxis(ap=to_ix[q][:, h:h + 1], axis=0),
                        in_=y[q % 2][:, h, :], in_offset=None, compute_op=ALU.add).then_inc(s_added, 16)

            gather(0, 0)
            gather(1, 1)
            gather(2, 2)
            down_lo(0, 0)
            with pool.Fori(0, E // 4 - 1) as i:
                for q in range(4):
                    gather(i * 4 + (q + 3), (q + 3) % 4)
                    down_lo(i * 4 + (q + 1), (q + 1) % 2)
                    add_rows(i * 4 + q, q)
            for q in range(4):
                e = E - 4 + q
                if q < 1:
                    gather(e + 3, q + 3)
                if q < 3:
                    down_lo(e + 1, (q + 1) % 2)
                add_rows(e, q)

        @block.scalar
        def _(act):
            act.dma_start(con[:, :], consts).then_inc(s_small, 16)
            act.dma_start(mask_s[:, :], masks).then_inc(s_small, 16)
            act.dma_start(wpre[:, :], w_pre).then_inc(s_small, 16)
            act.dma_start(tokid[:, :], tokids).then_inc(s_small, 16)
            act.dma_start(ebias[:, :], e_bias.unsqueeze(0).to_broadcast([P, E])).then_inc(s_small, 16)
            act.dma_start(wqn_s[:, :], w_qn.unsqueeze(0).to_broadcast([P, HD])).then_inc(s_small, 16)
            act.dma_start(wkn_s[:, :], w_kn.unsqueeze(0).to_broadcast([P, HD])).then_inc(s_small, 16)
            act.dma_start(wq[:, :, :], wq_t).then_inc(s_weights, 16)
            act.dma_start(wkv[:, :, :], wkv_t).then_inc(s_weights, 16)
            act.dma_start(wo[:, :, :], wo_t).then_inc(s_weights, 16)
            act.dma_start(rw[:, :, :], router_t).then_inc(s_weights, 16)
            act.wait_ge(s_mod_in, 32)
            act.activation(silu_c[:, :, :], ct_s[:, :, :], ACT.Silu).then_inc(s_silu, 1)

            def modulate(b, i):
                t = b * TPB + i
                hold(act, s_xT, t + 1)
                hold(act, s_q, b * TPB + max(i - 1, 0))
                for cc in range(KC):
                    last = act.activation(hT[:, i % 2, cc, :], ps[:, 6, cc * P:(cc + 1) * P], ACT.Identity,
                                          bias=mcol[:, 0, cc, ds(b, 1)], scale=mcol[:, 1, cc, ds(b, 1)])
                last.then_inc(s_hT, 1)

            def project(b, i):
                t = b * TPB + i
                hold(act, s_rope, t)
                hold(act, s_on, b * (QC * NG))
                act.wait_ge(s_q, t + 1)
                act.activation(qk[:, 0:H, :], ps[:, 6 if i - 2 in BESIDE else 4, :].rearrange("p (h d) -> p h d", d=HD), ACT.Copy)
                act.activation(qk[:, H, :], ps[:, kv_bank(i), 0:HD], ACT.Copy)
                act.activation(v_sb[:, i, :], ps[:, kv_bank(i), HD:2 * HD], ACT.Copy).then_inc(s_qk, 1)
                act.wait_ge(s_qk, t + 1)
                act.activation(sq[:, :, :], qk[:, :, :], ACT.Square).then_inc(s_square, 1)

            def pack(b, i):
                t = b * TPB + i
                act.wait_ge(s_pack, t + 1)
                act.activation(qpT[:, :, :], ps[:, 6 if i in BESIDE else 5, :].rearrange("p (g t) -> p g t", t=P), ACT.Copy)
                act.activation(kT[:, i * P:i * P + P], ps[:, 7, 0:P], ACT.Copy)
                for j in range(GH):
                    r = slice(HD * j, HD * j + HD)
                    last = act.activation(kpad[r, j, i * P:i * P + P], ps[r, 7, P:2 * P], ACT.Copy)
                last.then_inc(s_packT, 1)

            def stack(b, i):
                ii = i % TPC
                for q4 in range(NG):
                    act.wait_ge(s_st, (b * TPB + i) * NG + q4 + 1)
                    act.activation(qT[:, GH * q4:GH * q4 + GH, ii * P:ii * P + P],
                                   ps[:, stack_bank(i, q4), :].rearrange("p (g t) -> p g t", t=P), ACT.Copy)\
                       .then_inc(s_qT, 1)

            act.wait_ge(s_modv, 1)
            act.sem_inc(s_exp, 2)
            def copy_out(b, qc, g):
                before = b * (QC * NG) + qc * NG + g
                hold(act, s_sq, before)
                if qc:
                    hold(act, s_var2, b * TPB + (g + 1))
                hold(act, s_pv, b * PVS_B + qc * (NG * TPC) + g * (TPC * (qc + 1)) + (TPC * (qc + 1) + 2))
                act.activation(oT[:, qc, ds(g, 1), :].rearrange("p a n -> p (a n)"), ps[:, 4, :], ACT.Copy)
                act.activation(scratch[:, :], ps[:, 5, :], ACT.Copy).then_inc(s_on, 1)

            def exponentials_of(b, qc, g, kt, buffers):
                off = max(0, kt - TPC * qc) * P
                pv = b * PVS_B + qc * (NG * TPC) + g * (TPC * (qc + 1)) + kt
                hold(act, s_pv, pv + 1)
                for pr in range(2):
                    if pr and qc == 0 and kt == 1 and g:
                        copy_out(b, 0, g - 1)
                    hold(act, s_sc, unit_of(b, qc, g, kt, pr) + 1)
                    act.activation(probs[:, kt % 2, 2 * pr:2 * pr + 2, off:CH],
                                   pair(buffers[pr])[:, :, off:CH], ACT.Exp).then_inc(s_exp, 1)

            def exponentials(b, qc):
                with act.Fori(0, NG) as g:
                    for kt in range(TPC * (qc + 1)):
                        exponentials_of(b, qc, g, kt, (0, 1))
                        if kt == AT_TURN + 1:
                            rows_T(b * TPB + g, 6, 0, b * TPB + g)
                    copy_out(b, qc, g)

            def rows_T(t, bank, slot, routed):
                hold(act, s_lg, routed)
                act.wait_ge(s_h2t, t + 1)
                act.activation(h2T[:, slot, :, :], ps[:, bank, :].rearrange("p (c t) -> p c t", t=P), ACT.Copy)\
                   .then_inc(s_h2T, 1)

            def begin(b):
                modulate(b, 0)
                modulate(b, 1)
                project(b, 0)

            def batch(b, followed):
                project(b, 1)
                modulate(b, 2)
                for i in range(TPB):
                    pack(b, i)
                    if i == 1:
                        act.wait_ge(s_rows_out, 16)
                        hold(act, s_wts_out, b * 16)
                    if i - 1 in LATER:
                        stack(b, i - 1)
                    if i in BESIDE:
                        for k in range(beside(i, 0), beside(i, H)):
                            exponentials_of(b, 0, k // TPC, k % TPC, (0, 0))
                    if i + 2 < TPB:
                        project(b, i + 2)
                    if i + 3 < TPB:
                        modulate(b, i + 3)
                    if i == BESIDE[1]:
                        stack(b, i - 1)
                        copy_out(b, 0, NG - 1)
                    if i != BESIDE[0] and i not in LATER:
                        stack(b, i)
                exponentials(b, 1)
                for ii in range(TPC):
                    rows_T(b * TPB + (TPC + ii), ii % 2, ii % 2, b * TPB + (TPC + max(ii - 1, 0)))
                hold(act, s_lg, (b + 1) * TPB)
                act.activation(ex[:, :, :], ps[:, 7, :].rearrange("p (t e) -> p t e", e=E), ACT.Exp,
                               scale=-1.0).then_inc(s_ex, 1)
                if followed:
                    begin(b + 1)

            begin(0)
            with act.Fori(0, B - 1) as b:
                batch(b, True)
            batch(B - 1, False)

            flat = "p a n -> p (a n)"

            def rows_hi(n, p):
                hold(act, s_gu, n + 1)
                act.wait_ge(s_T, n + 3)
                act.activation(x_hi[p][:, :, :].rearrange(flat), pair(0).rearrange(flat), ACT.Copy).then_inc(s_xa, 1)

            def gates(n, p):
                hold(act, s_hidden, n + 1)
                act.wait_ge(s_gu, n + 3)
                act.activation(gact_a[p][:, :], ps[0:IA, 2 + p, 0:CAP], ACT.Silu)
                act.activation(gact_b[p][:, :], ps[0:IB, 4 + p, 0:CAP], ACT.Silu).then_inc(s_act, 1)

            def hidden_hi(n, p):
                hold(act, s_dn, n + 1)
                act.wait_ge(s_hidden, n + 3)
                act.activation(hid_hi[p][0:IA, 0, :], hid[:, 0, :], ACT.Copy)
                for r in range(2):
                    last = act.activation(hid_hi[p][r * IB:(r + 1) * IB, 1, :], hid[0:IB, 1, :], ACT.Copy)
                last.then_inc(s_hh, 1)

            def split_down(hi, whole):
                act.activation(hi[0:IA, 0, :], whole[:, 0, :], ACT.Copy)
                return act.activation(hi[0:IB, 1, :], whole[0:IB, 1, :], ACT.Copy)

            def up_hi(e, p, loads):
                hold(act, s_gu, e + (NSH + 1))
                hold(act, s_wu[p], loads * 16)
                act.activation(e_gu_hi[p][:, :, :].rearrange(flat), e_gu[p][:, :, :].rearrange(flat), ACT.Copy)\
                   .then_inc(s_guh, 1)

            def down_hi(e, p, loads):
                hold(act, s_dn, e + (NSH + 1))
                hold(act, s_wd[p], loads * 32)
                split_down(e_d_hi[p], e_d[p]).then_inc(s_dh, 1)

            act.wait_ge(s_sh_w, 48)
            act.activation(sh_gu_hi[:, :, :].rearrange(flat), sh_gu[:, :, :].rearrange(flat), ACT.Copy)
            rows_hi(0, 0)
            split_down(sh_d_hi, sh_d).then_inc(s_shh, 1)
            gates(0, 0)
            rows_hi(1, 1)
            hidden_hi(0, 0)

            def step(n, p):
                gates(n + 1, 1 - p)
                rows_hi(n + 2, p)
                hidden_hi(n + 1, 1 - p)

            with act.Fori(0, NSH // 2 - 1) as i:
                for p in range(2):
                    step(i * 2 + p, p)
            up_hi(0, 0, 1)
            step(NSH - 2, 0)
            up_hi(1, 1, 1)
            down_hi(0, 0, 1)
            step(NSH - 1, 1)

            def weighted(e, p):
                hold(act, s_yfree, e)
                hold(act, s_dn, e + NSH + 3)
                act.activation(y[p][:, 0, :], ps[:, 6, :], ACT.Copy,
                               scale=weight[:, ds(e * HALVES, 1)]).then_inc(s_ya, 1)

            with act.Fori(0, E // 2 - 1) as i:
                for p in range(2):
                    e = i * 2 + p
                    up_hi(e + 2, p, i + 2)
                    down_hi(e + 1, 1 - p, i + (1 + p))
                    step(e + NSH, p)
                    weighted(e, p)
            down_hi(E - 1, 1, E // 2)
            gates(E + NSH - 1, 1)
            hidden_hi(E + NSH - 1, 1)
            for p in range(2):
                weighted(E - 2 + p, p)
            ov = out.rearrange("(t p) n -> p t n", p=P)
            for c in range(NT // TPC):
                act.wait_ge(s_fin, c + 1)
                act.dma_start(ov[:, TPC * c:TPC * c + TPC, :], xres[:, TPC * c:TPC * c + TPC, :]).then_inc(s_out, 16)

        @block.tensor
        def _(pe):
            pe.wait_ge(s_silu, 1)
            for m in range(2):
                for cc in range(KC):
                    for k in range(KC):
                        col = (m * KC + cc) * B
                        last = pe.matmul(ps[:, 0, col:col + B], wmod_s[:, k, m * D + cc * P:m * D + (cc + 1) * P],
                                         silu_c[:, k, :], start=(k == 0), stop=(k == KC - 1))
            last.then_inc(s_mod, 1)
            pe.wait_ge(s_small, 112)
            pe.wait_ge(s_weights, 64)
            pe.wait_ge(s_ready, 1)
            pe.sem_inc(s_pv, 2)

            def turn_x(b, i):
                t = b * TPB + i
                pe.wait_ge(s_hT, t)
                pe.wait_ge(s_xn, t + 1)
                for cc in range(KC):
                    last = pe.transpose(ps[:, 6, cc * P:(cc + 1) * P], xn[:, i % 2, cc * P:(cc + 1) * P], ident)
                last.then_inc(s_xT, 1)

            def project(b, i, step):
                t = b * TPB + i
                cc = step % KC
                if step == 0:
                    pe.wait_ge(s_hT, t + 1)
                if step == KC and i - 3 in LATER:
                    pe.wait_ge(s_qT, (t - 2) * NG)
                if step < KC:
                    pe.matmul(ps[:, 6 if i - 2 in BESIDE else 4, :], hT[:, i % 2, cc, :], wq[:, cc, :], start=(cc == 0), stop=(cc == KC - 1))
                else:
                    last = pe.matmul(ps[:, kv_bank(i), 0:2 * HD], hT[:, i % 2, cc, :], wkv[:, cc, :],
                                     start=(cc == 0), stop=(cc == KC - 1))
                    if step == 2 * KC - 1:
                        last.then_inc(s_q, 1)

            def pack(b, i):
                t = b * TPB + i
                pe.wait_ge(s_parts, t + 1)
                pe.wait_ge(s_qk, t + min(2, TPB - i))
                pe.wait_ge(s_qT, (t - 1 if i == BESIDE[1] or i - 1 in LATER else t) * NG)
                if i in BESIDE:
                    pe.wait_ge(s_hT, t + 3)
                pe.transpose(ps[:, 7, 0:P], ks[:, :], ident)
                pe.transpose(ps[:, 7, P:2 * P], kh4[:, :, :].rearrange("p j d -> p (j d)"), ident)
                for g in range(NG):
                    last = pe.transpose(ps[:, 6 if i in BESIDE else 5, g * P:(g + 1) * P],
                                        qh[:, GH * g:GH * g + GH, :].rearrange("p j d -> p (j d)"), ident)
                last.then_inc(s_pack, 1)

            def row_max(b, i):
                t = b * TPB + i
                pe.wait_ge(s_packT, t + 1)
                width = (i + 1) * P
                step = 2 if width <= 512 else 1
                reduced = b * MAXES[TPB] + MAXES[i]
                if i == 0:
                    pe.wait_ge(s_ready, 2)
                if i == BESIDE[0]:
                    stack(b, i - 1)
                for h in range(H):
                    query, heads_k = qpT[:, h // GH, :], kpad[:, h % GH, :]
                    if i in BESIDE:
                        if h % 2:
                            project(b, i + 2, h // 2)
                        pe.wait_ge(s_max, reduced + max(2 * h - 1, 0))
                        pe.matmul(ps[:, 2, :], query, heads_k[:, 0:512], start=True, stop=True).then_inc(s_mm, 1)
                        pe.wait_ge(s_max, reduced + 2 * h)
                        pe.matmul(ps[:, 3, 0:width - 512], query, heads_k[:, 512:width], start=True, stop=False)
                        last = ps[:, 3, width - P - 512:width - 512]
                    else:
                        buf = h // step
                        if h % step == 0:
                            pe.wait_ge(s_max, reduced + max(buf - 1, 0) * step)
                        flat = pair(buf % 2).rearrange("p a n -> p (a n)")
                        at = (h % step) * 512
                        for lo in range(0, width, 512):
                            hi = min(lo + 512, width)
                            pe.matmul(flat[:, at + lo:at + hi], query, heads_k[:, lo:hi], start=True, stop=(hi < width))
                        last = flat[:, at + width - P:at + width]
                    pe.matmul(last, ident_b[:, :], bias_b[:, :], start=False, stop=True).then_inc(s_mm, 1)
                    if i in BESIDE:
                        k = beside(i, h)
                        scores(b, 0, k // TPC, k % TPC, h % 2, 0, 2)
                        behind = k - 2 + h % 2
                        if behind >= 0:
                            (values if h % 2 else sums)(b, 0, behind // TPC, behind % TPC)
                    elif h == 11 and i + 3 < TPB:
                        for step_ahead in range(2 * KC):
                            project(b, i + 2, step_ahead)
                        turn_x(b, i + 3)
                    if h == 3 and i - 1 in LATER and i not in BESIDE:
                        stack(b, i - 1)

            def stack(b, i):
                t = b * TPB + i
                pe.wait_ge(s_nmax, t + 1)
                if i < TPB - 2:
                    pe.wait_ge(s_qk, t + (4 if i == BESIDE[0] else 3))
                if i == BESIDE[0]:
                    pe.wait_ge(s_hT, t + 4)
                if i == BESIDE[1] or i - 1 in LATER:
                    pe.wait_ge(s_qT, t * NG)
                for q4 in range(NG):
                    if q4 >= 2:
                        pe.wait_ge(s_qT, t * NG + (q4 - 1))
                    for j in range(GH):
                        last = pe.transpose(ps[:, stack_bank(i, q4), j * P:(j + 1) * P], qs[:, i % 2, GH * q4 + j, :], ident)
                    last.then_inc(s_st, 1)

            def scores(b, qc, g, kt, pr, buffer, free):
                off = max(0, kt - TPC * qc) * P
                hold(pe, s_exp, unit_of(b, qc, g, kt, pr) + free)
                for jj in range(2):
                    last = pe.matmul(ps[:, 2 * buffer + jj, off:CH], kT[:, kt * P:kt * P + P],
                                     qT[:, ds(g * GH + (2 * pr + jj), 1), off:CH], start=True, stop=True)
                last.then_inc(s_sc, 1)

            def accumulate(qc, kt, bank, left):
                off = max(0, kt - TPC * qc) * P
                for j in range(GH):
                    last = pe.matmul(ps[HD * j:HD * j + HD, bank, off:CH], left, probs[:, kt % 2, j, off:CH],
                                     start=(kt == 0), stop=(kt == TPC * (qc + 1) - 1))
                return last

            def values(b, qc, g, kt):
                if kt == 0:
                    pe.wait_ge(s_on, b * (QC * NG) + qc * NG + g)
                if kt >= TPC * qc:
                    pe.wait_ge(s_mask, b * (QC * NG * TPC) + qc * (NG * TPC) + g * TPC + (kt - TPC * qc + 1))
                else:
                    pe.wait_ge(s_exp, unit_of(b, qc, g, kt, 0) + 4)
                accumulate(qc, kt, 4, v_sb[:, kt, :])

            def sums(b, qc, g, kt):
                accumulate(qc, kt, 5, ones[:, :]).then_inc(s_pv, 1)

            def attend(b):
                kts = 2 * TPC
                hold(pe, s_qT, (b + 1) * (TPB * NG))
                with pe.Fori(0, NG) as g:
                    for kt in range(kts):
                        for pr in range(2):
                            scores(b, 1, g, kt, pr, pr, 1)
                        if kt:
                            values(b, 1, g, kt - 1)
                            sums(b, 1, g, kt - 1)
                        if kt == AT_PROJECT:
                            pe.wait_ge(s_ot, b * NG + (g + 1))
                            out_project(o_tile, 6)
                        if kt == AT_TURN:
                            turn(b * TPB + g, 6, 0)
                        if kt == AT_LOGITS:
                            logits(b * TPB + g, g, 0)
                    values(b, 1, g, kts - 1)
                    sums(b, 1, g, kts - 1)

            def square_sums(b, qc):
                pe.wait_ge(s_sq, b * (QC * NG) + (qc + 1) * NG)
                for ii in range(TPC):
                    last = pe.matmul(ps[:, 4 + qc, ii:ii + 1], osq[:, ii * P:ii * P + P], ones[:, 0:1],
                                     start=True, stop=True)
                last.then_inc(s_oss, 1)

            def out_project(rows_t, bank):
                for g in range(NG):
                    last = pe.matmul(ps[:, bank, :], rows_t[:, g, :], wo[:, g, :], start=(g == 0), stop=(g == NG - 1))
                last.then_inc(s_at, 1)

            def turn(t, bank, slot):
                pe.wait_ge(s_h2, t + 1)
                for cc in range(KC):
                    last = pe.transpose(ps[:, bank, cc * P:(cc + 1) * P], h2[:, slot, cc * P:(cc + 1) * P], ident)
                last.then_inc(s_h2t, 1)

            def logits(t, i, slot):
                pe.wait_ge(s_h2T, t + 1)
                for cc in range(KC):
                    last = pe.matmul(ps[:, 7, ds(i * E, E)], h2T[:, slot, cc, :], rw[:, cc, :],
                                     start=(cc == 0), stop=(cc == KC - 1))
                last.then_inc(s_lg, 1)

            def finish_chunk(b):
                for ii in range(TPC):
                    out_project(oT[:, 1, :, ii * P:ii * P + P], OUT_BANKS[ii])
                for ii in range(TPC):
                    turn(b * TPB + (TPC + ii), ii % 2, ii % 2)
                    if ii:
                        logits(b * TPB + (TPC + ii - 1), TPC + ii - 1, (ii - 1) % 2)
                logits(b * TPB + (TPB - 1), TPB - 1, 1)

            def count(b):
                pe.wait_ge(s_sel, b + 1)
                for i in range(TPB):
                    dst = ps[:, 7, i * E:(i + 1) * E]
                    pe.matmul(dst, ones_b[:, :], seen_b[:, :], start=True, stop=False)
                    for before in range(i):
                        pe.matmul(dst, ones_b[:, :], sel_b[:, before, :], start=False, stop=False)
                    last = pe.matmul(dst, upper_b[:, :], sel_b[:, i, :], start=False, stop=True)
                last.then_inc(s_pos, 1)

            def begin(b):
                turn_x(b, 0)
                turn_x(b, 1)
                for step in range(2 * KC):
                    project(b, 0, step)

            def batch(b, followed):
                pe.wait_ge(s_qk, b * TPB + 1)
                for step in range(2 * KC):
                    project(b, 1, step)
                turn_x(b, 2)
                pe.wait_ge(s_pay, b + 1)
                for i in range(TPB):
                    pack(b, i)
                    row_max(b, i)
                    if i == BESIDE[0]:
                        pe.wait_ge(s_qk, b * TPB + (i + 3))
                        turn_x(b, i + 3)
                    if i == BESIDE[1]:
                        sums(b, 0, NG - 1, TPC - 2)
                        values(b, 0, NG - 1, TPC - 1)
                        sums(b, 0, NG - 1, TPC - 1)
                        stack(b, i - 1)
                    if i != BESIDE[0] and i not in LATER:
                        stack(b, i)
                    if i == SQUARED:
                        square_sums(b, 0)
                pe.wait_ge(s_oms, b * QC + 1)
                attend(b)
                square_sums(b, 1)
                finish_chunk(b)
                if followed:
                    begin(b + 1)
                count(b)

            begin(0)
            for n, m in enumerate((2, 3, 4, 5)):
                pe.wait_ge(s_rows_in[n // 2], 16)
                for k in range(KC):
                    last = pe.matmul(ps[0:B, n, :], silu_c[:, k, :], wmod_s[:, k, m * D:(m + 1) * D],
                                     start=(k == 0), stop=(k == KC - 1))
                last.then_inc(s_mod, 1)
            with pe.Fori(0, B - 1) as b:
                batch(b, True)
            batch(B - 1, False)

            pe.sem_inc(s_T, 2)
            pe.sem_inc(s_gu, 2)
            pe.sem_inc(s_dn, 2)

            def turn_rows(n, p, arrived, loads):
                pe.wait_ge(s_xa, n)
                pe.wait_ge(s_xd, n)
                pe.wait_ge(arrived[p], loads * 32)
                for cc in range(KC):
                    for h in range(HALVES):
                        col = (cc % 2) * CAP + h * P
                        last = pe.transpose(ps[:, cc // 2, col:col + P], xg[p][:, h, cc * P:(cc + 1) * P], ident)
                last.then_inc(s_T, 1)

            def up(n, p, w_hi, w_lo):
                pe.wait_ge(s_hidden, n + 1)
                pe.wait_ge(s_xa, n + 1)
                both = (ps[:, 4 + p, 0:CAP], IA, 2 * IB)
                gate = (ps[0:IA, 2 + p, 0:CAP], 0, IA)
                upper = (ps[0:IA, 2 + p, CAP:2 * CAP], IA + 2 * IB, IA)
                parts = ((w_hi, x_hi[p]), (w_lo, x_hi[p]), (w_hi, x_lo[p]))

                def products(to, k):
                    dst, col, wide = to
                    w, rows_t = parts[k]
                    for cc in range(KC):
                        last = pe.matmul(dst, w[:, cc, col:col + wide], rows_t[:, cc, :],
                                         start=(k == 0 and cc == 0), stop=(k == 2 and cc == KC - 1))
                    return last

                for to in (both, gate):
                    for k in range(2):
                        products(to, k)
                pe.wait_ge(s_xd, n + 1)
                for to in (both, gate):
                    products(to, 2)
                for k in range(3):
                    last = products(upper, k)
                last.then_inc(s_gu, 1)

            def down(n, p, w_hi, w_lo):
                pe.wait_ge(s_hid, n + 1)
                pe.wait_ge(s_ya, n)
                pe.wait_ge(s_yd, n)
                products = ((hid_hi[p][0:IA, 0, :], w_hi[0:IA, 0, :]), (hid_hi[p][:, 1, :], w_hi[:, 1, :]),
                            (hid_hi[p][0:IA, 0, :], w_lo[:, :]), (hid_lo[p][0:IA, 0, :], w_hi[0:IA, 0, :]),
                            (hid_lo[p][:, 1, :], w_hi[:, 1, :]))
                for h in range(HALVES):
                    for k, (left, w) in enumerate(products):
                        last = pe.matmul(ps[:, 6 + h, :], left[:, h * P:(h + 1) * P], w, start=(k == 0),
                                         stop=(k == len(products) - 1))
                last.then_inc(s_dn, 1)

            turn_rows(0, 0, s_xg, 1)
            pe.wait_ge(s_shl, 1)
            up(0, 0, sh_gu_hi, sh_gu_lo)
            turn_rows(1, 1, s_xg, 1)
            with pe.Fori(0, NSH // 2 - 1) as i:
                for p in range(2):
                    n = i * 2 + p
                    up(n + 1, 1 - p, sh_gu_hi, sh_gu_lo)
                    turn_rows(n + 2, p, s_xg, i + 2)
                    down(n, p, sh_d_hi, sh_d_lo)

            def expert_up(e, p):
                pe.wait_ge(s_gul, e + 1)
                up(e + NSH, p, e_gu_hi[p], e_gu_lo[p])

            def expert_down(e, p):
                pe.wait_ge(s_dl, e + 1)
                pe.wait_ge(s_dp, e + 1)
                down(e + NSH, p, e_d_hi[p], e_d_lo[p])

            up(NSH - 1, 1, sh_gu_hi, sh_gu_lo)
            turn_rows(NSH, 0, s_eg, 1)
            down(NSH - 2, 0, sh_d_hi, sh_d_lo)
            expert_up(0, 0)
            turn_rows(NSH + 1, 1, s_eg, 1)
            down(NSH - 1, 1, sh_d_hi, sh_d_lo)
            with pe.Fori(0, E // 2 - 1) as i:
                for p in range(2):
                    e = i * 2 + p
                    expert_up(e + 1, 1 - p)
                    turn_rows(e + (NSH + 2), p, s_eg, i + 2)
                    expert_down(e, p)
            expert_up(E - 1, 1)
            for p in range(2):
                expert_down(E - 2 + p, p)

        @block.vector
        def _(dve):
            dve.memset(qs[:, :, :, :], 0.0)
            dve.memset(kpad[:, :, :].bitcast(f32), 0.0)
            dve.memset(ones[:, :], 1.0)
            dve.memset(ones_b[:, :], 1.0)
            dve.memset(mhalf[:, :], -0.5)
            dve.memset(ks[:, :], 0.0)
            dve.memset(seen[:, :], 0.0)
            dve.memset(seen_b[:, :], 0.0)
            def statistics(b):
                dve.wait_ge(s_x[b], 16 * (TPB // TPC))
                for t in range(b * TPB, (b + 1) * TPB):
                    dve.bn_stats(st[:, t, :], xres[:, t, :])
                dve.drain()
                for t in range(b * TPB, (b + 1) * TPB):
                    dve.bn_aggr(mv[:, t, :], st[:, t, :])
                dve.drain()
                tiles = slice(b * TPB, (b + 1) * TPB)
                dve.tensor_scalar(ve[:, tiles], mv[:, tiles, 1], LN_EPS, None, ALU.add).then_inc(s_var, 1)

            statistics(0)
            dve.wait_ge(s_small, 112)
            dve.tensor_copy(ident_b[:, :], ident)
            dve.tensor_copy(bias_b[:, :], mask_s[:, 0:P])
            dve.tensor_copy(upper_b[:, :], mask_s[:, P:2 * P])
            dve.drain()
            dve.memset(ks[:, 3 * HD:3 * HD + 2], 1.0)
            dve.scalar_tensor_tensor(wkq[:, :], wqn_s[:, :], float(HD) ** -0.5, wkn_s[:, :], ALU.mult, ALU.mult)
            dve.drain()
            dve.sem_inc(s_ready, 1)
            dve.wait_ge(s_mod, 1)
            cols = ps[:, 0, 0:2 * KC * B].rearrange("p (m c b) -> p m c b", m=2, c=KC)
            dve.tensor_copy(mcol[:, 0, :, :], cols[:, 0, :, :])
            dve.tensor_scalar(mcol[:, 1, :, :], cols[:, 1, :, :], 1.0, None, ALU.add).then_inc(s_modv, 1)
            dve.memset(pay[:, :], 0)
            dve.tensor_scalar(idx8[:, :, :], trash, -1.0, None, ALU.add).then_inc(s_pay, 1)

            def modulation_rows():
                for n in range(4):
                    dve.wait_ge(s_mod, n + 2)
                    src, dst = ps[0:B, n, :], mod_rows[:, n, :]
                    if n == 1:
                        dve.tensor_copy(dst, src)
                    elif n == 2:
                        dve.tensor_scalar(dst, src, 1.0, None, ALU.add)
                    else:
                        dve.drain()
                        dve.tensor_scalar(gate_t[:, :], src, 0.0, 0.5, ALU.is_ge, ALU.subtract)
                        dve.drain()
                        dve.scalar_tensor_tensor(gate_a[:, :], gate_t[:, :], 2.0, src, ALU.mult, ALU.mult)
                        dve.drain()
                        dve.tensor_scalar(gate_a[:, :], gate_a[:, :], 0.25, 2.0, ALU.max, ALU.mult)
                        dve.drain()
                        dve.tensor_tensor(dst, gate_t[:, :], gate_a[:, :], ALU.mult)
                dve.drain()
                dve.sem_inc(s_rows, 1)
                dve.sem_inc(s_ready, 1)

            def normalise(b, i):
                dve.wait_ge(s_xT, b * TPB + max(i - 1, 0))
                t = b * TPB + i
                dve.tensor_scalar(xn[:, i % 2, :], xtile(t), mv[:, ds(t, 1), 0], rstd[:, ds(t, 1)],
                                  ALU.subtract, ALU.mult).then_inc(s_xn, 1)

            def rotate(b, i):
                t = b * TPB + i
                half = HD // 2
                shape = [P, H + 1, half]
                dve.drain()
                dve.wait_ge(s_qk, t + 1)
                dve.tensor_tensor(t1[:, :, :], qk[:, :, :], cos[:, i, :].unsqueeze(1).to_broadcast([P, H + 1, HD]), ALU.mult)
                dve.tensor_tensor(t2[:, :, 0:half], qk[:, :, half:HD],
                                  sin[:, i, 0:half].unsqueeze(1).to_broadcast(shape), ALU.mult)
                dve.tensor_tensor(t2[:, :, half:HD], qk[:, :, 0:half],
                                  sin[:, i, half:HD].unsqueeze(1).to_broadcast(shape), ALU.mult)
                dve.wait_ge(s_square, t + 1)
                dve.reduce_sum(ssq[:, :], sq[:, :, :], AX.X).then_inc(s_rope, 1)
                dve.drain()
                dve.tensor_scalar(ms[:, :], ssq[:, :], 1.0 / HD, RMS_EPS, ALU.mult, ALU.add).then_inc(s_ms, 1)
                dve.tensor_tensor(qr[:, :, :], t1[:, :, :], t2[:, :, :], ALU.add)

            def split(b, i):
                t = b * TPB + i
                q_parts = qs[:, i % 2, :, :]
                dve.drain()
                dve.wait_ge(s_rr, t + 1)
                dve.tensor_tensor(t2[:, :, :], qr[:, :, :], rr[:, :].unsqueeze(2).to_broadcast([P, H + 1, HD]), ALU.mult)
                dve.drain()
                dve.wait_ge(s_st, (b * TPB + max(i - 1, 0)) * NG)
                dve.tensor_copy(q_parts[:, :, 0:HD].bitcast(f32r), t2[:, 0:H, :])
                dve.tensor_copy(q_parts[:, :, HD:2 * HD].bitcast(f32r), t2[:, 0:H, :])
                dve.tensor_tensor(t1[:, H, :], t2[:, H, :], wkq[:, :], ALU.mult)
                dve.drain()
                dve.wait_ge(s_pack, t)
                dve.tensor_copy(qh[:, :, :].bitcast(f32r), t2[:, 0:H, :])
                dve.tensor_copy(ks[:, 0:HD].bitcast(f32r), t1[:, H, :])
                dve.tensor_copy(ks[:, 2 * HD:3 * HD].bitcast(f32r), t1[:, H, :])
                dve.tensor_copy(kh4[:, :, :].bitcast(f32r), t1[:, H, :].unsqueeze(1).to_broadcast([P, GH, HD]))
                dve.tensor_tensor(q_parts[:, :, 2 * HD:3 * HD].bitcast(f32r), t2[:, 0:H, :], q_parts[:, :, 0:HD],
                                  ALU.subtract)
                dve.drain()
                dve.tensor_tensor(ks[:, HD:2 * HD].bitcast(f32r), t1[:, H, :], ks[:, 0:HD], ALU.subtract)\
                   .then_inc(s_parts, 1)

            def row_max(b, i):
                t = b * TPB + i
                q_parts = qs[:, i % 2, :, :]
                width = (i + 1) * P
                step = 2 if width <= 512 else 1
                reduced = b * MAXES[TPB] + MAXES[i]
                dve.drain()
                for h in range(0, H, step):
                    if h == 8 and i + 3 < TPB:
                        normalise(b, i + 3)
                    if h == 8 and i + 1 in EARLY:
                        split(b, i + 1)
                    if TPC <= i <= SQUARED:
                        for g in range(NG):
                            n = (i - TPC) * H + h - divided_from(g)
                            if 0 <= n < DIVIDE_STEPS and (i in BESIDE or g == NG - 1):
                                divide_step(b, 0, g, n)
                    if i in BESIDE:
                        for half, n in enumerate((512, width - 512)):
                            dve.wait_ge(s_mm, reduced + (2 * h + half + 1))
                            dve.tensor_reduce(nmax[:, half, h:h + 1], ps[:, 2 + half, 0:n], AX.X, ALU.max, negate=True)\
                               .then_inc(s_max, 1)
                    else:
                        dve.wait_ge(s_mm, reduced + (h + step))
                        buf = pair(h // step % 2)
                        scores = buf[:, :, 0:width] if step == 2 else buf.rearrange("p a n -> p (a n)")[:, 0:width]
                        dve.tensor_reduce(nmax[:, 0, h:h + step], scores, AX.X, ALU.max, negate=True).then_inc(s_max, step)
                dve.drain()
                if i in BESIDE:
                    dve.tensor_tensor(nmax[:, 0, :], nmax[:, 0, :], nmax[:, 1, :], ALU.min)
                    dve.drain()
                dve.tensor_copy(q_parts[:, :, 3 * HD].bitcast(f32r), nmax[:, 0, :])
                dve.drain()
                dve.tensor_tensor(q_parts[:, :, 3 * HD + 1].bitcast(f32r), nmax[:, 0, :], q_parts[:, :, 3 * HD],
                                  ALU.subtract).then_inc(s_nmax, 1)

            def begin_squares(b, qc):
                dve.wait_ge(s_oss, b * QC + qc)
                dve.memset(osq[:, :], 0.0)
                dve.drain()

            def divide_step(b, qc, g, n):
                row = oT[:, qc, ds(g, 1), :].rearrange("p a n -> p (a n)")
                if n == 0:
                    hold(dve, s_on, b * (QC * NG) + qc * NG + (g + 1))
                if n < TPC:
                    piece = scratch[:, n * P:n * P + P]
                    dve.reciprocal(piece, piece)
                elif n == TPC:
                    dve.drain()
                    dve.tensor_tensor(row, row, scratch[:, :], ALU.mult)
                else:
                    dve.drain()
                    dve.tensor_tensor(scratch[:, :], row, row, ALU.mult)
                    dve.drain()
                    dve.tensor_tensor(osq[:, :], osq[:, :], scratch[:, :], ALU.add).then_inc(s_sq, 1)
                    dve.drain()

            def divide(b, qc, g):
                for n in range(DIVIDE_STEPS):
                    divide_step(b, qc, g, n)

            def mean_square(b, qc):
                dve.wait_ge(s_oss, b * QC + (qc + 1))
                dve.tensor_scalar(oms[:, :], ps[:, 4 + qc, 0:TPC], 1.0 / D, RMS_EPS, ALU.mult, ALU.add)\
                   .then_inc(s_oms, 1)

            def residual(b, qc, ii, bank, slot):
                t = b * TPB + (ii + qc * TPC)
                dve.wait_ge(s_gates, 32)
                dve.wait_ge(s_orstd, b * QC + (qc + 1))
                dve.wait_ge(s_at, t + 1)
                dve.scalar_tensor_tensor(scratch[:, :], ps[:, bank, :], orstd[:, qc, ds(ii, 1)], rows(b, ga),
                                         ALU.mult, ALU.mult).then_inc(s_atd, 1)
                dve.drain()
                xt = xtile(t)
                dve.tensor_tensor(xt, xt, scratch[:, :], ALU.add)
                dve.drain()
                dve.bn_stats(st2[:, slot, :], xt)
                dve.drain()
                dve.bn_aggr(mv2[:, slot, :], st2[:, slot, :])
                dve.drain()
                dve.tensor_scalar(ve2[:, slot:slot + 1], mv2[:, slot, 1:2], LN_EPS, None, ALU.add).then_inc(s_var2, 1)

            def shift(b, qc, ii, slot):
                t = b * TPB + (ii + qc * TPC)
                row = h2[:, slot, :]
                dve.wait_ge(s_rstd2, t + 1)
                dve.wait_ge(s_init, 32)
                dve.wait_ge(s_h2_out[slot], (b * STORED[slot] + (ii if qc == 0 else TPC * (1 - slot) + ii // 2)) * 16)
                dve.wait_ge(s_h2t, b * TPB + (ii if qc == 0 else TPC + max(ii - 1, 0)))
                dve.tensor_scalar(row, xtile(t), mv2[:, slot, 0:1], rstd2[:, slot:slot + 1], ALU.subtract, ALU.mult)
                dve.drain()
                dve.tensor_tensor(row, row, rows(b, cscale), ALU.mult)
                dve.drain()
                dve.tensor_tensor(row, row, rows(b, sbias), ALU.add).then_inc(s_h2, 1)

            def route(b, followed):
                all_e = [P, TPB, E]
                grp = [P, TPB, GROUPS, GROUPS]
                dve.wait_ge(s_ex, b + 1)
                dve.tensor_scalar(biased[:, :, :], ex[:, :, :], 1.0, None, ALU.add)
                dve.drain()
                dve.reciprocal(score[:, :, :], biased[:, :, :])
                dve.drain()
                dve.tensor_tensor(biased[:, :, :], score[:, :, :], ebias[:, :].unsqueeze(1).to_broadcast(all_e), ALU.add)
                dve.drain()
                v = biased[:, :, :].rearrange("p t (g m) -> p (t g) m", m=GROUPS)
                dve.tensor_tensor(hi4[:, :, :], v[:, :, 0:4], v[:, :, 4:8], ALU.max)
                dve.tensor_tensor(lo4[:, :, :], v[:, :, 0:4], v[:, :, 4:8], ALU.min)
                dve.drain()
                dve.tensor_tensor(hi2[:, :, :], hi4[:, :, 0:2], hi4[:, :, 2:4], ALU.max)
                dve.tensor_tensor(mid2[:, :, :], hi4[:, :, 0:2], hi4[:, :, 2:4], ALU.min)
                dve.tensor_tensor(lo2[:, :, :], lo4[:, :, 0:2], lo4[:, :, 2:4], ALU.max)
                dve.drain()
                dve.tensor_tensor(lo2[:, :, :], lo2[:, :, :], mid2[:, :, :], ALU.max)
                dve.tensor_tensor(hi1[:, :], hi2[:, :, 0], hi2[:, :, 1], ALU.max)
                dve.tensor_tensor(mid1[:, :], hi2[:, :, 0], hi2[:, :, 1], ALU.min)
                dve.drain()
                dve.tensor_tensor(lo1[:, :], lo2[:, :, 0], lo2[:, :, 1], ALU.max)
                dve.drain()
                dve.tensor_tensor(lo1[:, :], lo1[:, :], mid1[:, :], ALU.max)
                dve.drain()
                gs = gsum[:, :, :]
                dve.tensor_tensor(gs.rearrange("p t g -> p (t g)"), hi1[:, :], lo1[:, :], ALU.add)
                dve.drain()
                other, own = gs.unsqueeze(2).to_broadcast(grp), gs.unsqueeze(3).to_broadcast(grp)
                dve.tensor_tensor(cmp_a[:, :, :, :], other, own, ALU.is_gt)
                dve.tensor_tensor(cmp_b[:, :, :, :], other, own, ALU.is_equal)
                dve.drain()
                dve.tensor_tensor(cmp_b[:, :, :, :], cmp_b[:, :, :, :], tri.unsqueeze(1).to_broadcast(grp), ALU.mult)
                dve.drain()
                dve.tensor_tensor(cmp_a[:, :, :, :], cmp_a[:, :, :, :], cmp_b[:, :, :, :], ALU.add)
                dve.drain()
                dve.reduce_sum(grank[:, :, :], cmp_a[:, :, :, :], AX.X)
                dve.drain()
                dve.tensor_scalar(grank[:, :, :], grank[:, :, :], float(TOPG), None, ALU.is_lt)
                dve.drain()
                dve.tensor_tensor(masked[:, :, :].rearrange("p t (g m) -> p t g m", m=GROUPS),
                                  biased[:, :, :].rearrange("p t (g m) -> p t g m", m=GROUPS),
                                  grank[:, :, :].unsqueeze(3).to_broadcast(grp), ALU.mult)
                dve.drain()
                for ii in range(TPB):
                    dve.max(top8[:, ii, :], masked[:, ii, :])
                dve.drain()
                for ii in range(TPB):
                    dve.match_replace(marked[:, ii, :], top8[:, ii, :], masked[:, ii, :], -3e38)
                dve.drain()
                dve.tensor_scalar(sel_b[:, :, :], marked[:, :, :], -3e38, None, ALU.is_equal).then_inc(s_sel, 1)
                dve.tensor_scalar(sel[:, :, :], marked[:, :, :], -3e38, None, ALU.is_equal)
                dve.drain()
                dve.tensor_tensor(wts[:, :, :], score[:, :, :], sel[:, :, :], ALU.mult)
                dve.reduce_sum(selsum[:, :], sel[:, :, :].rearrange("p t e -> p e t"), AX.X)
                dve.drain()
                dve.reduce_sum(wsum[:, :], wts[:, :, :], AX.X)
                dve.tensor_tensor(seen[:, :], seen[:, :], selsum[:, :], ALU.add)
                dve.drain()
                dve.tensor_scalar(wsum[:, :], wsum[:, :], 1e-20, None, ALU.add)
                dve.drain()
                dve.reciprocal(wrec[:, :], wsum[:, :])
                dve.drain()
                dve.scalar_tensor_tensor(wts[:, :, :], wts[:, :, :], ROUTED_SCALE,
                                         wrec[:, :].unsqueeze(2).to_broadcast(all_e), ALU.mult, ALU.mult).then_inc(s_wts, 1)
                if followed:
                    rotate(b + 1, 0)
                    normalise(b + 1, 2)
                dve.wait_ge(s_pos, b + 1)
                pos = ps[:, 7, :].rearrange("p (t e) -> p t e", e=E)
                dve.tensor_copy(seen_b[:, :], seen[:, :])
                dve.tensor_scalar(hv[:, :, :], pos, float(P), 1.0 - P * P, ALU.is_ge, ALU.mult)
                dve.scalar_tensor_tensor(valid[:, :, :], pos, float(CAP), sel[:, :, :], ALU.is_lt, ALU.mult)
                dve.drain()
                dve.scalar_tensor_tensor(key[:, :, :], pos, float(P), hv[:, :, :], ALU.mult, ALU.add)
                dve.drain()
                dve.tensor_tensor(key[:, :, :], key[:, :, :], erow.unsqueeze(1).to_broadcast(all_e), ALU.add)
                dve.drain()
                dve.tensor_tensor(key[:, :, :], key[:, :, :], valid[:, :, :], ALU.mult)
                dve.drain()
                for ii in range(TPB):
                    dve.max(key8[:, ii, :], key[:, ii, :])
                dve.drain()
                dve.wait_ge(s_slot, (b + 1) * SLOTTED)
                dve.tensor_copy(pay[:, :], tokid[:, ds(b * TPB, TPB)])
                dve.scalar_tensor_tensor(miss8[:, :, :], key8[:, :, :], 0.0, trash, ALU.is_equal, ALU.mult)
                dve.drain()
                dve.scalar_tensor_tensor(idx8[:, :, :], key8[:, :, :], -1.0, miss8[:, :, :], ALU.add, ALU.add)\
                   .then_inc(s_pay, 1)

            dve.wait_ge(s_rstd, 1)
            normalise(0, 0)
            normalise(0, 1)
            statistics(1)
            dve.wait_ge(s_weights, 64)
            for cc in range(KC):
                dve.tensor_scalar(wo[:, cc, :], wo[:, cc, :], wpre[:, cc:cc + 1], None, ALU.mult)
            rotate(0, 0)
            normalise(0, 2)
            split(0, 0)
            modulation_rows()
            dve.wait_ge(s_rstd, B)

            def batch(b, followed):
                for i in range(TPB):
                    if i and i not in EARLY:
                        split(b, i)
                    if i + 1 < TPB:
                        rotate(b, i + 1)
                    if i == BESIDE[0]:
                        begin_squares(b, 0)
                    row_max(b, i)
                    if i == BESIDE[1]:
                        for g in range(NG - 1):
                            for n in range(max(2 * H - divided_from(g), 0), DIVIDE_STEPS):
                                divide_step(b, 0, g, n)
                    if i == SQUARED:
                        mean_square(b, 0)
                begin_squares(b, 1)
                with dve.Fori(0, NG) as g:
                    residual(b, 0, g, 6, 0)
                    shift(b, 0, g, 0)
                    divide(b, 1, g)
                mean_square(b, 1)
                residual(b, 1, 0, OUT_BANKS[0], 0)
                for ii in range(TPC):
                    if ii + 1 < TPC:
                        residual(b, 1, ii + 1, OUT_BANKS[ii + 1], (ii + 1) % 2)
                    shift(b, 1, ii, ii % 2)
                if followed:
                    normalise(b + 1, 0)
                    normalise(b + 1, 1)
                route(b, followed)
                if followed:
                    split(b + 1, 0)

            with dve.Fori(0, B - 1) as b:
                batch(b, True)
            batch(B - 1, False)

            dve.drain()
            for p in range(2):
                dve.memset(hid_lo[p][IB:2 * IB, 1, :].bitcast(f32), 0.0)
            dve.drain()
            dve.sem_inc(s_hidden, 2)
            flat = "p a n -> p (a n)"

            def lo_part(dst, whole, hi):
                return dve.tensor_tensor(dst[:, :, :].rearrange(flat), whole[:, :, :].rearrange(flat),
                                         hi[:, :, :].bitcast(f32).rearrange(flat), ALU.subtract)

            def rows_lo(n, p):
                dve.wait_ge(s_xa, n + 1)
                lo_part(x_lo[p], pair(0), x_hi[p]).then_inc(s_xd, 1)

            def hidden(n, p):
                dve.wait_ge(s_hh, n)
                dve.wait_ge(s_act, n + 1)
                dve.tensor_tensor(hid[:, 0, :], gact_a[p][:, :], ps[0:IA, 2 + p, CAP:2 * CAP], ALU.mult)
                dve.tensor_tensor(hid[0:IB, 1, :], gact_b[p][:, :], ps[IB:2 * IB, 4 + p, 0:CAP], ALU.mult)\
                   .then_inc(s_hidden, 1)

            def hidden_lo(n, p):
                dve.wait_ge(s_hh, n + 1)
                dve.tensor_tensor(hid_lo[p][0:IA, 0, :], hid[:, 0, :], hid_hi[p][0:IA, 0, :].bitcast(f32), ALU.subtract)
                dve.tensor_tensor(hid_lo[p][0:IB, 1, :], hid[0:IB, 1, :], hid_hi[p][0:IB, 1, :].bitcast(f32), ALU.subtract)\
                   .then_inc(s_hid, 1)
                dve.drain()

            def up_lo(e, p):
                dve.wait_ge(s_guh, e + 1)
                lo_part(e_gu_lo[p], e_gu[p], e_gu_hi[p]).then_inc(s_gul, 1)

            def down_lo(e, p):
                dve.wait_ge(s_dh, e + 1)
                dve.tensor_tensor(e_d_hi[p][IB:2 * IB, 1, :], e_d[p][0:IB, 1, :], e_d_hi[p][0:IB, 1, :].bitcast(f32),
                                  ALU.subtract)\
                   .then_inc(s_dl, 1)

            def take_weights(e, p):
                dve.wait_ge(s_xa, e + (NSH + 1))
                dve.tensor_copy(weight[:, ds(e * HALVES, HALVES)], xg[p][:, :, ds(e + D, 1)].rearrange("p h a -> p (h a)"))

            def step(n, p, expert=None):
                hidden(n + 1, 1 - p)
                if expert is not None:
                    take_weights(expert, p)
                rows_lo(n + 2, p)
                hidden_lo(n + 1, 1 - p)

            def shared_out(n, p, b):
                dve.wait_ge(s_dn, n + 3)
                for h, done in enumerate((s_ya, s_yd)):
                    dve.tensor_tensor(y[p][:, h, :], ps[:, 6 + h, :], b, ALU.mult).then_inc(done, 1)
                dve.drain()
                for h in range(HALVES):
                    xt = xtile(n * HALVES + h)
                    dve.tensor_tensor(xt, xt, y[p][:, h, :], ALU.add)
                dve.drain()

            dve.wait_ge(s_shh, 1)
            lo_part(sh_gu_lo, sh_gu, sh_gu_hi)
            dve.tensor_tensor(sh_d_lo[:, :], sh_d[:, 0, :], sh_d_hi[0:IA, 0, :].bitcast(f32), ALU.subtract)
            dve.tensor_tensor(sh_d_hi[IB:2 * IB, 1, :], sh_d[0:IB, 1, :], sh_d_hi[0:IB, 1, :].bitcast(f32), ALU.subtract)\
               .then_inc(s_shl, 1)
            rows_lo(0, 0)
            hidden(0, 0)
            rows_lo(1, 1)
            hidden_lo(0, 0)
            with dve.Fori(0, NSH // 2 - 1) as i:
                for p in range(2):
                    n = i * 2 + p
                    step(n, p)
                    shared_out(n, p, rows(i // (NSH // 2 // B), gb))
            up_lo(0, 0)
            step(NSH - 2, 0, 0)
            shared_out(NSH - 2, 0, gb[:, B - 1, :])
            up_lo(1, 1)
            down_lo(0, 0)
            step(NSH - 1, 1, 1)
            shared_out(NSH - 1, 1, gb[:, B - 1, :])

            def weighted(e, p):
                dve.wait_ge(s_yfree, e)
                dve.wait_ge(s_dn, e + NSH + 3)
                dve.tensor_scalar(y[p][:, 1, :], ps[:, 7, :], weight[:, ds(e * HALVES + 1, 1)], None,
                                  ALU.mult).then_inc(s_yd, 1)

            with dve.Fori(0, E // 2 - 1) as i:
                for p in range(2):
                    e = i * 2 + p
                    up_lo(e + 2, p)
                    down_lo(e + 1, 1 - p)
                    step(e + NSH, p, e + 2)
                    weighted(e, p)
            down_lo(E - 1, 1)
            hidden(E + NSH - 1, 1)
            hidden_lo(E + NSH - 1, 1)
            for p in range(2):
                weighted(E - 2 + p, p)

            for c in range(NT // TPC):
                dve.wait_ge(s_fin_in[c], 16)
                part = fin_acc[:, c, :, :]
                dve.tensor_tensor(part, part, gb[:, c // QC, :].unsqueeze(1).to_broadcast([P, TPC, D]), ALU.mult)
                dve.drain()
                xc = xres[:, TPC * c:TPC * c + TPC, :]
                dve.tensor_tensor(xc, xc, part, ALU.add).then_inc(s_fin, 1)


def shape_constants(np):
    p = np.arange(P)
    con = np.zeros((P, NCONST), np.float32)
    con[:, C_ID:C_ID + P] = np.eye(P)
    masks = np.zeros((P, 2 * P), np.float32)
    masks[:, 0:P] = np.where(p[None, :] <= p[:, None], 0.0, -1e30)
    masks[:, P:2 * P] = p[:, None] < p[None, :]
    inv = np.float32(1.0) / np.float32(10000.0) ** (np.arange(0, HD, 2, dtype=np.float32) / np.float32(HD))
    ang = np.arange(S, dtype=np.float32)[:, None] * inv[None, :]
    c, s = np.cos(ang), np.sin(ang)
    tile = lambda a: a.reshape(TPB, P, HD).transpose(1, 0, 2).reshape(P, TPB * HD)
    con[:, C_COS:C_SIN] = tile(np.concatenate([c, c], 1))
    con[:, C_SIN:C_EROW] = tile(np.concatenate([-s, s], 1))
    con[:, C_EROW:C_TRI] = 2 * np.arange(E) + 1
    g = np.arange(GROUPS)
    con[:, C_TRI:C_TRASH] = (g[None, :] < g[:, None]).reshape(1, -1)
    con[:, C_TRASH:NCONST] = NSLOT + 1 + np.arange(TPB * TOPK)[None, :] * P + p[:, None]
    tokid = (np.arange(NT)[None, :] * P + p[:, None]).astype(np.int32)
    slot = (NTOK + (np.arange(E * HALVES) % HALVES)[None, :] * P + p[:, None]).astype(np.int32)
    return con, masks, tokid, slot


def kernel(**inputs):
    import numpy as np
    import concourse.bacc as bacc
    from concourse.bass_utils import run_bass_kernel_spmd

    a = {k: np.asarray(v) for k, v in inputs.items()}
    chunks = lambda w: np.ascontiguousarray(w.reshape(KC, P, -1).transpose(1, 0, 2))
    con, masks, tokid, slot = shape_constants(np)
    join = lambda g, u: np.concatenate([g, u[..., IA:], u[..., :IA]], axis=-1)
    gate_up = join(a["L0_ffn_w_gate"], a["L0_ffn_w_up"])
    arrays = {
        "x": np.ascontiguousarray(a["L0_attn_x"].reshape(NTOK, D)),
        "c_t": chunks(np.ascontiguousarray(a["L0_c"].T)),
        "wmod": np.ascontiguousarray(a["L0_wmod"]),
        "wq_t": chunks(np.ascontiguousarray(a["L0_attn_Wq"].T)),
        "wkv_t": chunks(np.concatenate([a["L0_attn_Wk"].T, a["L0_attn_Wv"].T], axis=1)),
        "wo_t": chunks(np.ascontiguousarray(a["L0_attn_Wo"].T)),
        "w_pre": np.ascontiguousarray(a["L0_attn_w_pre"].reshape(KC, P).T),
        "w_qn": np.ascontiguousarray(a["L0_attn_w_qn"]),
        "w_kn": np.ascontiguousarray(a["L0_attn_w_kn"]),
        "router_t": chunks(np.ascontiguousarray(a["L0_ffn_router_weight"].T)),
        "e_bias": np.ascontiguousarray(a["L0_ffn_e_bias"]),
        "gate_up": np.ascontiguousarray(gate_up.reshape(E, KC, P, 2 * EI).transpose(0, 2, 1, 3)),
        "w_down": np.ascontiguousarray(a["L0_ffn_w_down"]),
        "sh_gate_up": chunks(join(a["L0_ffn_sh_gate"], a["L0_ffn_sh_up"])),
        "sh_down": np.ascontiguousarray(a["L0_ffn_sh_down"]),
        "consts": con,
        "masks": masks,
        "tokids": tokid,
        "slot_init": slot,
    }
    nc = bacc.Bacc("TRN2", target_bir_lowering=False, num_devices=1)
    args = [nc.dram_tensor(f"in_{n}", v.shape, mybir.dt.from_np(v.dtype), kind="ExternalInput").ap()
            for n, v in arrays.items()]
    out = nc.dram_tensor("out", (NTOK, D), mybir.dt.float32, kind="ExternalOutput").ap()
    build_program(nc, *args, out)
    r = run_bass_kernel_spmd(nc, [{f"in_{n}": v for n, v in arrays.items()}], core_ids=[0])
    return r.results[0]["out"].reshape(B, S, D)
```
